# Optimizing a Trainium2 kernel written in Bass

```python
import numpy as np
import jax
import jax.numpy as jnp

def _softmax(x, axis=-1):
    return jax.nn.softmax(x, axis=axis)

def _gelu(x):
    return jax.nn.gelu(x, approximate=True)

def _silu(x):
    return jax.nn.silu(x)

def _sigmoid(x):
    return jax.nn.sigmoid(x)

def _layernorm(x, axis=-1, eps=1e-05):
    m = jnp.mean(x, axis=axis, keepdims=True)
    v = jnp.var(x, axis=axis, keepdims=True)
    return (x - m) / jnp.sqrt(v + eps)

def _scatter_add(tgt, idx, src, axis=0):
    return tgt.at[idx].add(src)

def _segment_sum(src, seg, n):
    return jax.ops.segment_sum(src, seg, n)
kernel_name = 'mk_recurrent_d2_jaxref_r8_d36422'

def setup_inputs(seed: int=0):
    np.random.seed(seed)
    _w = jnp.asarray

    def _L0_attn_setup():
        import jax, jax.numpy as jnp
        import numpy as np
        D = 128
        B = 4
        S = 512
        LN_EPS = 1e-05

        def _layer_norm(x, gamma, beta):
            mu = jnp.mean(x, axis=-1, keepdims=True)
            var = jnp.mean(jnp.square(x - mu), axis=-1, keepdims=True)
            return (x - mu) * jax.lax.rsqrt(var + LN_EPS) * gamma + beta
        key = jax.random.key(seed)
        ks = jax.random.split(key, 5)
        scale = 1.0 / np.sqrt(D)
        return {'hidden_states': jax.random.normal(ks[0], (B, S, D), dtype=jnp.float32), 'attention_mask': jnp.ones((B, S), dtype=jnp.int32), 'Wk': jax.random.normal(ks[1], (D, D), dtype=jnp.float32) * scale, 'bk': jnp.zeros((D,), dtype=jnp.float32), 'Wka': jax.random.normal(ks[2], (D, D), dtype=jnp.float32) * scale, 'bka': jnp.zeros((D,), dtype=jnp.float32), 'Wv': jax.random.normal(ks[3], (D, D), dtype=jnp.float32) * scale, 'bv': jnp.zeros((D,), dtype=jnp.float32), 'gamma': jnp.ones((D,), dtype=jnp.float32), 'beta': jnp.zeros((D,), dtype=jnp.float32)}
    _L0_attn_in = _L0_attn_setup()

    def _L0_ffn_setup():
        import jax, jax.numpy as jnp
        import numpy as np
        DIM = 128
        DEPTH = 2
        HEADS = 8
        DIM_HEAD = 64
        WINDOW = 64
        INNER = HEADS * DIM_HEAD
        HID = int(DIM * 4 * 2 / 3)
        B, N = (2, 1024)
        QK_SCALE = 8.0

        def shift_token(t):
            t1, t2 = jnp.split(t, 2, axis=-1)
            t2 = jnp.pad(t2, ((0, 0), (1, 0), (0, 0)))[:, :-1]
            return jnp.concatenate([t1, t2], axis=-1)

        def l2norm(t):
            return t / jnp.clip(jnp.linalg.norm(t, axis=-1, keepdims=True), 1e-12)

        def rotate_half(x):
            x1, x2 = jnp.split(x, 2, axis=-1)
            return jnp.concatenate([-x2, x1], axis=-1)

        def rotary_xpos(q, k):
            n = q.shape[-2]
            half_idx = jnp.arange(0, DIM_HEAD, 2, dtype=jnp.float32)
            inv_freq = 1.0 / 10000.0 ** (half_idx / DIM_HEAD)
            t = jnp.arange(n, dtype=jnp.float32)
            freqs = t[:, None] * inv_freq[None, :]
            freqs = jnp.concatenate([freqs, freqs], axis=-1)
            base = (half_idx + 0.4 * DIM_HEAD) / (1.4 * DIM_HEAD)
            power = (t - n // 2) / float(WINDOW // 2)
            scale = base[None, :] ** power[:, None]
            scale = jnp.concatenate([scale, scale], axis=-1)
            cos, sin = (jnp.cos(freqs), jnp.sin(freqs))
            q = q * cos * scale + rotate_half(q) * sin * scale
            k = k * cos / scale + rotate_half(k) * sin / scale
            return (q, k)

        def local_attention(q, k, v):
            b, h, n, d = q.shape
            w = n // WINDOW
            bq = q.reshape(b, h, w, WINDOW, d) * QK_SCALE
            bk = k.reshape(b, h, w, WINDOW, d)
            bv = v.reshape(b, h, w, WINDOW, d)

            def look_around(t):
                p = jnp.pad(t, ((0, 0), (0, 0), (1, 0), (0, 0), (0, 0)))
                return jnp.concatenate([p[:, :, :w], p[:, :, 1:]], axis=3)
            bk, bv = (look_around(bk), look_around(bv))
            bt = jnp.arange(n).reshape(w, WINDOW)
            btp = jnp.pad(bt, ((1, 0), (0, 0)), constant_values=-1)
            btk = jnp.concatenate([btp[:w], btp[1:]], axis=1)
            sim = jnp.einsum('bhwid,bhwjd->bhwij', bq, bk)
            i = bt[:, :, None]
            j = btk[:, None, :]
            mask = (i < j) | (i > j + WINDOW) | (j == -1)
            sim = jnp.where(mask, -jnp.finfo(sim.dtype).max, sim)
            attn = jax.nn.softmax(sim, axis=-1)
            out = jnp.einsum('bhwij,bhwjd->bhwid', attn, bv)
            return out.reshape(b, h, n, d)

        def _layer(x, wqkv, qs, ksc, wo, lg, lb, w1, b1, w2, b2):
            b, n, _ = x.shape
            h = shift_token(x)
            qkv = h @ wqkv
            q, k, v = jnp.split(qkv, 3, axis=-1)
            to_heads = lambda t: t.reshape(b, n, HEADS, DIM_HEAD).transpose(0, 2, 1, 3)
            q, k, v = (to_heads(q), to_heads(k), to_heads(v))
            q = l2norm(q) * qs
            k = l2norm(k) * ksc
            q, k = rotary_xpos(q, k)
            o = local_attention(q, k, v)
            o = o.transpose(0, 2, 1, 3).reshape(b, n, INNER)
            x = x + o @ wo
            h = shift_token(x)
            mu = h.mean(-1, keepdims=True)
            var = h.var(-1, keepdims=True)
            h = (h - mu) / jnp.sqrt(var + 1e-05) * lg + lb
            h = h @ w1 + b1
            a, g = jnp.split(h, 2, axis=-1)
            h = a * jax.nn.gelu(g, approximate=False)
            x = x + h @ w2 + b2
            return x
        key = jax.random.key(seed)
        ks = jax.random.split(key, 6)
        return {'x': jax.random.normal(ks[0], (B, N, DIM), jnp.float32), 'wqkv': jax.random.normal(ks[1], (DEPTH, DIM, 3 * INNER), jnp.float32) * 0.02, 'q_scale': jnp.ones((DEPTH, DIM_HEAD), jnp.float32), 'k_scale': jnp.ones((DEPTH, DIM_HEAD), jnp.float32), 'wo': jax.random.normal(ks[2], (DEPTH, INNER, DIM), jnp.float32) * 0.02, 'ln_g': jnp.ones((DEPTH, DIM), jnp.float32), 'ln_b': jnp.zeros((DEPTH, DIM), jnp.float32), 'w1': jax.random.normal(ks[3], (DEPTH, DIM, 2 * HID), jnp.float32) * 0.02, 'b1': jnp.zeros((DEPTH, 2 * HID), jnp.float32), 'w2': jax.random.normal(ks[4], (DEPTH, HID, DIM), jnp.float32) * 0.02, 'b2': jnp.zeros((DEPTH, DIM), jnp.float32)}
    _L0_ffn_in = _L0_ffn_setup()

    def _L1_attn_setup():
        import jax, jax.numpy as jnp
        import numpy as np
        import math
        DIM, H, T, B = (128, 16, 256, 1)
        BASE = 15000.0

        def _count_mask(t_len, n_heads):
            idx = jnp.arange(t_len)
            hm = jnp.arange(n_heads)
            count = jnp.zeros((n_heads, t_len, t_len), jnp.float32)
            for X in range(int(math.log2(t_len))):
                S, r = (2 ** (X + 2), 2 ** X)
                same_seg = idx[:, None] // S == idx[None, :] // S
                ok = idx[None, :] % r == hm[:, None] % r
                pat = same_seg[None, :, :] & ok[:, :, None] & ok[:, None, :]
                count = count + pat.astype(jnp.float32)
            return count
        key = jax.random.key(seed)
        ks = jax.random.split(key, 9)
        s = 0.02
        d = DIM
        return {'x': jax.random.normal(ks[0], (B, T, d), jnp.float32), 'Wq': jax.random.normal(ks[1], (d, d), jnp.float32) * s, 'bq': jnp.zeros((d,), jnp.float32), 'Wk': jax.random.normal(ks[2], (d, d), jnp.float32) * s, 'bk': jnp.zeros((d,), jnp.float32), 'Wv': jax.random.normal(ks[3], (d, d), jnp.float32) * s, 'bv': jnp.zeros((d,), jnp.float32), 'Wo': jax.random.normal(ks[4], (d, d), jnp.float32) * s, 'bo': jnp.zeros((d,), jnp.float32)}
    _L1_attn_in = _L1_attn_setup()

    def _L1_ffn_setup():
        import jax, jax.numpy as jnp
        import numpy as np
        D_MODEL = 128
        D_FF = 512
        NUM_EXPERTS = 8
        key = jax.random.key(seed)
        ks = jax.random.split(key, 8)
        scale_in = 1.0 / np.sqrt(D_MODEL)
        scale_ff = 1.0 / np.sqrt(D_FF)
        x = jax.random.normal(ks[0], (4, 256, D_MODEL), dtype=jnp.float32)
        gate_w = jax.random.uniform(ks[1], (NUM_EXPERTS, D_MODEL), jnp.float32, -scale_in, scale_in)
        gate_b = jax.random.uniform(ks[2], (NUM_EXPERTS,), jnp.float32, -scale_in, scale_in)
        expert_bias = jnp.zeros((NUM_EXPERTS,), dtype=jnp.float32)
        w1 = jax.random.uniform(ks[3], (NUM_EXPERTS, D_MODEL, D_FF), jnp.float32, -scale_in, scale_in)
        b1 = jax.random.uniform(ks[4], (NUM_EXPERTS, D_FF), jnp.float32, -scale_in, scale_in)
        w2 = jax.random.uniform(ks[5], (NUM_EXPERTS, D_FF, D_MODEL), jnp.float32, -scale_ff, scale_ff)
        b2 = jax.random.uniform(ks[6], (NUM_EXPERTS, D_MODEL), jnp.float32, -scale_ff, scale_ff)
        return {'x': x, 'gate_w': gate_w, 'gate_b': gate_b, 'expert_bias': expert_bias, 'w1': w1, 'b1': b1, 'w2': w2, 'b2': b2}
    _L1_ffn_in = _L1_ffn_setup()
    _d = {'L0_attn_hidden_states': _L0_attn_in['hidden_states'], 'L0_attn_attention_mask': _L0_attn_in['attention_mask'], 'L0_attn_Wk': _L0_attn_in['Wk'], 'L0_attn_bk': _L0_attn_in['bk'], 'L0_attn_Wka': _L0_attn_in['Wka'], 'L0_attn_bka': _L0_attn_in['bka'], 'L0_attn_Wv': _L0_attn_in['Wv'], 'L0_attn_bv': _L0_attn_in['bv'], 'L0_attn_gamma': _L0_attn_in['gamma'], 'L0_attn_beta': _L0_attn_in['beta'], 'L0_ffn_wqkv': _L0_ffn_in['wqkv'], 'L0_ffn_q_scale': _L0_ffn_in['q_scale'], 'L0_ffn_k_scale': _L0_ffn_in['k_scale'], 'L0_ffn_wo': _L0_ffn_in['wo'], 'L0_ffn_ln_g': _L0_ffn_in['ln_g'], 'L0_ffn_ln_b': _L0_ffn_in['ln_b'], 'L0_ffn_w1': _L0_ffn_in['w1'], 'L0_ffn_b1': _L0_ffn_in['b1'], 'L0_ffn_w2': _L0_ffn_in['w2'], 'L0_ffn_b2': _L0_ffn_in['b2'], 'L1_attn_Wq': _L1_attn_in['Wq'], 'L1_attn_bq': _L1_attn_in['bq'], 'L1_attn_Wk': _L1_attn_in['Wk'], 'L1_attn_bk': _L1_attn_in['bk'], 'L1_attn_Wv': _L1_attn_in['Wv'], 'L1_attn_bv': _L1_attn_in['bv'], 'L1_attn_Wo': _L1_attn_in['Wo'], 'L1_attn_bo': _L1_attn_in['bo'], 'L1_ffn_gate_w': _L1_ffn_in['gate_w'], 'L1_ffn_gate_b': _L1_ffn_in['gate_b'], 'L1_ffn_expert_bias': _L1_ffn_in['expert_bias'], 'L1_ffn_w1': _L1_ffn_in['w1'], 'L1_ffn_b1': _L1_ffn_in['b1'], 'L1_ffn_w2': _L1_ffn_in['w2'], 'L1_ffn_b2': _L1_ffn_in['b2']}
    _x0 = _d['L0_attn_hidden_states']
    _d['L0_attn_hidden_states'] = jax.random.normal(jax.random.fold_in(jax.random.key(seed), 1), (16, 512, 128), dtype=_x0.dtype)
    del _x0
    return _d

def reference(L0_attn_hidden_states, L0_attn_attention_mask, L0_attn_Wk, L0_attn_bk, L0_attn_Wka, L0_attn_bka, L0_attn_Wv, L0_attn_bv, L0_attn_gamma, L0_attn_beta, L0_ffn_wqkv, L0_ffn_q_scale, L0_ffn_k_scale, L0_ffn_wo, L0_ffn_ln_g, L0_ffn_ln_b, L0_ffn_w1, L0_ffn_b1, L0_ffn_w2, L0_ffn_b2, L1_attn_Wq, L1_attn_bq, L1_attn_Wk, L1_attn_bk, L1_attn_Wv, L1_attn_bv, L1_attn_Wo, L1_attn_bo, L1_ffn_gate_w, L1_ffn_gate_b, L1_ffn_expert_bias, L1_ffn_w1, L1_ffn_b1, L1_ffn_w2, L1_ffn_b2):

    def _L0_attn_ref(hidden_states, attention_mask, Wk, bk, Wka, bka, Wv, bv, gamma, beta):
        import jax, jax.numpy as jnp
        import numpy as np
        D = 128
        B = 4
        S = 512
        LN_EPS = 1e-05

        def _layer_norm(x, gamma, beta):
            mu = jnp.mean(x, axis=-1, keepdims=True)
            var = jnp.mean(jnp.square(x - mu), axis=-1, keepdims=True)
            return (x - mu) * jax.lax.rsqrt(var + LN_EPS) * gamma + beta
        h = _layer_norm(hidden_states, gamma, beta)
        d_model = h.shape[-1]
        keys = jnp.einsum('bsd,ed->bse', h, Wk) + bk
        values = jnp.einsum('bsd,ed->bse', h, Wv) + bv
        key_att = jnp.einsum('bsd,ed->bse', keys, Wka) + bka
        keys_weight = jnp.exp(key_att / jnp.sqrt(jnp.asarray(d_model, h.dtype)))
        keys_weight = keys_weight / jnp.cumsum(keys_weight, axis=1)
        pooled_keys = jnp.cumsum(keys_weight * keys, axis=1)
        return pooled_keys * values

    def _L0_ffn_ref(x, wqkv, q_scale, k_scale, wo, ln_g, ln_b, w1, b1, w2, b2):
        import jax, jax.numpy as jnp
        import numpy as np
        DIM = 128
        DEPTH = 2
        HEADS = 8
        DIM_HEAD = 64
        WINDOW = 64
        INNER = HEADS * DIM_HEAD
        HID = int(DIM * 4 * 2 / 3)
        B, N = (2, 1024)
        QK_SCALE = 8.0

        def shift_token(t):
            t1, t2 = jnp.split(t, 2, axis=-1)
            t2 = jnp.pad(t2, ((0, 0), (1, 0), (0, 0)))[:, :-1]
            return jnp.concatenate([t1, t2], axis=-1)

        def l2norm(t):
            return t / jnp.clip(jnp.linalg.norm(t, axis=-1, keepdims=True), 1e-12)

        def rotate_half(x):
            x1, x2 = jnp.split(x, 2, axis=-1)
            return jnp.concatenate([-x2, x1], axis=-1)

        def rotary_xpos(q, k):
            n = q.shape[-2]
            half_idx = jnp.arange(0, DIM_HEAD, 2, dtype=jnp.float32)
            inv_freq = 1.0 / 10000.0 ** (half_idx / DIM_HEAD)
            t = jnp.arange(n, dtype=jnp.float32)
            freqs = t[:, None] * inv_freq[None, :]
            freqs = jnp.concatenate([freqs, freqs], axis=-1)
            base = (half_idx + 0.4 * DIM_HEAD) / (1.4 * DIM_HEAD)
            power = (t - n // 2) / float(WINDOW // 2)
            scale = base[None, :] ** power[:, None]
            scale = jnp.concatenate([scale, scale], axis=-1)
            cos, sin = (jnp.cos(freqs), jnp.sin(freqs))
            q = q * cos * scale + rotate_half(q) * sin * scale
            k = k * cos / scale + rotate_half(k) * sin / scale
            return (q, k)

        def local_attention(q, k, v):
            b, h, n, d = q.shape
            w = n // WINDOW
            bq = q.reshape(b, h, w, WINDOW, d) * QK_SCALE
            bk = k.reshape(b, h, w, WINDOW, d)
            bv = v.reshape(b, h, w, WINDOW, d)

            def look_around(t):
                p = jnp.pad(t, ((0, 0), (0, 0), (1, 0), (0, 0), (0, 0)))
                return jnp.concatenate([p[:, :, :w], p[:, :, 1:]], axis=3)
            bk, bv = (look_around(bk), look_around(bv))
            bt = jnp.arange(n).reshape(w, WINDOW)
            btp = jnp.pad(bt, ((1, 0), (0, 0)), constant_values=-1)
            btk = jnp.concatenate([btp[:w], btp[1:]], axis=1)
            sim = jnp.einsum('bhwid,bhwjd->bhwij', bq, bk)
            i = bt[:, :, None]
            j = btk[:, None, :]
            mask = (i < j) | (i > j + WINDOW) | (j == -1)
            sim = jnp.where(mask, -jnp.finfo(sim.dtype).max, sim)
            attn = jax.nn.softmax(sim, axis=-1)
            out = jnp.einsum('bhwij,bhwjd->bhwid', attn, bv)
            return out.reshape(b, h, n, d)

        def _layer(x, wqkv, qs, ksc, wo, lg, lb, w1, b1, w2, b2):
            b, n, _ = x.shape
            h = shift_token(x)
            qkv = h @ wqkv
            q, k, v = jnp.split(qkv, 3, axis=-1)
            to_heads = lambda t: t.reshape(b, n, HEADS, DIM_HEAD).transpose(0, 2, 1, 3)
            q, k, v = (to_heads(q), to_heads(k), to_heads(v))
            q = l2norm(q) * qs
            k = l2norm(k) * ksc
            q, k = rotary_xpos(q, k)
            o = local_attention(q, k, v)
            o = o.transpose(0, 2, 1, 3).reshape(b, n, INNER)
            x = x + o @ wo
            h = shift_token(x)
            mu = h.mean(-1, keepdims=True)
            var = h.var(-1, keepdims=True)
            h = (h - mu) / jnp.sqrt(var + 1e-05) * lg + lb
            h = h @ w1 + b1
            a, g = jnp.split(h, 2, axis=-1)
            h = a * jax.nn.gelu(g, approximate=False)
            x = x + h @ w2 + b2
            return x
        for l in range(DEPTH):
            x = _layer(x, wqkv[l], q_scale[l], k_scale[l], wo[l], ln_g[l], ln_b[l], w1[l], b1[l], w2[l], b2[l])
        return x

    def _L1_attn_ref(x, Wq, bq, Wk, bk, Wv, bv, Wo, bo):
        import jax, jax.numpy as jnp
        import numpy as np
        import math
        DIM, H, T, B = (128, 16, 256, 1)
        BASE = 15000.0

        def _count_mask(t_len, n_heads):
            idx = jnp.arange(t_len)
            hm = jnp.arange(n_heads)
            count = jnp.zeros((n_heads, t_len, t_len), jnp.float32)
            for X in range(int(math.log2(t_len))):
                S, r = (2 ** (X + 2), 2 ** X)
                same_seg = idx[:, None] // S == idx[None, :] // S
                ok = idx[None, :] % r == hm[:, None] % r
                pat = same_seg[None, :, :] & ok[:, :, None] & ok[:, None, :]
                count = count + pat.astype(jnp.float32)
            return count
        Bsz, t_len, d = x.shape
        dh = d // H
        q = x @ Wq.T + bq
        k = x @ Wk.T + bk
        v = x @ Wv.T + bv
        inv_freq = 1.0 / BASE ** (jnp.arange(0, d, 2, dtype=jnp.float32) / d)
        tpos = jnp.arange(t_len, dtype=jnp.float32)
        freqs = tpos[:, None] * inv_freq[None, :]
        emb = jnp.concatenate([freqs, freqs], axis=-1)
        cos, sin = (jnp.cos(emb), jnp.sin(emb))

        def rot_half(u):
            return jnp.concatenate([-u[..., d // 2:], u[..., :d // 2]], axis=-1)
        q = q * cos + rot_half(q) * sin
        k = k * cos + rot_half(k) * sin
        Q = q.reshape(Bsz, t_len, H, dh).transpose(0, 2, 1, 3)
        K = k.reshape(Bsz, t_len, H, dh).transpose(0, 2, 1, 3)
        V = v.reshape(Bsz, t_len, H, dh).transpose(0, 2, 1, 3)
        scores = jnp.einsum('bhtd,bhsd->bhts', Q, K)
        count = _count_mask(t_len, H)
        causal = jnp.tril(jnp.ones((t_len, t_len), bool))
        valid = (count > 0) & causal
        att = jnp.where(valid, scores * count, -jnp.inf)
        att = jax.nn.softmax(att, axis=-1)
        out = jnp.einsum('bhts,bhsd->bhtd', att, V)
        out = out.transpose(0, 2, 1, 3).reshape(Bsz, t_len, d)
        return out @ Wo.T + bo

    def _L1_ffn_ref(x, gate_w, gate_b, expert_bias, w1, b1, w2, b2):
        import jax, jax.numpy as jnp
        import numpy as np
        D_MODEL = 128
        D_FF = 512
        NUM_EXPERTS = 8
        gate_logits = jnp.einsum('bsd,ed->bse', x, gate_w) + gate_b + expert_bias
        top_idx = jnp.argmax(gate_logits, axis=-1)
        out = jnp.zeros_like(x)
        for e in range(NUM_EXPERTS):
            mask = (top_idx == e)[..., None].astype(x.dtype)
            h = jax.nn.relu(jnp.einsum('bsd,df->bsf', x, w1[e]) + b1[e])
            y = jnp.einsum('bsf,fd->bsd', h, w2[e]) + b2[e]
            out = out + mask * y
        return out
    x = L0_attn_hidden_states
    xn = _layernorm(x, axis=-1)
    s = _L0_attn_ref(xn, L0_attn_attention_mask, L0_attn_Wk, L0_attn_bk, L0_attn_Wka, L0_attn_bka, L0_attn_Wv, L0_attn_bv, L0_attn_gamma, L0_attn_beta)
    g = _silu(_L0_ffn_ref(xn, L0_ffn_wqkv, L0_ffn_q_scale, L0_ffn_k_scale, L0_ffn_wo, L0_ffn_ln_g, L0_ffn_ln_b, L0_ffn_w1, L0_ffn_b1, L0_ffn_w2, L0_ffn_b2))
    x = x + s * g
    xn = _layernorm(x, axis=-1)
    s = _L1_attn_ref(xn, L1_attn_Wq, L1_attn_bq, L1_attn_Wk, L1_attn_bk, L1_attn_Wv, L1_attn_bv, L1_attn_Wo, L1_attn_bo)
    g = _silu(_L1_ffn_ref(xn, L1_ffn_gate_w, L1_ffn_gate_b, L1_ffn_expert_bias, L1_ffn_w1, L1_ffn_b1, L1_ffn_w2, L1_ffn_b2))
    x = x + s * g
    return x

_drawn_inputs = setup_inputs


def setup_inputs(seed=0):
    import zlib

    import numpy as np

    out = dict(_drawn_inputs(seed))
    spreads = {'L0_attn_bk': (0.0, 0.1),
     'L0_attn_bka': (0.0, 2.0),
     'L0_attn_bv': (0.0, 0.1),
     'L0_attn_gamma': (1.0, 0.2),
     'L0_attn_beta': (0.0, 0.1),
     'L0_ffn_q_scale': (1.0, 0.6),
     'L0_ffn_k_scale': (1.0, 0.6),
     'L0_ffn_ln_g': (1.0, 0.6),
     'L0_ffn_ln_b': (0.0, 0.8),
     'L0_ffn_b1': (0.0, 0.8),
     'L0_ffn_b2': (0.0, 0.1),
     'L1_attn_bq': (0.0, 0.8),
     'L1_attn_bk': (0.0, 0.8),
     'L1_attn_bv': (0.0, 0.8),
     'L1_attn_bo': (0.0, 0.8),
     'L1_ffn_expert_bias': (0.0, 0.8)}
    factors = {'L0_ffn_w1': 4.178,
     'L0_ffn_w2': 4.119,
     'L1_attn_Wq': 8.0,
     'L1_attn_Wk': 8.0,
     'L1_attn_Wv': 8.0,
     'L1_attn_Wo': 8.0,
     'L1_ffn_gate_w': 6.901,
     'L1_ffn_gate_b': 8.0,
     'L1_ffn_w1': 8.0,
     'L1_ffn_b1': 8.0,
     'L1_ffn_w2': 6.649,
     'L1_ffn_b2': 27.357}
    for name, (base, spread) in spreads.items():
        noise = np.random.default_rng([zlib.crc32(name.encode()), seed]).standard_normal(out[name].shape)
        drawn = base * np.exp(spread * noise) if base else spread * noise
        out[name] = jnp.asarray(drawn.astype(out[name].dtype))
    for name, factor in factors.items():
        out[name] = (out[name] * factor).astype(out[name].dtype)
    return out
```

```python
from contextlib import ExitStack

import numpy as np
import concourse.bass as bass
from concourse import mybir

DEPTH = 2
F32 = mybir.dt.float32
BF16 = mybir.dt.bfloat16
ALU = mybir.AluOpType
ACT = mybir.ActivationFunctionType
AX_X = mybir.AxisListType.X

D = 128
B, N = 16, 512
TT = N // D
EPS = 1e-5
EXP_LN = "natural_log_exp_and_others"


def reach(eng, sem, count):
    if isinstance(count, (int, np.integer)) and count <= 0:
        return
    eng.wait_ge(sem, count)


def columns(i, width=N):
    return bass.ds(i * width, width)


def run_steps(eng, step, steps, lead, unroll):
    for s in range(-lead, unroll):
        step(s, s % unroll, s // unroll)
    with eng.Fori(1, steps // unroll - 1) as r:
        for u in range(unroll):
            step(r * unroll + u, u, r)
    for u in range(unroll):
        step(steps - unroll + u, u, steps // unroll - 1)


def known(s):
    return isinstance(s, (int, np.integer))


def phase_mixer(nc, x_dram, weights, vectors, ident, hid, s_res):
    with ExitStack() as ctx:
        def sb(name, shape, dt=F32):
            return ctx.enter_context(nc.sbuf_tensor("a_" + name, shape, dt))

        def ps(name):
            return ctx.enter_context(nc.psum_tensor("a_" + name, [D, N], F32))

        def sem(name):
            return ctx.enter_context(nc.semaphore("a_" + name))

        x_in = [sb(f"x_in{p}", [D, TT, D]) for p in range(2)]
        xn = [sb(f"xn{p}", [D, TT, D]) for p in range(2)]
        hn = [sb(f"hn{p}", [D, TT, D]) for p in range(2)]
        stats = [sb(f"stats{k}", [D, TT, 6]) for k in range(2)]
        mean_var = [sb(f"mean_var{k}", [D, TT, 2]) for k in range(2)]
        var_eps = [sb(f"var_eps{k}", [D, TT]) for k in range(2)]
        ln_var = [sb(f"ln_var{k}", [D, TT]) for k in range(2)]
        rstd = [sb(f"rstd{k}", [D, TT]) for k in range(2)]
        h_t = [sb(f"h_t{p}", [D, N]) for p in range(2)]
        w_t = sb("w_t", [D, 3, D])
        vecs = sb("vecs", [D, 6])
        bka_scaled = sb("bka_scaled", [D, 1])
        ones = sb("ones", [D, N])
        carrier = sb("carrier", [D, 4])
        keys = sb("keys", [D, N])
        kw = sb("kw", [D, N])
        kw_sum = sb("kw_sum", [D, N])
        kw_inv = sb("kw_inv", [D, N])
        share = sb("share", [D, N])
        weighted = sb("weighted", [D, N])
        pooled = sb("pooled", [D, N])
        xn_ps, hn_ps, k_ps, v_ps, ka_ps = (ps(n) for n in ("xn_ps", "hn_ps", "k_ps", "v_ps", "ka_ps"))

        consts_in = sem("consts_in")
        consts_made = sem("consts_made")
        x_loaded = [sem(f"x_loaded{p}") for p in range(2)]
        bn_done = sem("bn_done")
        aggr_done = sem("aggr_done")
        var_ready = sem("var_ready")
        ln_ready = sem("ln_ready")
        rstd_ready = sem("rstd_ready")
        xn_ready = sem("xn_ready")
        hn_ready = sem("hn_ready")
        xn_turned = sem("xn_turned")
        hn_turned = sem("hn_turned")
        hid_ready = sem("hid_ready")
        h_ready = sem("h_ready")
        k_done = sem("k_done")
        v_done = sem("v_done")
        keys_ready = sem("keys_ready")
        ka_done = sem("ka_done")
        kw_ready = sem("kw_ready")
        sum_ready = sem("sum_ready")
        inv_ready = sem("inv_ready")
        share_ready = sem("share_ready")
        weighted_ready = sem("weighted_ready")
        pooled_ready = sem("pooled_ready")
        s_ready = sem("s_ready")

        scale = 1.0 / np.sqrt(np.float32(D))
        GAMMA, BETA, BK, BKA, BV = range(5)

        with nc.Block() as block:

            @block.sync
            def _(sp):
                sp.dma_start(w_t[:], weights).then_inc(consts_in, 16)
                sp.dma_start(vecs[:, 0:5], vectors).then_inc(consts_in, 16)

                def step(s, u, r):
                    if known(s) and s + 1 >= B:
                        return
                    reach(sp, xn_ready, (s + 1 - 1) * TT)
                    sp.dma_start(x_in[(u + 1) % 2][:], x_dram[s + 1 if known(s) else bass.ds(s + 1, 1)]
                                 .rearrange("(t p) d -> p t d" if known(s) else "o (t p) d -> p (o t) d", p=D)
                                 ).then_inc(x_loaded[(u + 1) % 2], 16)
                run_steps(sp, step, B, 1, 2)

            @block.gpsimd
            def _(pool):
                pool.memset(ones[:], 1.0).then_inc(consts_made, 1)

                def step(s, u, r):
                    if known(s) and s < 0:
                        return
                    pool.wait_ge(share_ready, s + 1)
                    pool.wait_ge(keys_ready, s + 1)
                    reach(pool, pooled_ready, s)
                    pool.tensor_tensor(weighted[:], share[:], keys[:], ALU.mult).then_inc(weighted_ready, 1)
                run_steps(pool, step, B, 1, 2)

            @block.scalar
            def _(act):
                act.preload_act_table_set(EXP_LN)
                act.wait_ge(consts_in, 32)
                act.mul(bka_scaled[:], vecs[:, BKA:BKA + 1], float(scale)).then_inc(consts_made, 1)
                act.wait_ge(consts_made, 2)

                def rstd_of(k, n):
                    act.wait_ge(var_ready, n)
                    act.activation(ln_var[k][:], var_eps[k][:], ACT.Ln).then_inc(ln_ready, 1)
                    act.wait_ge(ln_ready, n)
                    act.activation(rstd[k][:], ln_var[k][:], ACT.Exp, scale=-0.5).then_inc(rstd_ready, 1)

                def step(s, u, r):
                    main = not (known(s) and s < 0)
                    ahead = not (known(s) and s + 1 >= B)
                    if main:
                        act.wait_ge(k_done, s + 1)
                        reach(act, weighted_ready, s)
                        act.activation(keys[:], k_ps[:], ACT.Identity,
                                       bias=vecs[:, BK:BK + 1]).then_inc(keys_ready, 1)
                    if ahead:
                        rstd_of(0, 2 * s + 3)
                    if main:
                        act.wait_ge(ka_done, s + 1)
                        reach(act, share_ready, s)
                        act.activation(kw[:], ka_ps[:], ACT.Exp, scale=float(scale),
                                       bias=bka_scaled[:]).then_inc(kw_ready, 1)
                    if ahead:
                        act.wait_ge(xn_turned, s + 2)
                        act.activation(hid[:, columns(s + 1)], xn_ps[:], ACT.Copy).then_inc(hid_ready, 1)
                        rstd_of(1, 2 * s + 4)
                        act.wait_ge(hn_turned, s + 2)
                        reach(act, v_done, s)
                        act.activation(h_t[(u + 1) % 2][:], hn_ps[:], ACT.Identity,
                                       scale=vecs[:, GAMMA:GAMMA + 1],
                                       bias=vecs[:, BETA:BETA + 1]).then_inc(h_ready, 1)
                run_steps(act, step, B, 1, 2)

            @block.tensor
            def _(pe):
                pe.wait_ge(consts_in, 32)

                def turn(out, src, done):
                    for t in range(TT):
                        ins = pe.transpose(out[:, t * D:(t + 1) * D], src[:, t, :], ident[:])
                    ins.then_inc(done, 1)

                def step(s, u, r):
                    main = not (known(s) and s < 0)
                    ahead = not (known(s) and s + 1 >= B)
                    if main:
                        pe.wait_ge(h_ready, s + 1)
                        reach(pe, keys_ready, s)
                        pe.matmul(k_ps[:], w_t[:, 0, :], h_t[u % 2][:], start=True, stop=True).then_inc(k_done, 1)
                        reach(pe, s_ready, s)
                        pe.matmul(v_ps[:], w_t[:, 2, :], h_t[u % 2][:], start=True, stop=True).then_inc(v_done, 1)
                    if ahead:
                        pe.wait_ge(xn_ready, TT * (s + 2))
                        reach(pe, hid_ready, s + 1)
                        turn(xn_ps, xn[(u + 1) % 2], xn_turned)
                    if main:
                        pe.wait_ge(keys_ready, s + 1)
                        reach(pe, kw_ready, s)
                        pe.matmul(ka_ps[:], w_t[:, 1, :], keys[:], start=True, stop=True).then_inc(ka_done, 1)
                    if ahead:
                        pe.wait_ge(hn_ready, TT * (s + 2))
                        reach(pe, h_ready, s + 1)
                        turn(hn_ps, hn[(u + 1) % 2], hn_turned)
                run_steps(pe, step, B, 1, 2)

            @block.vector
            def _(dve):
                dve.wait_ge(consts_made, 2)

                def variance(k, src, n):
                    for t in range(TT):
                        dve.bn_stats(stats[k][:, t, :], src[:, t, :]).then_inc(bn_done, 1)
                    dve.wait_ge(bn_done, TT * n)
                    reach(dve, xn_ready if k == 0 else hn_ready, TT * ((n - 1) // 2) if known(n) else TT * (n - 1 - k) // 2)
                    dve.memset(carrier[:, 2 * k:2 * k + 1], 0.0)
                    for t in range(TT):
                        dve.bn_aggr(mean_var[k][:, t, :], stats[k][:, t, :]).then_inc(aggr_done, 1)
                    dve.wait_ge(aggr_done, TT * n)
                    dve.tensor_scalar(var_eps[k][:], mean_var[k][:, :, 1], EPS, None, ALU.add).then_inc(var_ready, 1)

                def normalise(k, dst, src, n, ready):
                    dve.wait_ge(rstd_ready, n)
                    for t in range(TT):
                        dve.tensor_scalar(dst[:, t, :], src[:, t, :], mean_var[k][:, t, 0:1], rstd[k][:, t:t + 1],
                                          ALU.subtract, ALU.mult).then_inc(ready, 1)

                def step(s, u, r):
                    main = not (known(s) and s < 0)
                    ahead = not (known(s) and s + 1 >= B)
                    q = (u + 1) % 2
                    if ahead:
                        dve.wait_ge(x_loaded[q], 16 * (r + (u + 1) // 2 + 1))
                        variance(0, x_in[q], 2 * s + 3)
                        reach(dve, xn_turned, s)
                        normalise(0, xn[q], x_in[q], 2 * s + 3, xn_ready)
                        dve.wait_ge(xn_ready, TT * (s + 2))
                        variance(1, xn[q], 2 * s + 4)
                    if main:
                        dve.wait_ge(kw_ready, s + 1)
                        dve.tensor_tensor_scan(kw_sum[:], ones[:], kw[:], 0.0, ALU.mult, ALU.add).then_inc(sum_ready, 1)
                        dve.wait_ge(sum_ready, s + 1)
                        dve.reciprocal(kw_inv[:], kw_sum[:]).then_inc(inv_ready, 1)
                        dve.wait_ge(inv_ready, s + 1)
                        reach(dve, weighted_ready, s)
                        dve.tensor_tensor(share[:], kw[:], kw_inv[:], ALU.mult).then_inc(share_ready, 1)
                    if ahead:
                        reach(dve, hn_turned, s)
                        normalise(1, hn[q], xn[q], 2 * s + 4, hn_ready)
                    if main:
                        dve.wait_ge(weighted_ready, s + 1)
                        dve.tensor_tensor_scan(pooled[:], ones[:], weighted[:], 0.0, ALU.mult, ALU.add).then_inc(pooled_ready, 1)
                        dve.wait_ge(pooled_ready, s + 1)
                        dve.wait_ge(v_done, s + 1)
                        dve.scalar_tensor_tensor(out=s_res[:, columns(s)], in0=v_ps[:], scalar=vecs[:, BV:BV + 1],
                                                 in1=pooled[:], op0=ALU.add, op1=ALU.mult).then_inc(s_ready, 1)
                run_steps(dve, step, B, 1, 2)


HEADS, DH = 8, 64
WIN = 64
INNER = HEADS * DH
NT = B * TT
PAIR = HEADS // 2


def run_tiles(eng, step, lead, lag):
    for s in range(-lead, TT):
        step(s, s % TT)
    with eng.Fori(1, B - 1) as seq:
        for u in range(TT):
            step(seq * TT + u, u)
    for s in range(NT - TT, NT + lag):
        step(s, s % TT)


def inside(t):
    return not known(t) or 0 <= t < NT


def local_attention(nc, own, dram, ident, ident_bf, hid):
    def sb(name, shape, dt=F32):
        return own.enter_context(nc.sbuf_tensor("b_" + name, shape, dt))

    def sem(name):
        return own.enter_context(nc.semaphore("b_" + name))

    wqkv = sb("wqkv", [D, 3 * INNER])
    wo = sb("wo", [D, INNER // D, D])
    scales = sb("scales", [D, 4, DH])
    rope_base = sb("rope_base", [D, 4, TT, DH])
    rope = sb("rope", [D, 4, TT, DH])
    mask = sb("mask", [D, 2, PAIR, D], BF16)
    shift = [sb(f"shift{u}", [D, D]) for u in range(TT)]
    squares = [sb(f"squares{k}", [D, HEADS, DH]) for k in range(2)]
    norm2 = sb("norm2", [D, 2, HEADS])
    norm2_clip = sb("norm2_clip", [D, 2, HEADS])
    norm_ln = sb("norm_ln", [D, 2, HEADS])
    norm_inv = sb("norm_inv", [D, 2, HEADS])
    half_log = sb("half_log", [D, 1])
    by_cos = [sb(f"by_cos{k}", [D, HEADS, DH]) for k in range(2)]
    by_sin = [sb(f"by_sin{k}", [D, HEADS, DH]) for k in range(2)]
    rope_sum = [sb(f"rope_sum{k}", [D, HEADS, DH]) for k in range(2)]
    roped = [sb(f"roped{k}", [D, INNER]) for k in range(2)]
    q_t = sb("q_t", [D, PAIR, D])
    k_t = [sb(f"k_t{u}", [D, PAIR, D]) for u in range(TT)]
    v_odd = [sb(f"v_odd{u}", [D, HEADS, DH + 1]) for u in range(TT)]
    v_even = [sb(f"v_even{u}", [D, HEADS, DH + 1]) for u in range(TT)]
    neg_max = sb("neg_max", [D, 2, PAIR])
    logits = [sb(f"logits{p}", [D, PAIR, D]) for p in range(2)]
    probs = [sb(f"probs{p}", [D, PAIR, D]) for p in range(2)]
    sum_inv = sb("sum_inv", [D, 2, PAIR])
    heads_out = sb("heads_out", [D, HEADS, DH])
    o_t = sb("o_t", [D, INNER // D, D])

    weights_in = sem("weights_in")
    fixed_in = sem("fixed_in")
    tables_ready = sem("tables_ready")
    shifted = sem("shifted")
    proj_done = [sem(f"{x}_done") for x in "qkv"]
    squared = [sem(f"{x}_squared") for x in "qk"]
    products = sem("rope_products")
    sums = sem("rope_sums")
    norms_summed = sem("norms_summed")
    norms_clipped = sem("norms_clipped")
    norms_ln = sem("norms_ln")
    norms_ready = sem("norms_ready")
    roped_ready = sem("roped_ready")
    turned = [sem(f"{x}_turned") for x in "qko"]
    turned_out = [sem(f"{x}_t_ready") for x in "qko"]
    v_ready = sem("v_ready")
    scores_done = sem("scores_done")
    max_ready = sem("max_ready")
    logits_ready = sem("logits_ready")
    logits_turned = sem("logits_turned")
    probs_ready = sem("probs_ready")
    weighed = sem("weighed")
    sum_inv_ready = sem("sum_inv_ready")
    heads_ready = sem("heads_ready")
    y_done = sem("y_done")
    x_updated = sem("x_updated")

    LIFT = 2.0 ** 30

    with nc.Block() as block:

        @block.sync
        def _(sp):
            sp.dma_start(rope_base[:], dram["rope_base"]).then_inc(fixed_in, 16)
            sp.dma_start(mask[:], dram["window_mask"]).then_inc(fixed_in, 16)
            sp.wait_ge(fixed_in, 32)

        @block.vector
        def _(dve):
            for u in range(TT):
                for v in (v_odd, v_even):
                    dve.memset(v[u][:, :, DH:DH + 1], 1.0)
            dve.memset(half_log[:], float(0.5 * np.log(LIFT)))
            dve.memset(shift[0][DH:D, 0:1], 0.0)

    def phase(layer):
        def wait(eng, semaphore, tiles, per=1, more=0):
            if known(tiles) and tiles * per + more <= 0:
                return
            eng.wait_ge(semaphore, layer * (NT * per) + tiles * per + more)

        with ExitStack() as ctx:
            def ps(name, shape):
                return ctx.enter_context(nc.psum_tensor("b_" + name, shape, F32))

            qk_ps = [ps("q_ps", [D, HEADS, DH]), ps("k_ps", [D, HEADS, DH])]
            v_ps = ps("v_ps", [D, HEADS, DH])
            turn_ps = ps("turn_ps", [D, PAIR, D])
            score_ps = [ps(f"score_ps{p}", [D, PAIR, D]) for p in range(2)]
            probs_ps = ps("probs_ps", [D, PAIR, D])
            out_ps = ps("out_ps", [D, 512])
            weighed_ps = out_ps[:, 0:PAIR * (DH + 1)].rearrange("p (h d) -> p h d", h=PAIR)
            y_ps = out_ps[:, 512 - D:512]

            with nc.Block() as block:

                @block.sync
                def _(sp):
                    one = bass.ds(layer, 1)
                    sp.dma_start(wqkv[:], dram["wqkv"][one].rearrange("l p n -> p (l n)")).then_inc(weights_in, 16)
                    sp.dma_start(wo[:], dram["wo"][one].rearrange("l (c p) n -> p (l c) n", p=D)).then_inc(weights_in, 16)
                    for k, name in enumerate(("q_scale", "k_scale")):
                        row = dram[name][one]
                        sp.dma_start(scales[:, 2 * k, :], row.to_broadcast([D, DH])).then_inc(weights_in, 16)
                        for a, b in ((0, DH // 2), (DH // 2, 0)):
                            sp.dma_start(scales[:, 2 * k + 1, a:a + DH // 2],
                                         row[:, b:b + DH // 2].to_broadcast([D, DH // 2])).then_inc(weights_in, 16)

                @block.gpsimd
                def _(pool):
                    def step(s, u):
                        w = (u + 3) % TT
                        if inside(s + 2):
                            for k in range(2):
                                wait(pool, products, s + 2, 6, 3 * k + 3)
                                wait(pool, roped_ready, s + 1, 2, k + 1)
                                pool.tensor_tensor(rope_sum[k][:], by_cos[k][:], by_sin[k][:], ALU.add).then_inc(sums, 1)
                    run_tiles(pool, step, 2, 0)

                @block.scalar
                def _(act):
                    act.preload_act_table_set(EXP_LN)

                    def turn_out(i, dst, t):
                        wait(act, turned[i], t + 1)
                        act.activation(dst[:], turn_ps[:], ACT.Copy).then_inc(turned_out[i], 1)

                    def square(k, t):
                        wait(act, proj_done[k], t + 1)
                        wait(act, norms_summed, t, 2)
                        act.activation(squares[k][:], qk_ps[k][:], ACT.Square).then_inc(squared[k], 1)

                    def exponentials(p, t):
                        wait(act, logits_turned, t, 2, p + 1)
                        wait(act, weighed, t - 1, 2, p + 1)
                        act.activation(probs[p][:], probs_ps[:], ACT.Exp).then_inc(probs_ready, 1)

                    def shift_tokens(t, w):
                        wait(act, proj_done[2], t - 3)
                        act.activation(shift[w][0:DH, :], hid[0:DH, columns(t, D)], ACT.Copy).then_inc(shifted, 1)
                        a = 1 if w == 0 else 0
                        act.activation(shift[w][DH:D, a:D], hid[DH:D, bass.ds(t * D - 1 + a, D - a)],
                                       ACT.Copy).then_inc(shifted, 1)

                    def step(s, u):
                        if inside(s + 3):
                            shift_tokens(s + 3, (u + 3) % TT)
                        if inside(s - 1):
                            wait(act, y_done, s - 1)
                            turn_out(2, o_t, s - 1)
                        if inside(s):
                            exponentials(0, s)
                        if inside(s + 2):
                            square(0, s + 2)
                        if inside(s + 1):
                            wait(act, scores_done, s + 1, 2)
                            turn_out(0, q_t, s + 1)
                            turn_out(1, k_t[(u + 1) % TT], s + 1)
                        if inside(s + 2):
                            square(1, s + 2)
                        if inside(s):
                            exponentials(1, s)
                        if inside(s + 2):
                            w = (u + 2) % TT
                            wait(act, proj_done[2], s + 3)
                            wait(act, weighed, s - 1, 2)
                            act.activation(v_odd[w][:, :, 0:DH], v_ps[:], ACT.Copy).then_inc(v_ready, 1)
                            act.activation(v_even[w][0:WIN, :, 0:DH], v_ps[0:WIN], ACT.Copy).then_inc(v_ready, 1)
                            act.activation(v_even[(w + 1) % TT][WIN:D, :, 0:DH], v_ps[WIN:D], ACT.Copy).then_inc(v_ready, 1)
                            wait(act, norms_clipped, s + 3)
                            act.activation(norm_ln[:], norm2_clip[:], ACT.Ln, scale=LIFT).then_inc(norms_ln, 1)
                            wait(act, norms_ln, s + 3)
                            wait(act, roped_ready, s + 2, 2)
                            act.activation(norm_inv[:], norm_ln[:], ACT.Exp, scale=-0.5, bias=half_log[:]).then_inc(norms_ready, 1)
                    run_tiles(act, step, 3, 1)

                @block.tensor
                def _(pe):
                    pe.wait_ge(weights_in, (layer + 1) * 128)

                    def project(i, t, w, out):
                        wait(pe, shifted, t + 1, 2)
                        pe.matmul(out, shift[w][:], wqkv[:, i * INNER:(i + 1) * INNER],
                                  start=True, stop=True).then_inc(proj_done[i], 1)

                    def turn(i, src, t):
                        for c in range(PAIR):
                            ins = pe.transpose(turn_ps[:, c, :], src[:, c * D:(c + 1) * D], ident[:])
                        ins.then_inc(turned[i], 1)

                    def turn_logits(p, t):
                        wait(pe, logits_ready, t, 2, p + 1)
                        wait(pe, probs_ready, t, 2, p)
                        for h in range(PAIR):
                            ins = pe.transpose(probs_ps[:, h, :], logits[p][:, h, :], ident[:])
                        ins.then_inc(logits_turned, 1)

                    def scores(t, w):
                        wait(pe, turned_out[0], t + 1)
                        wait(pe, turned_out[1], t + 1)
                        for p in range(2):
                            wait(pe, logits_ready, t - 1, 2, p + 1)
                            pe.matmul(score_ps[p][:], ident_bf[:], mask[:, 0 if w == 0 else 1],
                                      start=True, stop=False, skip_group_check=True)
                        for h in range(PAIR):
                            for p in range(2):
                                rows = slice(p * DH, (p + 1) * DH)
                                pe.matmul(score_ps[p][0:WIN, h, 0:WIN], q_t[rows, h, 0:WIN], k_t[w][rows, h, 0:WIN],
                                          start=False, stop=True, skip_group_check=True)
                                if w > 0:
                                    pe.matmul(score_ps[p][0:WIN, h, WIN:D], q_t[rows, h, 0:WIN],
                                              k_t[w - 1][rows, h, WIN:D], start=False, stop=True, skip_group_check=True)
                                ins = pe.matmul(score_ps[p][WIN:D, h, :], q_t[rows, h, WIN:D], k_t[w][rows, h, :],
                                                start=False, stop=True, skip_group_check=True)
                                if h == PAIR - 1:
                                    ins.then_inc(scores_done, 1)

                    def weigh(p, t, w):
                        wait(pe, probs_ready, t, 2, p + 1)
                        wait(pe, v_ready, t + 1, 3)
                        if p == 0:
                            wait(pe, x_updated, t)
                        wait(pe, heads_ready, t, 2, p)
                        keys = D if w > 0 else WIN
                        for h in range(PAIR):
                            pe.matmul(weighed_ps[WIN:D, h, :], probs[p][:, h, WIN:D], v_odd[w][:, 2 * h + p, :],
                                      start=True, stop=True, skip_group_check=True)
                            ins = pe.matmul(weighed_ps[0:WIN, h, :], probs[p][0:keys, h, 0:WIN],
                                            v_even[w][0:keys, 2 * h + p, :], start=True, stop=True, skip_group_check=True)
                        ins.then_inc(weighed, 1)

                    def step(s, u):
                        w1, w2 = (u + 1) % TT, (u + 2) % TT
                        if inside(s - 1):
                            wait(pe, heads_ready, s, 2)
                            wait(pe, turned_out[1], s + 1 if inside(s) else s)
                            turn(2, heads_out[:].rearrange("p h d -> p (h d)"), s - 1)
                        if inside(s):
                            turn_logits(0, s)
                        if inside(s + 2):
                            wait(pe, products, s + 2, 6)
                            project(0, s + 2, w2, qk_ps[0][:])
                        if inside(s + 1):
                            wait(pe, roped_ready, s + 1, 2, 1)
                            wait(pe, turned_out[2], s)
                            turn(0, roped[0], s + 1)
                        if inside(s - 1):
                            wait(pe, turned_out[2], s)
                            wait(pe, heads_ready, s, 2)
                            for c in range(INNER // D):
                                ins = pe.matmul(y_ps, wo[:, c, :], o_t[:, c, :], start=(c == 0), stop=(c == INNER // D - 1))
                            ins.then_inc(y_done, 1)
                        if inside(s):
                            weigh(0, s, u)
                        if inside(s + 1):
                            wait(pe, roped_ready, s + 2, 2)
                            wait(pe, turned_out[0], s + 2)
                            turn(1, roped[1], s + 1)
                        if inside(s + 2):
                            wait(pe, products, s + 2, 6)
                            project(1, s + 2, w2, qk_ps[1][:])
                        if inside(s):
                            turn_logits(1, s)
                        if inside(s + 2):
                            wait(pe, v_ready, s + 2, 3)
                            project(2, s + 2, w2, v_ps[:])
                        if inside(s + 1):
                            scores(s + 1, w1)
                        if inside(s):
                            weigh(1, s, u)
                    run_tiles(pe, step, 3, 1)

                @block.vector
                def _(dve):
                    dve.wait_ge(weights_in, (layer + 1) * 128)
                    for k in range(4):
                        dve.tensor_tensor(rope[:, k], rope_base[:, k],
                                          scales[:, k:k + 1, :].to_broadcast([D, TT, DH]), ALU.mult).then_inc(tables_ready, 1)
                    dve.wait_ge(tables_ready, layer * 4 + 4)

                    half = DH // 2

                    def rotate(k, t, w):
                        wait(dve, squared[k], t + 1)
                        wait(dve, sums, t - 1, 2, k + 1)
                        cos = rope[:, 2 * k, w:w + 1, :]
                        sin = rope[:, 2 * k + 1, w:w + 1, :]
                        dve.tensor_tensor(by_cos[k][:], qk_ps[k][:], cos.to_broadcast([D, HEADS, DH]),
                                          ALU.mult).then_inc(products, 1)
                        for a, b in ((0, half), (half, 0)):
                            dve.tensor_tensor(by_sin[k][:, :, a:a + half], qk_ps[k][:, :, b:b + half],
                                              sin[:, :, a:a + half].to_broadcast([D, HEADS, half]),
                                              ALU.mult).then_inc(products, 1)
                        wait(dve, norms_clipped, t)
                        dve.tensor_reduce(norm2[:, k, :], squares[k][:], AX_X, ALU.add).then_inc(norms_summed, 1)

                    def subtract_max(p, t):
                        wait(dve, scores_done, t, 2, p + 1)
                        dve.tensor_reduce(neg_max[:, p, :], score_ps[p][:], AX_X, ALU.max, negate=True).then_inc(max_ready, 1)
                        wait(dve, max_ready, t, 2, p + 1)
                        wait(dve, logits_turned, t - 1, 2, p + 1)
                        dve.tensor_tensor(logits[p][:], score_ps[p][:],
                                          neg_max[:, p, :].unsqueeze(2).to_broadcast([D, PAIR, D]),
                                          ALU.add).then_inc(logits_ready, 1)

                    def normalise(p, t):
                        wait(dve, weighed, t, 2, p + 1)
                        dve.reciprocal(sum_inv[:, p, :], weighed_ps[:, :, DH]).then_inc(sum_inv_ready, 1)
                        wait(dve, sum_inv_ready, t, 2, p + 1)
                        wait(dve, turned[2], t)
                        dve.tensor_tensor(heads_out[:, p::2, :], weighed_ps[:, :, 0:DH],
                                          sum_inv[:, p, :].unsqueeze(2).to_broadcast([D, PAIR, DH]),
                                          ALU.mult).then_inc(heads_ready, 1)

                    def step(s, u):
                        w1, w2 = (u + 1) % TT, (u + 2) % TT
                        if inside(s - 1):
                            wait(dve, y_done, s)
                            wait(dve, shifted, s + 1 if inside(s) else s, 2)
                            x = hid[:, columns(s - 1, D)]
                            dve.tensor_tensor(x, y_ps, x, ALU.add).then_inc(x_updated, 1)
                        if inside(s + 2):
                            rotate(0, s + 2, w2)
                        if inside(s):
                            normalise(0, s)
                        if inside(s + 2):
                            rotate(1, s + 2, w2)
                            wait(dve, norms_summed, s + 3, 2)
                            wait(dve, norms_ln, s + 2)
                            dve.tensor_scalar(norm2_clip[:], norm2[:], 1e-24, None, ALU.max).then_inc(norms_clipped, 1)
                        if inside(s + 1):
                            subtract_max(0, s + 1)
                            subtract_max(1, s + 1)
                        if inside(s):
                            normalise(1, s)
                        if inside(s + 2):
                            wait(dve, norms_ready, s + 3)
                            for k in range(2):
                                wait(dve, sums, s + 2, 2, k + 1)
                                wait(dve, turned[k], s + 2)
                                dve.tensor_tensor(roped[k][:].rearrange("p (h d) -> p h d", h=HEADS), rope_sum[k][:],
                                                  norm_inv[:, k, :].unsqueeze(2).to_broadcast([D, HEADS, DH]),
                                                  ALU.mult).then_inc(roped_ready, 1)
                    run_tiles(dve, step, 3, 1)
    return phase


def rope_base_table():
    f = np.float32
    half = np.arange(0, DH, 2, dtype=f)
    inv_freq = (f(1.0) / f(10000.0) ** (half / f(DH))).astype(f)
    t = np.arange(N, dtype=f)
    freqs = t[:, None] * inv_freq[None, :]
    freqs = np.concatenate([freqs, freqs], -1)
    base = (half + f(0.4 * DH)) / f(1.4 * DH)
    power = (t - f(N // 2)) / f(WIN // 2)
    scale = (base[None, :] ** power[:, None]).astype(f)
    scale = np.concatenate([scale, scale], -1)
    sign = np.where(np.arange(DH) < DH // 2, f(-1), f(1))
    cos, sin = np.cos(freqs), np.sin(freqs) * sign
    kinds = np.stack([cos * scale * f(8), sin * scale * f(8), cos / scale, sin / scale], 0)
    return np.ascontiguousarray(kinds.reshape(4, TT, D, DH).transpose(2, 0, 1, 3).astype(f))


def window_mask_table():
    i, j = np.arange(WIN)[:, None], np.arange(WIN)[None, :]
    own, prev = j <= i, j >= i
    never = np.zeros_like(own)
    out = np.stack([np.block([[own, never], [prev, own]]), np.block([[own, prev], [prev, own]])], 0)
    out = np.where(out, 0.0, -1e30).astype(mybir.dt.np(BF16))
    return np.ascontiguousarray(np.repeat(out.transpose(1, 0, 2)[:, :, None, :], PAIR, 2))


HID = 341
CHUNKS = [(a, min(D, HID - a)) for a in range(0, HID, D)]


def feed_forward(nc, own, dram, centre, average, hid):
    def sb(name, shape, dt=F32):
        return own.enter_context(nc.sbuf_tensor("f_" + name, shape, dt))

    def sem(name):
        return own.enter_context(nc.semaphore("f_" + name))

    nch = len(CHUNKS)
    w1 = sb("w1", [D, 2 * HID])
    w2 = sb("w2", [D, nch, D])
    b1 = sb("b1", [D, 2, nch])
    vecs = sb("vecs", [D, 3])
    eps = sb("eps", [D, 1])
    LG, LB, B2 = range(3)
    shift = [sb(f"shift{p}", [D, N]) for p in range(2)]
    squares = sb("squares", [D, N])
    ln_var = sb("ln_var", [D, N])
    rstd = sb("rstd", [D, N])
    unit = sb("unit", [D, N])
    h = [sb(f"h{p}", [D, N]) for p in range(2)]
    gate = [sb(f"gate{p}", [D, N]) for p in range(2)]
    gated = [sb(f"gated{c}", [D, N]) for c in range(nch)]

    weights_in = sem("weights_in")
    shifted = sem("shifted")
    centred = sem("centred")
    squared = sem("squared")
    var_done = sem("var_done")
    ln_ready = sem("ln_ready")
    rstd_ready = sem("rstd_ready")
    unit_ready = sem("unit_ready")
    h_ready = sem("h_ready")
    a_done = sem("a_done")
    g_done = sem("g_done")
    gate_ready = sem("gate_ready")
    gated_ready = sem("gated_ready")
    y_done = sem("y_done")
    x_updated = sem("x_updated")
    ALL_WEIGHTS = 16 * (1 + 3 * nch + 3)

    half = D // 2

    with nc.Block() as block:

        @block.vector
        def _(dve):
            dve.memset(eps[:], EPS)
            for p in range(2):
                dve.memset(shift[p][half:D, 0:1], 0.0)

    def phase(layer):
        def wait(eng, semaphore, seqs, per=1, more=0):
            if known(seqs) and seqs * per + more <= 0:
                return
            eng.wait_ge(semaphore, layer * (B * per) + seqs * per + more)

        with ExitStack() as ctx:
            def ps(name):
                return ctx.enter_context(nc.psum_tensor("f_" + name, [D, N], F32))

            centred_ps, var_ps, y_ps = ps("centred_ps"), ps("var_ps"), ps("y_ps")
            a_ps = [ps(f"a_ps{p}") for p in range(2)]
            g_ps = [ps(f"g_ps{p}") for p in range(2)]

            with nc.Block() as block:

                @block.sync
                def _(sp):
                    one = bass.ds(layer, 1)
                    sp.dma_start(w1[:], dram["w1"][one].rearrange("l p n -> p (l n)")).then_inc(weights_in, 16)
                    for c, (a, n) in enumerate(CHUNKS):
                        sp.dma_start(w2[0:n, c, :], dram["w2"][one, a:a + n, :].rearrange("l p n -> p (l n)")).then_inc(weights_in, 16)
                        for k in range(2):
                            sp.dma_start(b1[0:n, k, c:c + 1], dram["b1"][one, k * HID + a:k * HID + a + n]
                                         .rearrange("l p -> p l")).then_inc(weights_in, 16)
                    for k, name in enumerate(("ln_g", "ln_b", "b2")):
                        sp.dma_start(vecs[:, k:k + 1], dram[name][one].rearrange("l p -> p l")).then_inc(weights_in, 16)

                @block.scalar
                def _(act):
                    act.preload_act_table_set(EXP_LN)
                    act.wait_ge(weights_in, (layer + 1) * ALL_WEIGHTS)

                    def shift_tokens(s, w):
                        wait(act, centred, s - 1)
                        act.activation(w[0:half, :], hid[0:half, columns(s)], ACT.Copy).then_inc(shifted, 1)
                        act.activation(w[half:D, 1:N], hid[half:D, bass.ds(s * N, N - 1)], ACT.Copy).then_inc(shifted, 1)

                    def step(s, u, r):
                        main = not (known(s) and s < 0)
                        ahead = not (known(s) and s + 1 >= B)

                        def gelu(c):
                            q, n = (nch * u + c) % 2, CHUNKS[c][1]
                            wait(act, g_done, s, nch, c + 1)
                            wait(act, gated_ready, s, nch, c - 1)
                            act.activation(gate[q][0:n], g_ps[q][0:n], ACT.Gelu, bias=b1[0:n, 1, c:c + 1]).then_inc(gate_ready, 1)
                        if main:
                            gelu(0)
                        if ahead:
                            if known(s) and s < 0:
                                shift_tokens(0, shift[0])
                            wait(act, centred, s + 2)
                            wait(act, var_done, s + 1)
                            act.activation(squares[:], centred_ps[:], ACT.Square).then_inc(squared, 1)
                        if main:
                            gelu(1)
                            gelu(2)
                        if not (known(s) and s + 2 >= B):
                            shift_tokens(s + 2, shift[u % 2])
                        if ahead:
                            act.preload_act_table_set(EXP_LN)
                            wait(act, var_done, s + 2)
                            act.activation(ln_var[:], var_ps[:], ACT.Ln, bias=eps[:]).then_inc(ln_ready, 1)
                            wait(act, ln_ready, s + 2)
                            wait(act, unit_ready, s + 1)
                            act.activation(rstd[:], ln_var[:], ACT.Exp, scale=-0.5).then_inc(rstd_ready, 1)
                    run_steps(act, step, B, 1, 2)

                @block.tensor
                def _(pe):
                    pe.wait_ge(weights_in, (layer + 1) * ALL_WEIGHTS)

                    def step(s, u, r):
                        main = not (known(s) and s < 0)
                        ahead = not (known(s) and s + 1 >= B)

                        def widen(c):
                            (a, n), q = CHUNKS[c], (nch * u + c) % 2
                            wait(pe, h_ready, s + 1)
                            wait(pe, gate_ready, s, nch, c - 1)
                            pe.matmul(g_ps[q][0:n], w1[:, HID + a:HID + a + n], h[u % 2][:], start=True, stop=True).then_inc(g_done, 1)
                            wait(pe, gated_ready, s, nch, c - 1)
                            pe.matmul(a_ps[q][0:n], w1[:, a:a + n], h[u % 2][:], start=True, stop=True).then_inc(a_done, 1)

                        if main:
                            widen(0)
                        if ahead:
                            wait(pe, shifted, s + 2, 2)
                            wait(pe, unit_ready, s + 1)
                            pe.matmul(centred_ps[:], centre[:], shift[(u + 1) % 2][:], start=True, stop=True).then_inc(centred, 1)
                        if main:
                            widen(1)
                        if ahead:
                            wait(pe, squared, s + 2)
                            wait(pe, ln_ready, s + 1)
                            pe.matmul(var_ps[:], average[:], squares[:], start=True, stop=True).then_inc(var_done, 1)
                        if main:
                            widen(2)
                            wait(pe, x_updated, s)
                            for c, (a, n) in enumerate(CHUNKS):
                                wait(pe, gated_ready, s, nch, c + 1)
                                ins = pe.matmul(y_ps[:], w2[0:n, c, :], gated[c][0:n], start=(c == 0), stop=(c == nch - 1))
                            ins.then_inc(y_done, 1)
                    run_steps(pe, step, B, 1, 2)

                @block.vector
                def _(dve):
                    dve.wait_ge(weights_in, (layer + 1) * ALL_WEIGHTS)

                    def step(s, u, r):
                        main = not (known(s) and s < 0)
                        ahead = not (known(s) and s + 1 >= B)

                        def apply_gate(c):
                            q, n = (nch * u + c) % 2, CHUNKS[c][1]
                            wait(dve, gate_ready, s, nch, c + 1)
                            wait(dve, a_done, s, nch, c + 1)
                            wait(dve, y_done, s)
                            dve.scalar_tensor_tensor(out=gated[c][0:n], in0=a_ps[q][0:n], scalar=b1[0:n, 0, c:c + 1],
                                                     in1=gate[q][0:n], op0=ALU.add, op1=ALU.mult).then_inc(gated_ready, 1)
                        if main:
                            for c in range(nch):
                                apply_gate(c)
                        if ahead:
                            wait(dve, rstd_ready, s + 2)
                            wait(dve, h_ready, s + 1)
                            dve.tensor_tensor(unit[:], centred_ps[:], rstd[:], ALU.mult).then_inc(unit_ready, 1)
                            wait(dve, unit_ready, s + 2)
                            wait(dve, a_done, s, nch)
                            dve.tensor_scalar(h[(u + 1) % 2][:], unit[:], vecs[:, LG:LG + 1], vecs[:, LB:LB + 1],
                                              ALU.mult, ALU.add).then_inc(h_ready, 1)
                        if main:
                            wait(dve, y_done, s + 1)
                            x = hid[:, columns(s)]
                            dve.scalar_tensor_tensor(out=x, in0=y_ps[:], scalar=vecs[:, B2:B2 + 1], in1=x,
                                                     op0=ALU.add, op1=ALU.add).then_inc(x_updated, 1)
                    run_steps(dve, step, B, 1, 2)
    return phase


H1, DH1 = 16, 8
LEVELS = int(np.log2(N))
HALO = 3 * N // 4
SKEW = H1
RING = 2 * N + SKEW
NSLOT = [min(3, N // 2 ** x - 1) for x in range(LEVELS)]
NCOL = [N // 2 ** x for x in range(LEVELS)]
PAIRS = [0]
for _x in range(LEVELS):
    PAIRS.append(PAIRS[-1] + NSLOT[_x] * NCOL[_x])
PAIRS = [N + p for p in PAIRS]
NPAIR = -(-PAIRS[-1] // N) * N
NBANK = NPAIR // N


def phase_gate(nc, hid, s_res):
    with ExitStack() as ctx:
        th = [ctx.enter_context(nc.sbuf_tensor(f"g_tanh{p}", [D, N], F32)) for p in range(2)]
        silu2 = [ctx.enter_context(nc.sbuf_tensor(f"g_silu2{p}", [D, N], F32)) for p in range(2)]
        tanh_ready, silu_ready, gated_ready = (
            ctx.enter_context(nc.semaphore("g_" + n)) for n in ("tanh_ready", "silu_ready", "gated_ready"))
        with nc.Block() as block:

            @block.scalar
            def _(act):
                act.preload_act_table_set("exp_and_others")

                def step(s, u, r):
                    reach(act, silu_ready, s - 1)
                    act.activation(th[u][:], hid[:, columns(s)], ACT.Tanh, scale=0.5).then_inc(tanh_ready, 1)
                run_steps(act, step, B, 0, 2)

            @block.vector
            def _(dve):
                def step(s, u, r):
                    dve.wait_ge(tanh_ready, s + 1)
                    reach(dve, gated_ready, s - 1)
                    dve.scalar_tensor_tensor(out=silu2[u][:], in0=th[u][:], scalar=1.0, in1=hid[:, columns(s)],
                                             op0=ALU.add, op1=ALU.mult).then_inc(silu_ready, 1)
                    dve.wait_ge(silu_ready, s + 1)
                    dve.scalar_tensor_tensor(out=s_res[:, columns(s)], in0=silu2[u][:], scalar=0.5,
                                             in1=s_res[:, columns(s)], op0=ALU.mult, op1=ALU.mult).then_inc(gated_ready, 1)
                run_steps(dve, step, B, 0, 2)


def phase_sparse_attention(nc, dram, ident, ident_bf, centre, average, xres, s_res, xn_res):
    with ExitStack() as ctx:
        def sb(name, shape, dt=F32):
            return ctx.enter_context(nc.sbuf_tensor("c_" + name, shape, dt))

        def ps(name):
            return ctx.enter_context(nc.psum_tensor("c_" + name, [D, N], F32))

        def sem(name):
            return ctx.enter_context(nc.semaphore("c_" + name))

        w = sb("w", [D, 6, D])
        vecs = sb("vecs", [D, 6])
        eps = sb("eps", [D, 1])
        rope = sb("rope", [D, 2, N])
        counts = sb("counts", [D, NPAIR])
        mask = sb("mask", [D, NPAIR], BF16)
        same_head = sb("same_head", [D, D])
        x_in = [sb(f"x_in{p}", [D, TT, D]) for p in range(2)]
        squares, ln_var, rstd = sb("squares", [D, N]), sb("ln_var", [D, N]), sb("rstd", [D, N])
        by_cos, by_sin = sb("by_cos", [D, N]), sb("by_sin", [D, N])
        qkv = sb("qkv", [D, 3, N])
        q_skew = sb("q_skew", [D, N])
        kv_skew = [sb(f"kv_skew{p}", [D, 2, HALO + N]) for p in range(2)]
        product = sb("product", [D, NPAIR])
        logits = sb("logits", [D, NPAIR])
        largest = sb("largest", [D, N])
        level_out = [sb(f"level_out{k}", [D, N]) for k in range(2)]
        denominator = largest
        inverse = sb("inverse", [D, N])
        numerator = sb("numerator", [D, N])
        mixed = [sb(f"mixed{p}", [D, N]) for p in range(2)]
        mixed_back = sb("mixed_back", [D, N])
        ring = dram["ring"]
        back = dram["back"]

        x_ps, centred_ps, var_ps, out_ps = ps("x_ps"), ps("centred_ps"), ps("var_ps"), ps("out_ps")
        proj_ps = [ps(f"proj_ps{k}") for k in range(2)]
        pair_ps = [ps(f"pair_ps{k}") for k in range(2)]

        consts_in = sem("consts_in")
        consts_made = sem("consts_made")
        x_loaded = [sem(f"x_loaded{p}") for p in range(2)]
        x_turned = sem("x_turned")
        x_ready = sem("x_ready")
        centred = sem("centred")
        squared = sem("squared")
        var_done = sem("var_done")
        ln_ready = sem("ln_ready")
        rstd_ready = sem("rstd_ready")
        xn_ready = sem("xn_ready")
        proj_done = sem("proj_done")
        rope_products = sem("rope_products")
        qk_ready = sem("qk_ready")
        v_ready = sem("v_ready")
        ring_written = sem("ring_written")
        q_skewed = sem("q_skewed")
        kv_skewed = sem("kv_skewed")
        products = sem("products")
        counted_ready = sem("counted_ready")
        pairs_done = sem("pairs_done")
        logits_ready = sem("logits_ready")
        level_done = sem("level_done")
        folded = sem("folded")
        shifted = sem("shifted")
        exp_ready = sem("exp_ready")
        weighted = sem("weighted")
        inverse_ready = sem("inverse_ready")
        mixed_ready = sem("mixed_ready")
        back_written = sem("back_written")
        back_read = sem("back_read")
        out_done = sem("out_done")
        s_ready = sem("s_ready")
        BQ, BQR, BK, BKR, BV, BO = range(6)
        FOLDS = LEVELS
        CHUNK_COUNT = NBANK
        LOADS = 16 * (6 + 2 + 8 + 4)
        NOPS = 1 + LEVELS

        def slots(buf, x):
            return buf[:, PAIRS[x]:PAIRS[x + 1]].rearrange("p (k m) -> p k m", k=NSLOT[x])

        def queries(buf, x):
            v = buf[:, 0:N].rearrange("p (m r) -> p m r", r=2 ** x)[:, :, 0]
            return v.unsqueeze(1).to_broadcast([D, NSLOT[x], NCOL[x]])

        def own(buf, x):
            return buf[:, 0:N].rearrange("p (m r) -> p m r", r=2 ** x)[:, :, 0]

        def earlier(buf, x):
            r = 2 ** x
            start = HALO - NSLOT[x] * r
            base = buf[:, start:start + 1]
            a = [list(d) for d in base.ap]
            return bass.AP(base.tensor, base.offset, [a[0], [r, NSLOT[x]], [r, NCOL[x]]])

        def skewed(t, p, parts, start, width, rows, step):
            base = t[p]
            first = base.offset + start
            dims = [[DH1 * rows + step, H1], [rows, DH1]]
            if parts is not None:
                first += parts[0] * RING
                dims += [[RING, parts[1]]] if parts[1] > 1 else []
            return bass.AP(base.tensor, first, dims + [[1, width]])

        def ahead(s):
            return not (known(s) and s + 1 >= B)

        def main(s):
            return not (known(s) and not 0 <= s < B)

        def behind(s):
            return not (known(s) and not 0 <= s - 1 < B)

        def run(eng, step):
            run_steps(eng, step, B, 1, 2)
            step(B, 0, B // 2)

        with nc.Block() as block:

            @block.sync
            def _(sp):
                for k, name in enumerate(("Wq", "Wk")):
                    half = D // 2
                    sp.dma_start(w[:, 2 * k, :], dram[name]).then_inc(consts_in, 16)
                    for a, b in ((0, half), (half, 0)):
                        sp.dma_start(w[:, 2 * k + 1, a:a + half], dram[name][:, b:b + half]).then_inc(consts_in, 16)
                for k, name in enumerate(("Wv", "Wo")):
                    sp.dma_start(w[:, 4 + k, :], dram[name]).then_inc(consts_in, 16)
                for k, name in enumerate(("bq", "bk")):
                    half = D // 2
                    sp.dma_start(vecs[:, 2 * k:2 * k + 1], dram[name]).then_inc(consts_in, 16)
                    for a, b in ((0, half), (half, 0)):
                        sp.dma_start(vecs[a:a + half, 2 * k + 1:2 * k + 2], dram[name][b:b + half]).then_inc(consts_in, 16)
                for k, name in enumerate(("bv", "bo")):
                    sp.dma_start(vecs[:, 4 + k:5 + k], dram[name]).then_inc(consts_in, 16)
                for dst, name in ((rope, "rope1"), (counts, "counts"), (mask, "pair_mask"), (same_head, "same_head")):
                    sp.dma_start(dst[:], dram[name]).then_inc(consts_in, 16)

                def step(s, u, r):
                    n, q = s + 1, (u + 1) % 2
                    if ahead(s):
                        if not (known(s) and s < 0):
                            sp.wait_ge(x_turned, s)
                        src = (dram["x"][n] if known(n) else dram["x"][bass.ds(n, 1)].rearrange("o t d -> (o t) d"))
                        sp.dma_start(x_in[q][:], src.rearrange("(t p) d -> p t d", p=D)).then_inc(x_loaded[q], 16)
                    if behind(s):
                        reach(sp, out_done, s - 1)
                        sp.wait_ge(mixed_ready, s)
                        m = mixed[(u + 1) % 2]
                        sp.dma_start(back[(u + 1) % 2].rearrange("p (a n) -> p a n", a=2),
                                     m[:].unsqueeze(1).to_broadcast([D, 2, N])).then_inc(back_written, 16)
                        sp.wait_ge(back_written, 16 * s)
                        sp.dma_start(mixed_back[:],
                                     skewed(back, (u + 1) % 2, None, N, N, 2 * N, -1)).then_inc(back_read, 16)
                    if ahead(s):
                        sp.wait_ge(qk_ready, 2 * (s + 2))
                        sp.wait_ge(v_ready, s + 2)
                        sp.dma_start(ring[q][:, :, 0:2 * N].rearrange("p c (a n) -> p c a n", a=2)[:, :, 0],
                                     qkv[:]).then_inc(ring_written, 16)
                        sp.dma_start(ring[q][:, :, 0:2 * N].rearrange("p c (a n) -> p c a n", a=2)[:, :, 1],
                                     qkv[:]).then_inc(ring_written, 16)
                        sp.dma_start(ring[q][:, :, 2 * N:RING], qkv[:, :, 0:SKEW]).then_inc(ring_written, 16)
                        sp.wait_ge(ring_written, 48 * (s + 2))
                        reach(sp, products, NOPS * s + NOPS)
                        sp.dma_start(q_skew[:],
                                     skewed(ring, q, (0, 1), N, N, 3 * RING, 1)).then_inc(q_skewed, 16)
                        reach(sp, weighted, NOPS * s)
                        for c in range(2):
                            sp.dma_start(kv_skew[q][:, c, :],
                                         skewed(ring, q, (1 + c, 1), N - HALO, HALO + N, 3 * RING, 1)).then_inc(kv_skewed, 16)
                run(sp, step)

            @block.gpsimd
            def _(pool):
                pool.memset(product[:, PAIRS[-1]:NPAIR], 0.0).then_inc(consts_made, 1)
                pool.memset(eps[:], EPS).then_inc(consts_made, 1)
                pool.wait_ge(consts_in, LOADS)
                pool.wait_ge(consts_made, 2)

                def step(s, u, r):
                    if main(s):
                        for x in range(LEVELS + 1):
                            cols = slice(0, N) if x == LEVELS else slice(PAIRS[x], PAIRS[x + 1])
                            pool.wait_ge(products, NOPS * s + 1 + x if known(s) else s * NOPS + 1 + x)
                            pool.tensor_tensor(product[:, cols], product[:, cols], counts[:, cols],
                                               ALU.mult).then_inc(counted_ready, 1)
                run(pool, step)

            @block.scalar
            def _(act):
                act.preload_act_table_set(EXP_LN)
                act.wait_ge(consts_in, LOADS)
                act.wait_ge(consts_made, 2)

                def evacuate(b, s):
                    act.wait_ge(pairs_done, s * NBANK + b + 1)
                    if b == 0:
                        reach(act, weighted, s * NOPS)
                    act.activation(logits[:, b * N:(b + 1) * N], pair_ps[b % 2][:], ACT.Copy).then_inc(logits_ready, 1)

                def step(s, u, r):
                    if ahead(s):
                        act.wait_ge(centred, s + 2)
                        reach(act, var_done, s + 1)
                        act.activation(squares[:], centred_ps[:], ACT.Square).then_inc(squared, 1)
                    if main(s):
                        for b in range(NBANK):
                            evacuate(b, s)
                    if ahead(s):
                        act.wait_ge(var_done, s + 2)
                        act.activation(ln_var[:], var_ps[:], ACT.Ln, bias=eps[:]).then_inc(ln_ready, 1)
                        act.wait_ge(ln_ready, s + 2)
                        reach(act, xn_ready, s + 1)
                        act.activation(rstd[:], ln_var[:], ACT.Exp, scale=-0.5).then_inc(rstd_ready, 1)
                    if behind(s):
                        act.wait_ge(out_done, s)
                        act.activation(s_res[:, columns(s - 1)], out_ps[:], ACT.Identity,
                                       bias=vecs[:, BO:BO + 1]).then_inc(s_ready, 1)
                    if ahead(s):
                        act.wait_ge(proj_done, 5 * (s + 2))
                        reach(act, ring_written, 48 * (s + 1))
                        act.activation(qkv[:, 2, :], proj_ps[0][:], ACT.Identity, bias=vecs[:, BV:BV + 1]).then_inc(v_ready, 1)
                    if main(s):
                        act.wait_ge(shifted, NOPS * (s + 1))
                        act.activation(logits[:], logits[:], ACT.Exp).then_inc(exp_ready, 1)
                run(act, step)

            @block.tensor
            def _(pe):
                pe.wait_ge(consts_in, LOADS)

                def project(k, bank, s):
                    pe.matmul(proj_ps[bank][:], w[:, k, :], xn_res[:, columns(s + 1)], start=True, stop=True).then_inc(proj_done, 1)

                def step(s, u, r):
                    q = (u + 1) % 2
                    if ahead(s):
                        pe.wait_ge(x_loaded[q], 16 * (r + (u + 1) // 2 + 1))
                        reach(pe, x_ready, s + 1)
                        for t in range(TT):
                            ins = pe.transpose(x_ps[:, t * D:(t + 1) * D], x_in[q][:, t, :], ident[:])
                        ins.then_inc(x_turned, 1)
                        pe.wait_ge(x_ready, s + 2)
                        reach(pe, xn_ready, s + 1)
                        pe.matmul(centred_ps[:], centre[:], xres[:, columns(s + 1)], start=True, stop=True).then_inc(centred, 1)
                    if main(s):
                        for b in range(NBANK):
                            if b == 1 and ahead(s):
                                pe.wait_ge(squared, s + 2)
                                reach(pe, ln_ready, s + 1)
                                pe.matmul(var_ps[:], average[:], squares[:], start=True, stop=True).then_inc(var_done, 1)
                            reach(pe, logits_ready, s * NBANK + max(b - 1, 0))
                            pe.matmul(pair_ps[b % 2][:], ident_bf[:], mask[:, b * N:(b + 1) * N],
                                      start=True, stop=False, skip_group_check=True)
                            pe.wait_ge(counted_ready, s * NOPS + (LEVELS + 1))
                            pe.matmul(pair_ps[b % 2][:], same_head[:], product[:, b * N:(b + 1) * N],
                                      start=False, stop=True, skip_group_check=True).then_inc(pairs_done, 1)
                    elif ahead(s):
                        pe.wait_ge(squared, s + 2)
                        reach(pe, ln_ready, s + 1)
                        pe.matmul(var_ps[:], average[:], squares[:], start=True, stop=True).then_inc(var_done, 1)
                    if behind(s):
                        pe.wait_ge(back_read, 16 * s)
                        reach(pe, s_ready, s - 1)
                        pe.matmul(out_ps[:], w[:, 5, :], mixed_back[:], start=True, stop=True).then_inc(out_done, 1)
                    if ahead(s):
                        pe.wait_ge(xn_ready, s + 2)
                        reach(pe, v_ready, s + 1)
                        project(0, 0, s)
                        project(1, 1, s)
                        pe.wait_ge(rope_products, 4 * (s + 1) + 2)
                        project(2, 0, s)
                        project(3, 1, s)
                        pe.wait_ge(rope_products, 4 * (s + 1) + 4)
                        project(4, 0, s)
                run(pe, step)

            @block.vector
            def _(dve):
                dve.wait_ge(consts_in, LOADS)

                def fold(src, out, op, n, done):
                    x0 = slots(src, 0)
                    for x in range(LEVELS):
                        part = level_out[x % 2][:, 0:NCOL[x]]
                        if x >= 2:
                            dve.wait_ge(folded, n + x - 1)
                        else:
                            reach(dve, folded, n)
                        if NSLOT[x] > 1:
                            dve.tensor_reduce(part, slots(src, x).rearrange("p k m -> p m k"), AX_X, op).then_inc(level_done, 1)
                        else:
                            dve.tensor_copy(part, slots(src, x)[:, 0, :]).then_inc(level_done, 1)
                        dve.wait_ge(level_done, n + x + 1)
                        if x > 0:
                            dve.wait_ge(folded, n + x)
                        first = src[:, 0:N] if x == 0 else own(out, x)
                        dve.tensor_tensor(own(out, x), first, part, op).then_inc(folded, 1)
                    dve.wait_ge(folded, n + LEVELS)

                def step(s, u, r):
                    q = (u + 1) % 2
                    cols = columns(s + 1)
                    if ahead(s):
                        dve.wait_ge(x_turned, s + 2)
                        dve.tensor_tensor(xres[:, cols], x_ps[:], s_res[:, cols], ALU.add).then_inc(x_ready, 1)
                    if main(s):
                        dve.wait_ge(q_skewed, 16 * (s + 1))
                        dve.wait_ge(kv_skewed, 32 * (s + 1))
                        kv = kv_skew[u % 2]
                        reach(dve, mixed_ready, s)
                        reach(dve, counted_ready, s * NOPS)
                        for x in range(LEVELS):
                            dve.tensor_tensor(slots(product, x), queries(q_skew, x), earlier(kv[:, 0, :], x),
                                              ALU.mult).then_inc(products, 1)
                        dve.tensor_tensor(product[:, 0:N], q_skew[:], kv[:, 0, HALO:], ALU.mult).then_inc(products, 1)
                        dve.wait_ge(logits_ready, (s + 1) * NBANK)
                        fold(logits, largest, ALU.max, s * (3 * LEVELS), None)
                        for x in range(LEVELS):
                            dve.tensor_tensor(slots(logits, x), slots(logits, x), queries(largest, x),
                                              ALU.subtract).then_inc(shifted, 1)
                        dve.tensor_tensor(logits[:, 0:N], logits[:, 0:N], largest[:], ALU.subtract).then_inc(shifted, 1)
                    if ahead(s):
                        dve.wait_ge(rstd_ready, s + 2)
                        dve.tensor_tensor(xn_res[:, cols], centred_ps[:], rstd[:], ALU.mult).then_inc(xn_ready, 1)
                        for k in range(2):
                            dve.wait_ge(proj_done, 5 * (s + 1) + 2 * k + 2)
                            reach(dve, qk_ready, 2 * (s + 1) + k)
                            dve.scalar_tensor_tensor(out=by_cos[:], in0=proj_ps[0][:], scalar=vecs[:, 2 * k:2 * k + 1],
                                                     in1=rope[:, 0, :], op0=ALU.add, op1=ALU.mult).then_inc(rope_products, 1)
                            dve.scalar_tensor_tensor(out=by_sin[:], in0=proj_ps[1][:], scalar=vecs[:, 2 * k + 1:2 * k + 2],
                                                     in1=rope[:, 1, :], op0=ALU.add, op1=ALU.mult).then_inc(rope_products, 1)
                            dve.wait_ge(rope_products, 4 * (s + 1) + 2 * k + 2)
                            if k == 0:
                                reach(dve, ring_written, 48 * (s + 1))
                            dve.tensor_tensor(qkv[:, k, :], by_cos[:], by_sin[:], ALU.add).then_inc(qk_ready, 1)
                    if main(s):
                        n = s * (3 * LEVELS)
                        dve.wait_ge(exp_ready, s + 1)
                        fold(logits, denominator, ALU.add, n + LEVELS, None)
                        dve.reciprocal(inverse[:], denominator[:]).then_inc(inverse_ready, 1)
                        kv = kv_skew[u % 2]
                        for x in range(LEVELS):
                            dve.tensor_tensor(slots(product, x), slots(logits, x), earlier(kv[:, 1, :], x),
                                              ALU.mult).then_inc(weighted, 1)
                        dve.tensor_tensor(product[:, 0:N], logits[:, 0:N], kv[:, 1, HALO:], ALU.mult).then_inc(weighted, 1)
                        dve.wait_ge(weighted, (s + 1) * NOPS)
                        fold(product, numerator, ALU.add, n + 2 * LEVELS, None)
                        dve.wait_ge(inverse_ready, s + 1)
                        reach(dve, back_written, 16 * (s - 1))
                        dve.tensor_tensor(mixed[u % 2][:], numerator[:], inverse[:], ALU.mult).then_inc(mixed_ready, 1)
                run(dve, step)


def rope1_table():
    f = np.float32
    inv_freq = (f(1.0) / f(15000.0) ** (np.arange(0, D, 2, dtype=f) / f(D))).astype(f)
    freqs = np.arange(N, dtype=f)[:, None] * inv_freq[None, :]
    emb = np.concatenate([freqs, freqs], -1).T
    sign = np.where(np.arange(D) < D // 2, f(-1), f(1))[:, None]
    return np.ascontiguousarray(np.stack([np.cos(emb), np.sin(emb) * sign], 1).astype(f))


def pair_tables():
    counts = np.zeros((H1, NPAIR), np.float32)
    idx = np.arange(N)
    for h in range(H1):
        count = np.zeros((N, N), np.float32)
        for x in range(LEVELS):
            ok = idx % 2 ** x == h % 2 ** x
            count += (idx[:, None] // 2 ** (x + 2) == idx[None, :] // 2 ** (x + 2)) & ok[:, None] & ok[None, :]
        taken = np.zeros((N, N), bool)
        counts[h, 0:N] = count[(idx + h) % N, (idx + h) % N]
        for x in reversed(range(LEVELS)):
            r = 2 ** x
            for slot in range(NSLOT[x]):
                k = NSLOT[x] - slot
                for m in range(NCOL[x]):
                    i = (m * r + h) % N
                    j = i - k * r
                    if j < 0 or taken[i, j] or count[i, j] == 0:
                        continue
                    taken[i, j] = True
                    counts[h, PAIRS[x] + slot * NCOL[x] + m] = count[i, j]
        need = (count > 0) & (idx[None, :] < idx[:, None])
        assert (taken == need).all()
    mask = np.where(counts > 0, 0.0, -1e30).astype(mybir.dt.np(BF16))
    return np.repeat(counts, DH1, 0), np.repeat(mask, DH1, 0)


EXPERTS, DFF = 8, 512
FC = DFF // D


def phase_experts(nc, dram, ident, ident_bf, xres, s_res, xn_res):
    with ExitStack() as ctx:
        def sb(name, shape, dt=F32):
            return ctx.enter_context(nc.sbuf_tensor("e_" + name, shape, dt))

        def ps(name, shape=(D, N)):
            return ctx.enter_context(nc.psum_tensor("e_" + name, list(shape), F32))

        def sem(name):
            return ctx.enter_context(nc.semaphore("e_" + name))

        w1 = sb("w1", [D, EXPERTS, DFF])
        w2 = sb("w2", [D, EXPERTS, FC, D])
        b1 = sb("b1", [D, EXPERTS, FC])
        b2 = sb("b2", [EXPERTS, D])
        gate_w = sb("gate_w", [D, EXPERTS])
        gate_b = sb("gate_b", [D, 2, EXPERTS])
        rank = sb("rank", [D, EXPERTS])
        silence = sb("silence", [EXPERTS, EXPERTS, D], BF16)
        xs = [sb(f"xs{p}", [D, N]) for p in range(2)]
        small = [sb(f"small{k}", [D, TT, EXPERTS]) for k in range(4)]
        top = [sb(f"top{k}", [D, TT]) for k in range(2)]
        one_hot = sb("one_hot", [D, TT, EXPERTS], BF16)
        chosen = [sb(f"chosen{p}", [EXPERTS, N]) for p in range(2)]
        chosen_bf = [sb(f"chosen_bf{p}", [EXPERTS, N], BF16) for p in range(2)]
        hidden = [sb(f"hidden{k}", [D, N]) for k in range(2 * FC)]
        th, silu2, mixed, result = sb("th", [D, N]), sb("silu2", [D, N]), sb("mixed", [D, N]), sb("result", [D, N])
        out_sb = [sb(f"out_sb{p}", [D, TT, D]) for p in range(2)]

        logit_ps = ps("logit_ps", [D, TT, EXPERTS])
        chosen_ps = ps("chosen_ps")
        hidden_ps = [ps(f"hidden_ps{k}") for k in range(FC)]
        y_ps = ps("y_ps")
        out_ps = ps("out_ps", [D, TT, D])

        consts_in = sem("consts_in")
        xs_ready = sem("xs_ready")
        logits_done = sem("logits_done")
        small_done = sem("small_done")
        one_hot_ready = sem("one_hot_ready")
        chosen_done = sem("chosen_done")
        chosen_ready = sem("chosen_ready")
        hidden_done = sem("hidden_done")
        relu_act = sem("relu_act")
        relu_dve = sem("relu_dve")
        expert_done = sem("expert_done")
        tanh_ready = sem("tanh_ready")
        silu_ready = sem("silu_ready")
        mixed_ready = sem("mixed_ready")
        result_ready = sem("result_ready")
        result_turned = sem("result_turned")
        out_ready = sem("out_ready")
        out_stored = [sem(f"out_stored{p}") for p in range(2)]

        SMALL = 6
        LOADS = 16 * 10
        HALF = FC // 2

        def ahead(s):
            return not (known(s) and s + 1 >= B)

        def main(s):
            return not (known(s) and s < 0)

        with nc.Block() as block:

            @block.sync
            def _(sp):
                sp.dma_start(gate_w[:], dram["gate_w"]).then_inc(consts_in, 16)
                for k, name in enumerate(("gate_b", "expert_bias")):
                    sp.dma_start(gate_b[:, k, :], dram[name].to_broadcast([D, EXPERTS])).then_inc(consts_in, 16)
                sp.dma_start(rank[:], dram["rank"]).then_inc(consts_in, 16)
                sp.dma_start(silence[:], dram["silence"]).then_inc(consts_in, 16)
                sp.dma_start(b2[:], dram["b2"]).then_inc(consts_in, 16)
                sp.dma_start(b1[:], dram["b1"]).then_inc(consts_in, 16)
                sp.dma_start(w1[:], dram["w1"].rearrange("e p n -> p e n")).then_inc(consts_in, 16)
                for k in range(2):
                    e = slice(k * EXPERTS // 2, (k + 1) * EXPERTS // 2)
                    sp.dma_start(w2[:, e], dram["w2"][e].rearrange("e (c p) n -> p e c n", p=D)).then_inc(consts_in, 16)

                def step(s, u, r):
                    if main(s):
                        sp.wait_ge(out_ready, s + 1)
                        dst = (dram["out"][s] if known(s) else dram["out"][bass.ds(s, 1)].rearrange("o t d -> (o t) d"))
                        sp.dma_start(dst.rearrange("(t p) d -> p t d", p=D), out_sb[u][:]).then_inc(out_stored[u], 16)
                run_steps(sp, step, B, 1, 2)
                for p in range(2):
                    sp.wait_ge(out_stored[p], 16 * (B // 2))

            @block.scalar
            def _(act):
                act.preload_act_table_set("exp_and_others")
                act.wait_ge(consts_in, LOADS)

                def step(s, u, r):
                    q = (u + 1) % 2
                    if ahead(s):
                        reach(act, expert_done, EXPERTS * s)
                        act.activation(xs[q][:], xn_res[:, columns(s + 1)], ACT.Copy).then_inc(xs_ready, 1)
                    if main(s):
                        for e in range(EXPERTS):
                            for c in range(HALF):
                                act.wait_ge(hidden_done, s * EXPERTS * FC + e * FC + c + 1)
                                reach(act, expert_done, s * EXPERTS + e - 1)
                                act.activation(hidden[(e % 2) * FC + c][:], hidden_ps[c][:], ACT.Relu,
                                               bias=b1[:, e, c:c + 1]).then_inc(relu_act, 1)
                            if e == 3 and ahead(s):
                                act.wait_ge(chosen_done, s + 2)
                                reach(act, expert_done, EXPERTS * s)
                                act.activation(chosen[q][:], chosen_ps[0:EXPERTS], ACT.Copy).then_inc(chosen_ready, 1)
                                act.activation(chosen_bf[q][:], chosen_ps[0:EXPERTS], ACT.Copy).then_inc(chosen_ready, 1)
                        act.wait_ge(expert_done, EXPERTS * (s + 1))
                        reach(act, silu_ready, s)
                        act.activation(th[:], y_ps[:], ACT.Tanh, scale=0.5).then_inc(tanh_ready, 1)
                        act.wait_ge(result_turned, s + 1)
                        if not known(s) or s >= 2:
                            act.wait_ge(out_stored[u], 16 * r)
                        act.activation(out_sb[u][:], out_ps[:], ACT.Copy).then_inc(out_ready, 1)
                    else:
                        act.wait_ge(chosen_done, s + 2)
                        act.activation(chosen[q][:], chosen_ps[0:EXPERTS], ACT.Copy).then_inc(chosen_ready, 1)
                        act.activation(chosen_bf[q][:], chosen_ps[0:EXPERTS], ACT.Copy).then_inc(chosen_ready, 1)
                run_steps(act, step, B, 1, 2)

            @block.tensor
            def _(pe):
                pe.wait_ge(consts_in, LOADS)

                def step(s, u, r):
                    q = (u + 1) % 2

                    def route_logits():
                        pe.wait_ge(xs_ready, s + 2)
                        reach(pe, small_done, SMALL * (s + 1))
                        for t in range(TT):
                            ins = pe.matmul(logit_ps[:, t, :], xs[q][:, t * D:(t + 1) * D], gate_w[:],
                                            start=True, stop=True, skip_group_check=True)
                        ins.then_inc(logits_done, 1)

                    def turn_choice():
                        pe.wait_ge(one_hot_ready, s + 2)
                        reach(pe, chosen_ready, 2 * (s + 1))
                        for t in range(TT):
                            ins = pe.matmul(chosen_ps[0:EXPERTS, t * D:(t + 1) * D], one_hot[:, t, :], ident_bf[:],
                                            start=True, stop=True, skip_group_check=True)
                        ins.then_inc(chosen_done, 1)

                    def down(e):
                        for c in range(FC):
                            if c < HALF:
                                pe.wait_ge(relu_act, (s * EXPERTS + e) * HALF + c + 1)
                            else:
                                pe.wait_ge(relu_dve, (s * EXPERTS + e) * HALF + c - HALF + 1)
                            ins = pe.matmul(y_ps[:], w2[:, e, c, :], hidden[(e % 2) * FC + c][:],
                                            start=False, stop=(e == EXPERTS - 1 and c == FC - 1), skip_group_check=True)
                        ins.then_inc(expert_done, 1)

                    if ahead(s):
                        route_logits()
                    if main(s):
                        pe.wait_ge(chosen_ready, 2 * (s + 1))
                        reach(pe, silu_ready, s)
                        pe.matmul(y_ps[:], b2[:], chosen[u][:], start=True, stop=False, skip_group_check=True)
                        for e in range(EXPERTS):
                            for c in range(FC):
                                n = (s * EXPERTS + e - 1) * HALF + (c % HALF) + 1
                                reach(pe, relu_act if c < HALF else relu_dve, n)
                                pe.matmul(hidden_ps[c][:], silence[:, e, :], chosen_bf[u][:],
                                          start=True, stop=False, skip_group_check=True)
                                pe.matmul(hidden_ps[c][:], w1[:, e, c * D:(c + 1) * D], xs[u][:],
                                          start=False, stop=True, skip_group_check=True).then_inc(hidden_done, 1)
                            if e > 0:
                                down(e - 1)
                            if e == 2 and ahead(s):
                                turn_choice()
                        down(EXPERTS - 1)
                        pe.wait_ge(result_ready, s + 1)
                        reach(pe, out_ready, s)
                        for t in range(TT):
                            ins = pe.transpose(out_ps[:, t, :], result[:, t * D:(t + 1) * D], ident[:])
                        ins.then_inc(result_turned, 1)
                    else:
                        turn_choice()
                run_steps(pe, step, B, 1, 2)

            @block.vector
            def _(dve):
                dve.wait_ge(consts_in, LOADS)

                def step(s, u, r):
                    if ahead(s):
                        n = SMALL * (s + 1)
                        logit, logit2, tied, best = small
                        dve.wait_ge(logits_done, s + 2)
                        dve.tensor_tensor(logit[:], logit_ps[:], gate_b[:, 0:1, :].to_broadcast([D, TT, EXPERTS]),
                                          ALU.add).then_inc(small_done, 1)
                        dve.wait_ge(small_done, n + 1)
                        dve.tensor_tensor(logit2[:], logit[:], gate_b[:, 1:2, :].to_broadcast([D, TT, EXPERTS]),
                                          ALU.add).then_inc(small_done, 1)
                        dve.wait_ge(small_done, n + 2)
                        dve.tensor_reduce(top[0][:], logit2[:], AX_X, ALU.max).then_inc(small_done, 1)
                        dve.wait_ge(small_done, n + 3)
                        dve.tensor_tensor(tied[:], logit2[:], top[0][:].unsqueeze(2).to_broadcast([D, TT, EXPERTS]),
                                          ALU.is_ge).then_inc(small_done, 1)
                        dve.wait_ge(small_done, n + 4)
                        dve.tensor_tensor(best[:], tied[:], rank[:].unsqueeze(1).to_broadcast([D, TT, EXPERTS]),
                                          ALU.mult).then_inc(small_done, 1)
                        dve.wait_ge(small_done, n + 5)
                        dve.tensor_reduce(top[1][:], best[:], AX_X, ALU.max).then_inc(small_done, 1)
                        dve.wait_ge(small_done, n + 6)
                        reach(dve, chosen_done, s + 1)
                        dve.tensor_tensor(one_hot[:], best[:], top[1][:].unsqueeze(2).to_broadcast([D, TT, EXPERTS]),
                                          ALU.is_equal).then_inc(one_hot_ready, 1)
                    if main(s):
                        for e in range(EXPERTS):
                            for c in range(HALF, FC):
                                dve.wait_ge(hidden_done, (s * EXPERTS + e) * FC + c + 1)
                                reach(dve, expert_done, s * EXPERTS + e - 1)
                                dve.tensor_scalar(hidden[(e % 2) * FC + c][:], hidden_ps[c][:], b1[:, e, c:c + 1], 0.0,
                                                  ALU.add, ALU.max).then_inc(relu_dve, 1)
                        cols = columns(s)
                        dve.wait_ge(tanh_ready, s + 1)
                        dve.wait_ge(expert_done, EXPERTS * (s + 1))
                        dve.scalar_tensor_tensor(out=silu2[:], in0=th[:], scalar=1.0, in1=y_ps[:],
                                                 op0=ALU.add, op1=ALU.mult).then_inc(silu_ready, 1)
                        dve.wait_ge(silu_ready, s + 1)
                        dve.scalar_tensor_tensor(out=mixed[:], in0=silu2[:], scalar=0.5, in1=s_res[:, cols],
                                                 op0=ALU.mult, op1=ALU.mult).then_inc(mixed_ready, 1)
                        dve.wait_ge(mixed_ready, s + 1)
                        reach(dve, result_turned, s)
                        dve.tensor_tensor(result[:], mixed[:], xres[:, cols], ALU.add).then_inc(result_ready, 1)
                run_steps(dve, step, B, 1, 2)


def silence_table():
    off = 1 - np.eye(EXPERTS, dtype=np.float32)
    return np.ascontiguousarray(np.repeat((off * np.float32(-1e30))[:, :, None], D, 2).astype(mybir.dt.np(BF16)))


def rank_table():
    return np.ascontiguousarray(np.tile(np.arange(EXPERTS, 0, -1, dtype=np.float32), (D, 1)))


def build(nc, dram):
    with ExitStack() as ctx:
        def sb(name, shape, dt=F32):
            return ctx.enter_context(nc.sbuf_tensor(name, shape, dt))

        ident, centre, average = sb("ident", [D, D]), sb("centre", [D, D]), sb("average", [D, D])
        ident_bf = sb("ident_bf", [D, D], BF16)
        hid = sb("hid", [D, B * N])
        s_res = sb("s_res", [D, B * N])
        consts_in = ctx.enter_context(nc.semaphore("consts_in"))
        with nc.Block() as block:

            @block.sync
            def _(sp):
                for dst, name in ((ident, "ident"), (centre, "centre"), (average, "average"), (ident_bf, "ident_bf")):
                    sp.dma_start(dst[:], dram[name]).then_inc(consts_in, 16)
                sp.wait_ge(consts_in, 64)

        phase_mixer(nc, dram["x"], dram["A_w"], dram["A_vecs"], ident, hid, s_res)
        with ExitStack() as own:
            attend = local_attention(nc, own, sub(dram, "B_"), ident, ident_bf, hid)
            feed = feed_forward(nc, own, sub(dram, "B_"), centre, average, hid)
            with nc.Fori(0, DEPTH) as layer:
                attend(layer)
                feed(layer)
        phase_gate(nc, hid, s_res)
        xn_res = sb("xn_res", [D, B * N])
        phase_sparse_attention(nc, {**sub(dram, "C_"), "x": dram["x"]}, ident, ident_bf, centre, average, hid, s_res, xn_res)
        phase_experts(nc, {**sub(dram, "D_"), "out": dram["out"]}, ident, ident_bf, hid, s_res, xn_res)


def sub(dram, prefix):
    return {k[len(prefix):]: v for k, v in dram.items() if k.startswith(prefix)}


def kernel(**inputs):
    import concourse.bacc as _bacc
    from concourse.bass_utils import run_bass_kernel_spmd as _run

    a = {k: np.asarray(v) for k, v in inputs.items()}
    data = {"x": a["L0_attn_hidden_states"]}
    data["A_w"] = np.stack([a["L0_attn_" + k].T for k in ("Wk", "Wka", "Wv")], 1)
    data["A_vecs"] = np.stack([a["L0_attn_" + k] for k in ("gamma", "beta", "bk", "bka", "bv")], 1)
    for k in ("wqkv", "wo", "q_scale", "k_scale", "w1", "w2", "b1", "b2", "ln_g", "ln_b"):
        data["B_" + k] = a["L0_ffn_" + k]
    for k in ("Wq", "Wk", "Wv", "Wo"):
        data["C_" + k] = a["L1_attn_" + k].T
    for k in ("bq", "bk", "bv", "bo"):
        data["C_" + k] = a["L1_attn_" + k][:, None]
    data["D_gate_w"] = a["L1_ffn_gate_w"].T
    data["D_gate_b"], data["D_expert_bias"] = a["L1_ffn_gate_b"][None], a["L1_ffn_expert_bias"][None]
    data["D_b1"] = a["L1_ffn_b1"].reshape(EXPERTS, FC, D).transpose(2, 0, 1)
    for k in ("b2", "w1", "w2"):
        data["D_" + k] = a["L1_ffn_" + k]
    mean = np.full((D, D), 1.0 / D, np.float32)
    data["ident"], data["average"], data["centre"] = np.eye(D, dtype=np.float32), mean, np.eye(D, dtype=np.float32) - mean
    data["ident_bf"] = np.eye(D).astype(mybir.dt.np(BF16))
    data["B_rope_base"], data["B_window_mask"] = rope_base_table(), window_mask_table()
    data["C_counts"], data["C_pair_mask"] = pair_tables()
    data["C_rope1"] = rope1_table()
    data["C_same_head"] = np.kron(np.eye(H1), np.ones((DH1, DH1))).astype(np.float32)
    data["D_rank"], data["D_silence"] = rank_table(), silence_table()

    nc = _bacc.Bacc("TRN2", target_bir_lowering=False, num_devices=1)
    arrays, dram = {}, {}
    for name, value in data.items():
        arrays[f"in_{name}"] = np.ascontiguousarray(value)
        dram[name] = nc.dram_tensor(f"in_{name}", value.shape, mybir.dt.from_np(value.dtype), kind="ExternalInput").ap()
    dram["C_ring"] = nc.dram_tensor("ring", (2, D, 3, RING), F32).ap()
    dram["C_back"] = nc.dram_tensor("back", (2, D, 2 * N), F32).ap()
    dram["out"] = nc.dram_tensor("out", (B, N, D), F32, kind="ExternalOutput").ap()
    build(nc, dram)
    return _run(nc, [arrays], core_ids=[0]).results[0]["out"]
```

```python
from contextlib import ExitStack

import numpy as np
import concourse.bass as bass
from concourse import mybir

DEPTH = 2
F32 = mybir.dt.float32
BF16 = mybir.dt.bfloat16
ALU = mybir.AluOpType
ACT = mybir.ActivationFunctionType
AX_X = mybir.AxisListType.X

D = 128
B, N = 16, 512
TT = N // D
CLEARING = 104
EPS = 1e-5
EXP_LN = "natural_log_exp_and_others"


def reach(eng, sem, count):
    if isinstance(count, (int, np.integer)) and count <= 0:
        return
    eng.wait_ge(sem, count)


def columns(i, width=N):
    return bass.ds(i * width, width)


def run_steps(eng, step, steps, lead, unroll):
    for s in range(-lead, unroll):
        step(s, s % unroll, s // unroll)
    with eng.Fori(1, steps // unroll - 1) as r:
        for u in range(unroll):
            step(r * unroll + u, u, r)
    for u in range(unroll):
        step(steps - unroll + u, u, steps // unroll - 1)


def known(s):
    return isinstance(s, (int, np.integer))


def phase_mixer(nc, x_dram, weights, vectors, ident, hid, s_res, sorted_dram):
    with ExitStack() as ctx:
        def sb(name, shape, dt=F32):
            return ctx.enter_context(nc.sbuf_tensor("a_" + name, shape, dt))

        def ps(name):
            return ctx.enter_context(nc.psum_tensor("a_" + name, [D, N], F32))

        sems = []

        def sem(name):
            sems.append(ctx.enter_context(nc.semaphore("a_" + name)))
            return sems[-1]

        x_in = [sb(f"x_in{p}", [D, TT, D]) for p in range(2)]
        xn = [sb(f"xn{p}", [D, TT, D]) for p in range(2)]
        hn = [sb(f"hn{p}", [D, TT, D]) for p in range(2)]
        stats = [sb(f"stats{k}", [D, TT, 6]) for k in range(2)]
        mean_var = [sb(f"mean_var{k}", [D, TT, 2]) for k in range(2)]
        var_eps = [sb(f"var_eps{k}", [D, TT]) for k in range(2)]
        ln_var = [sb(f"ln_var{k}", [D, TT]) for k in range(2)]
        rstd = [sb(f"rstd{k}", [D, TT]) for k in range(2)]
        h_t = [sb(f"h_t{p}", [D, N]) for p in range(2)]
        w_t = sb("w_t", [D, 3, D])
        vecs = sb("vecs", [D, 6])
        bka_scaled = sb("bka_scaled", [D, 1])
        ones = sb("ones", [D, N])
        cleared_rows = sorted_dram.shape[0] // B
        zeros = sb("zeros", [CLEARING, cleared_rows // CLEARING * D])
        carrier = sb("carrier", [D, 4])
        keys = sb("keys", [D, N])
        kw = sb("kw", [D, N])
        kw_sum = sb("kw_sum", [D, N])
        kw_inv = sb("kw_inv", [D, N])
        share = sb("share", [D, N])
        weighted = sb("weighted", [D, N])
        pooled = sb("pooled", [D, N])
        xn_ps, hn_ps, k_ps, v_ps, ka_ps = (ps(n) for n in ("xn_ps", "hn_ps", "k_ps", "v_ps", "ka_ps"))

        consts_in = sem("consts_in")
        consts_made = sem("consts_made")
        zeros_made = sem("zeros_made")
        rows_cleared = sem("rows_cleared")
        x_loaded = [sem(f"x_loaded{p}") for p in range(2)]
        bn_done = sem("bn_done")
        aggr_done = sem("aggr_done")
        var_ready = sem("var_ready")
        ln_ready = sem("ln_ready")
        rstd_ready = sem("rstd_ready")
        xn_ready = sem("xn_ready")
        hn_ready = sem("hn_ready")
        xn_turned = sem("xn_turned")
        hn_turned = sem("hn_turned")
        hid_ready = sem("hid_ready")
        h_ready = sem("h_ready")
        k_done = sem("k_done")
        v_done = sem("v_done")
        keys_ready = sem("keys_ready")
        ka_done = sem("ka_done")
        kw_ready = sem("kw_ready")
        sum_ready = sem("sum_ready")
        inv_ready = sem("inv_ready")
        share_ready = sem("share_ready")
        weighted_ready = sem("weighted_ready")
        pooled_ready = sem("pooled_ready")
        s_ready = sem("s_ready")

        scale = 1.0 / np.sqrt(np.float32(D))
        GAMMA, BETA, BK, BKA, BV = range(5)

        with nc.Block() as block:

            @block.sync
            def _(sp):
                sp.dma_start(w_t[:], weights).then_inc(consts_in, 16)
                sp.dma_start(vecs[:, 0:5], vectors).then_inc(consts_in, 16)

                def clear(s):
                    if known(s) and s < 0:
                        return
                    rows = (sorted_dram[s * cleared_rows:(s + 1) * cleared_rows].rearrange("(p k) d -> p (k d)", p=CLEARING)
                            if known(s) else
                            sorted_dram.rearrange("(s p k) d -> s p (k d)", s=B, p=CLEARING)[bass.ds(s, 1)]
                            .rearrange("o p n -> (o p) n"))
                    sp.dma_start(rows, zeros[:]).then_inc(rows_cleared, 16)

                def step(s, u, r):
                    if known(s) and s == 0:
                        sp.wait_ge(zeros_made, 1)
                    load(s, u)
                    clear(s)

                def load(s, u):
                    if known(s) and s + 1 >= B:
                        return
                    reach(sp, xn_ready, (s + 1 - 1) * TT)
                    sp.dma_start(x_in[(u + 1) % 2][:], x_dram[s + 1 if known(s) else bass.ds(s + 1, 1)]
                                 .rearrange("(t p) d -> p t d" if known(s) else "o (t p) d -> p (o t) d", p=D)
                                 ).then_inc(x_loaded[(u + 1) % 2], 16)
                run_steps(sp, step, B, 1, 2)
                sp.wait_ge(rows_cleared, 16 * B)

            @block.gpsimd
            def _(pool):
                pool.memset(ones[:], 1.0).then_inc(consts_made, 1)
                pool.memset(zeros[:], 0.0).then_inc(zeros_made, 1)

                def step(s, u, r):
                    if known(s) and s < 0:
                        return
                    pool.wait_ge(share_ready, s + 1)
                    pool.wait_ge(keys_ready, s + 1)
                    reach(pool, pooled_ready, s)
                    pool.tensor_tensor(weighted[:], share[:], keys[:], ALU.mult).then_inc(weighted_ready, 1)
                run_steps(pool, step, B, 1, 2)

            @block.scalar
            def _(act):
                act.preload_act_table_set(EXP_LN)
                act.wait_ge(consts_in, 32)
                act.mul(bka_scaled[:], vecs[:, BKA:BKA + 1], float(scale)).then_inc(consts_made, 1)
                act.wait_ge(consts_made, 2)

                def rstd_of(k, n):
                    act.wait_ge(var_ready, n)
                    act.activation(ln_var[k][:], var_eps[k][:], ACT.Ln).then_inc(ln_ready, 1)
                    act.wait_ge(ln_ready, n)
                    act.activation(rstd[k][:], ln_var[k][:], ACT.Exp, scale=-0.5).then_inc(rstd_ready, 1)

                def step(s, u, r):
                    main = not (known(s) and s < 0)
                    ahead = not (known(s) and s + 1 >= B)
                    if main:
                        act.wait_ge(k_done, s + 1)
                        reach(act, weighted_ready, s)
                        act.activation(keys[:], k_ps[:], ACT.Identity,
                                       bias=vecs[:, BK:BK + 1]).then_inc(keys_ready, 1)
                    if ahead:
                        rstd_of(0, 2 * s + 3)
                    if main:
                        act.wait_ge(ka_done, s + 1)
                        reach(act, share_ready, s)
                        act.activation(kw[:], ka_ps[:], ACT.Exp, scale=float(scale),
                                       bias=bka_scaled[:]).then_inc(kw_ready, 1)
                    if ahead:
                        act.wait_ge(xn_turned, s + 2)
                        act.activation(hid[:, columns(s + 1)], xn_ps[:], ACT.Copy).then_inc(hid_ready, 1)
                        rstd_of(1, 2 * s + 4)
                        act.wait_ge(hn_turned, s + 2)
                        reach(act, v_done, s)
                        act.activation(h_t[(u + 1) % 2][:], hn_ps[:], ACT.Identity,
                                       scale=vecs[:, GAMMA:GAMMA + 1],
                                       bias=vecs[:, BETA:BETA + 1]).then_inc(h_ready, 1)
                run_steps(act, step, B, 1, 2)

            @block.tensor
            def _(pe):
                pe.wait_ge(consts_in, 32)

                def turn(out, src, done):
                    for t in range(TT):
                        ins = pe.transpose(out[:, t * D:(t + 1) * D], src[:, t, :], ident[:])
                    ins.then_inc(done, 1)

                def step(s, u, r):
                    main = not (known(s) and s < 0)
                    ahead = not (known(s) and s + 1 >= B)
                    if main:
                        pe.wait_ge(h_ready, s + 1)
                        reach(pe, keys_ready, s)
                        pe.matmul(k_ps[:], w_t[:, 0, :], h_t[u % 2][:], start=True, stop=True).then_inc(k_done, 1)
                        reach(pe, s_ready, s)
                        pe.matmul(v_ps[:], w_t[:, 2, :], h_t[u % 2][:], start=True, stop=True).then_inc(v_done, 1)
                    if ahead:
                        pe.wait_ge(xn_ready, TT * (s + 2))
                        reach(pe, hid_ready, s + 1)
                        turn(xn_ps, xn[(u + 1) % 2], xn_turned)
                    if main:
                        pe.wait_ge(keys_ready, s + 1)
                        reach(pe, kw_ready, s)
                        pe.matmul(ka_ps[:], w_t[:, 1, :], keys[:], start=True, stop=True).then_inc(ka_done, 1)
                    if ahead:
                        pe.wait_ge(hn_ready, TT * (s + 2))
                        reach(pe, h_ready, s + 1)
                        turn(hn_ps, hn[(u + 1) % 2], hn_turned)
                run_steps(pe, step, B, 1, 2)

            @block.vector
            def _(dve):
                dve.wait_ge(consts_made, 2)

                def variance(k, src, n):
                    for t in range(TT):
                        dve.bn_stats(stats[k][:, t, :], src[:, t, :]).then_inc(bn_done, 1)
                    dve.wait_ge(bn_done, TT * n)
                    reach(dve, xn_ready if k == 0 else hn_ready, TT * ((n - 1) // 2) if known(n) else TT * (n - 1 - k) // 2)
                    dve.memset(carrier[:, 2 * k:2 * k + 1], 0.0)
                    for t in range(TT):
                        dve.bn_aggr(mean_var[k][:, t, :], stats[k][:, t, :]).then_inc(aggr_done, 1)
                    dve.wait_ge(aggr_done, TT * n)
                    dve.tensor_scalar(var_eps[k][:], mean_var[k][:, :, 1], EPS, None, ALU.add).then_inc(var_ready, 1)

                def normalise(k, dst, src, n, ready):
                    dve.wait_ge(rstd_ready, n)
                    for t in range(TT):
                        dve.tensor_scalar(dst[:, t, :], src[:, t, :], mean_var[k][:, t, 0:1], rstd[k][:, t:t + 1],
                                          ALU.subtract, ALU.mult).then_inc(ready, 1)

                def step(s, u, r):
                    main = not (known(s) and s < 0)
                    ahead = not (known(s) and s + 1 >= B)
                    q = (u + 1) % 2
                    if ahead:
                        dve.wait_ge(x_loaded[q], 16 * (r + (u + 1) // 2 + 1))
                        variance(0, x_in[q], 2 * s + 3)
                        reach(dve, xn_turned, s)
                        normalise(0, xn[q], x_in[q], 2 * s + 3, xn_ready)
                        dve.wait_ge(xn_ready, TT * (s + 2))
                        variance(1, xn[q], 2 * s + 4)
                    if main:
                        dve.wait_ge(kw_ready, s + 1)
                        dve.tensor_tensor_scan(kw_sum[:], ones[:], kw[:], 0.0, ALU.mult, ALU.add).then_inc(sum_ready, 1)
                        dve.wait_ge(sum_ready, s + 1)
                        dve.reciprocal(kw_inv[:], kw_sum[:]).then_inc(inv_ready, 1)
                        dve.wait_ge(inv_ready, s + 1)
                        reach(dve, weighted_ready, s)
                        dve.tensor_tensor(share[:], kw[:], kw_inv[:], ALU.mult).then_inc(share_ready, 1)
                    if ahead:
                        reach(dve, hn_turned, s)
                        normalise(1, hn[q], xn[q], 2 * s + 4, hn_ready)
                    if main:
                        dve.wait_ge(weighted_ready, s + 1)
                        dve.tensor_tensor_scan(pooled[:], ones[:], weighted[:], 0.0, ALU.mult, ALU.add).then_inc(pooled_ready, 1)
                        dve.wait_ge(pooled_ready, s + 1)
                        dve.wait_ge(v_done, s + 1)
                        dve.scalar_tensor_tensor(out=s_res[:, columns(s)], in0=v_ps[:], scalar=vecs[:, BV:BV + 1],
                                                 in1=pooled[:], op0=ALU.add, op1=ALU.mult).then_inc(s_ready, 1)
                run_steps(dve, step, B, 1, 2)

        with nc.Block() as block:

            @block.gpsimd
            def _(pool):
                for used in sems:
                    pool.sem_clear(used)


HEADS, DH = 8, 64
WIN = 64
INNER = HEADS * DH
NT = B * TT
PAIR = HEADS // 2


def run_tiles(eng, step, lead, lag):
    for s in range(-lead, TT):
        step(s, s % TT)
    with eng.Fori(1, B - 1) as seq:
        for u in range(TT):
            step(seq * TT + u, u)
    for s in range(NT - TT, NT + lag):
        step(s, s % TT)


def inside(t):
    return not known(t) or 0 <= t < NT


def local_attention(nc, own, dram, ident, ident_bf, hid):
    def sb(name, shape, dt=F32):
        return own.enter_context(nc.sbuf_tensor("b_" + name, shape, dt))

    def sem(name):
        return own.enter_context(nc.semaphore("b_" + name))

    wqkv = sb("wqkv", [D, 3 * INNER])
    wo = sb("wo", [D, INNER // D, D])
    scales = sb("scales", [D, 4, DH])
    rope_base = sb("rope_base", [D, 4, TT, DH])
    rope = sb("rope", [D, 4, TT, DH])
    mask = sb("mask", [D, 2, PAIR, D], BF16)
    shift = [sb(f"shift{u}", [D, D]) for u in range(TT)]
    squares = [sb(f"squares{k}", [D, HEADS, DH]) for k in range(2)]
    norm2 = sb("norm2", [D, 2, HEADS])
    norm2_clip = sb("norm2_clip", [D, 2, HEADS])
    norm_ln = sb("norm_ln", [D, 2, HEADS])
    norm_inv = sb("norm_inv", [D, 2, HEADS])
    half_log = sb("half_log", [D, 1])
    by_cos = [sb(f"by_cos{k}", [D, HEADS, DH]) for k in range(2)]
    by_sin = [sb(f"by_sin{k}", [D, HEADS, DH]) for k in range(2)]
    rope_sum = [sb(f"rope_sum{k}", [D, HEADS, DH]) for k in range(2)]
    roped = [sb(f"roped{k}", [D, INNER]) for k in range(2)]
    q_t = sb("q_t", [D, PAIR, D])
    k_t = [sb(f"k_t{u}", [D, PAIR, D]) for u in range(TT)]
    v_odd = [sb(f"v_odd{u}", [D, HEADS, DH + 1]) for u in range(TT)]
    v_even = [sb(f"v_even{u}", [D, HEADS, DH + 1]) for u in range(TT)]
    neg_max = sb("neg_max", [D, 2, PAIR])
    logits = [sb(f"logits{p}", [D, PAIR, D]) for p in range(2)]
    probs = [sb(f"probs{p}", [D, PAIR, D]) for p in range(2)]
    sum_inv = sb("sum_inv", [D, 2, PAIR])
    heads_out = sb("heads_out", [D, HEADS, DH])
    o_t = sb("o_t", [D, INNER // D, D])

    weights_in = sem("weights_in")
    fixed_in = sem("fixed_in")
    tables_ready = sem("tables_ready")
    shifted = sem("shifted")
    proj_done = [sem(f"{x}_done") for x in "qkv"]
    squared = [sem(f"{x}_squared") for x in "qk"]
    products = sem("rope_products")
    sums = sem("rope_sums")
    norms_summed = sem("norms_summed")
    norms_clipped = sem("norms_clipped")
    norms_ln = sem("norms_ln")
    norms_ready = sem("norms_ready")
    roped_ready = sem("roped_ready")
    turned = [sem(f"{x}_turned") for x in "qko"]
    turned_out = [sem(f"{x}_t_ready") for x in "qko"]
    v_ready = sem("v_ready")
    scores_done = sem("scores_done")
    max_ready = sem("max_ready")
    logits_ready = sem("logits_ready")
    logits_turned = sem("logits_turned")
    probs_ready = sem("probs_ready")
    weighed = sem("weighed")
    sum_inv_ready = sem("sum_inv_ready")
    heads_ready = sem("heads_ready")
    y_done = sem("y_done")
    x_updated = sem("x_updated")

    LIFT = 2.0 ** 30

    with nc.Block() as block:

        @block.sync
        def _(sp):
            sp.dma_start(rope_base[:], dram["rope_base"]).then_inc(fixed_in, 16)
            sp.dma_start(mask[:], dram["window_mask"]).then_inc(fixed_in, 16)
            sp.wait_ge(fixed_in, 32)

        @block.vector
        def _(dve):
            for u in range(TT):
                for v in (v_odd, v_even):
                    dve.memset(v[u][:, :, DH:DH + 1], 1.0)
            dve.memset(half_log[:], float(0.5 * np.log(LIFT)))
            dve.memset(shift[0][DH:D, 0:1], 0.0)

    def phase(layer):
        def wait(eng, semaphore, tiles, per=1, more=0):
            if known(tiles) and tiles * per + more <= 0:
                return
            eng.wait_ge(semaphore, layer * (NT * per) + tiles * per + more)

        with ExitStack() as ctx:
            def ps(name, shape):
                return ctx.enter_context(nc.psum_tensor("b_" + name, shape, F32))

            qk_ps = [ps("q_ps", [D, HEADS, DH]), ps("k_ps", [D, HEADS, DH])]
            v_ps = ps("v_ps", [D, HEADS, DH])
            turn_ps = ps("turn_ps", [D, PAIR, D])
            score_ps = [ps(f"score_ps{p}", [D, PAIR, D]) for p in range(2)]
            probs_ps = ps("probs_ps", [D, PAIR, D])
            out_ps = ps("out_ps", [D, 512])
            weighed_ps = out_ps[:, 0:PAIR * (DH + 1)].rearrange("p (h d) -> p h d", h=PAIR)
            y_ps = out_ps[:, 512 - D:512]

            with nc.Block() as block:

                @block.sync
                def _(sp):
                    one = bass.ds(layer, 1)
                    sp.dma_start(wqkv[:], dram["wqkv"][one].rearrange("l p n -> p (l n)")).then_inc(weights_in, 16)
                    sp.dma_start(wo[:], dram["wo"][one].rearrange("l (c p) n -> p (l c) n", p=D)).then_inc(weights_in, 16)
                    for k, name in enumerate(("q_scale", "k_scale")):
                        row = dram[name][one]
                        sp.dma_start(scales[:, 2 * k, :], row.to_broadcast([D, DH])).then_inc(weights_in, 16)
                        for a, b in ((0, DH // 2), (DH // 2, 0)):
                            sp.dma_start(scales[:, 2 * k + 1, a:a + DH // 2],
                                         row[:, b:b + DH // 2].to_broadcast([D, DH // 2])).then_inc(weights_in, 16)

                @block.gpsimd
                def _(pool):
                    def step(s, u):
                        w = (u + 3) % TT
                        if inside(s + 2):
                            for k in range(2):
                                wait(pool, products, s + 2, 6, 3 * k + 3)
                                wait(pool, roped_ready, s + 1, 2, k + 1)
                                pool.tensor_tensor(rope_sum[k][:], by_cos[k][:], by_sin[k][:], ALU.add).then_inc(sums, 1)
                    run_tiles(pool, step, 2, 0)

                @block.scalar
                def _(act):
                    act.preload_act_table_set(EXP_LN)

                    def turn_out(i, dst, t):
                        wait(act, turned[i], t + 1)
                        act.activation(dst[:], turn_ps[:], ACT.Copy).then_inc(turned_out[i], 1)

                    def square(k, t):
                        wait(act, proj_done[k], t + 1)
                        wait(act, norms_summed, t, 2)
                        act.activation(squares[k][:], qk_ps[k][:], ACT.Square).then_inc(squared[k], 1)

                    def exponentials(p, t):
                        wait(act, logits_turned, t, 2, p + 1)
                        wait(act, weighed, t - 1, 2, p + 1)
                        act.activation(probs[p][:], probs_ps[:], ACT.Exp).then_inc(probs_ready, 1)

                    def shift_tokens(t, w):
                        wait(act, proj_done[2], t - 3)
                        act.activation(shift[w][0:DH, :], hid[0:DH, columns(t, D)], ACT.Copy).then_inc(shifted, 1)
                        a = 1 if w == 0 else 0
                        act.activation(shift[w][DH:D, a:D], hid[DH:D, bass.ds(t * D - 1 + a, D - a)],
                                       ACT.Copy).then_inc(shifted, 1)

                    def step(s, u):
                        if inside(s - 1):
                            wait(act, y_done, s - 1)
                            turn_out(2, o_t, s - 1)
                        if inside(s):
                            exponentials(0, s)
                        if inside(s + 3):
                            shift_tokens(s + 3, (u + 3) % TT)
                        if inside(s + 1):
                            wait(act, scores_done, s + 1, 2)
                            turn_out(0, q_t, s + 1)
                            turn_out(1, k_t[(u + 1) % TT], s + 1)
                        if inside(s):
                            exponentials(1, s)
                        if inside(s + 2):
                            wait(act, norms_clipped, s + 3)
                            act.activation(norm_ln[:], norm2_clip[:], ACT.Ln, scale=LIFT).then_inc(norms_ln, 1)
                            wait(act, norms_ln, s + 3)
                            wait(act, roped_ready, s + 2, 2)
                            act.activation(norm_inv[:], norm_ln[:], ACT.Exp, scale=-0.5, bias=half_log[:]).then_inc(norms_ready, 1)
                        if inside(s + 3):
                            square(0, s + 3)
                            square(1, s + 3)
                        if inside(s + 2):
                            w = (u + 2) % TT
                            wait(act, proj_done[2], s + 3)
                            wait(act, weighed, s, 2)
                            act.activation(v_odd[w][:, :, 0:DH], v_ps[:], ACT.Copy).then_inc(v_ready, 1)
                            act.activation(v_even[w][0:WIN, :, 0:DH], v_ps[0:WIN], ACT.Copy).then_inc(v_ready, 1)
                            act.activation(v_even[(w + 1) % TT][WIN:D, :, 0:DH], v_ps[WIN:D], ACT.Copy).then_inc(v_ready, 1)
                    run_tiles(act, step, 3, 1)

                @block.tensor
                def _(pe):
                    pe.wait_ge(weights_in, (layer + 1) * 128)

                    def project(i, t, w, out):
                        wait(pe, shifted, t + 1, 2)
                        pe.matmul(out, shift[w][:], wqkv[:, i * INNER:(i + 1) * INNER],
                                  start=True, stop=True).then_inc(proj_done[i], 1)

                    def turn(i, src, t):
                        for c in range(PAIR):
                            ins = pe.transpose(turn_ps[:, c, :], src[:, c * D:(c + 1) * D], ident[:])
                        ins.then_inc(turned[i], 1)

                    def turn_logits(p, t):
                        wait(pe, logits_ready, t, 2, p + 1)
                        wait(pe, probs_ready, t, 2, p)
                        for h in range(PAIR):
                            ins = pe.transpose(probs_ps[:, h, :], logits[p][:, h, :], ident[:])
                        ins.then_inc(logits_turned, 1)

                    def scores(t, w):
                        wait(pe, turned_out[0], t + 1)
                        wait(pe, turned_out[1], t + 1)
                        for p in range(2):
                            wait(pe, logits_ready, t - 1, 2, p + 1)
                            pe.matmul(score_ps[p][:], ident_bf[:], mask[:, 0 if w == 0 else 1],
                                      start=True, stop=False, skip_group_check=True)
                        for h in range(PAIR):
                            for p in range(2):
                                rows = slice(p * DH, (p + 1) * DH)
                                pe.matmul(score_ps[p][0:WIN, h, 0:WIN], q_t[rows, h, 0:WIN], k_t[w][rows, h, 0:WIN],
                                          start=False, stop=True, skip_group_check=True)
                                if w > 0:
                                    pe.matmul(score_ps[p][0:WIN, h, WIN:D], q_t[rows, h, 0:WIN],
                                              k_t[w - 1][rows, h, WIN:D], start=False, stop=True, skip_group_check=True)
                                ins = pe.matmul(score_ps[p][WIN:D, h, :], q_t[rows, h, WIN:D], k_t[w][rows, h, :],
                                                start=False, stop=True, skip_group_check=True)
                                if h == PAIR - 1:
                                    ins.then_inc(scores_done, 1)

                    def weigh(p, t, w):
                        wait(pe, probs_ready, t, 2, p + 1)
                        wait(pe, v_ready, t + 1, 3)
                        if p == 0:
                            wait(pe, x_updated, t)
                        wait(pe, heads_ready, t, 2, p)
                        keys = D if w > 0 else WIN
                        for h in range(PAIR):
                            pe.matmul(weighed_ps[WIN:D, h, :], probs[p][:, h, WIN:D], v_odd[w][:, 2 * h + p, :],
                                      start=True, stop=True, skip_group_check=True)
                            ins = pe.matmul(weighed_ps[0:WIN, h, :], probs[p][0:keys, h, 0:WIN],
                                            v_even[w][0:keys, 2 * h + p, :], start=True, stop=True, skip_group_check=True)
                        ins.then_inc(weighed, 1)

                    def step(s, u):
                        w1, w2, w3 = (u + 1) % TT, (u + 2) % TT, (u + 3) % TT
                        if inside(s - 1):
                            wait(pe, heads_ready, s, 2)
                            wait(pe, turned_out[1], s + 1 if inside(s) else s)
                            turn(2, heads_out[:].rearrange("p h d -> p (h d)"), s - 1)
                        if inside(s):
                            turn_logits(0, s)
                        if inside(s + 1):
                            wait(pe, roped_ready, s + 1, 2, 1)
                            wait(pe, turned_out[2], s)
                            turn(0, roped[0], s + 1)
                        if inside(s - 1):
                            wait(pe, turned_out[2], s)
                            wait(pe, heads_ready, s, 2)
                            for c in range(INNER // D):
                                ins = pe.matmul(y_ps, wo[:, c, :], o_t[:, c, :], start=(c == 0), stop=(c == INNER // D - 1))
                            ins.then_inc(y_done, 1)
                        if inside(s + 1):
                            wait(pe, roped_ready, s + 2, 2)
                            wait(pe, turned_out[0], s + 2)
                            turn(1, roped[1], s + 1)
                        if inside(s):
                            turn_logits(1, s)
                            weigh(0, s, u)
                        if inside(s + 1):
                            scores(s + 1, w1)
                        if inside(s):
                            weigh(1, s, u)
                        if inside(s + 3):
                            wait(pe, products, s + 2, 6, 3)
                            project(0, s + 3, w3, qk_ps[0][:])
                            wait(pe, products, s + 3, 6)
                            project(1, s + 3, w3, qk_ps[1][:])
                        if inside(s + 2):
                            wait(pe, v_ready, s + 2, 3)
                            project(2, s + 2, w2, v_ps[:])
                    run_tiles(pe, step, 3, 1)

                @block.vector
                def _(dve):
                    dve.wait_ge(weights_in, (layer + 1) * 128)
                    for k in range(4):
                        dve.tensor_tensor(rope[:, k], rope_base[:, k],
                                          scales[:, k:k + 1, :].to_broadcast([D, TT, DH]), ALU.mult).then_inc(tables_ready, 1)
                    dve.wait_ge(tables_ready, layer * 4 + 4)

                    half = DH // 2

                    def rotate(k, t, w):
                        wait(dve, squared[k], t + 1)
                        wait(dve, sums, t - 1, 2, k + 1)
                        cos = rope[:, 2 * k, w:w + 1, :]
                        sin = rope[:, 2 * k + 1, w:w + 1, :]
                        dve.tensor_tensor(by_cos[k][:], qk_ps[k][:], cos.to_broadcast([D, HEADS, DH]),
                                          ALU.mult).then_inc(products, 1)
                        for a, b in ((0, half), (half, 0)):
                            dve.tensor_tensor(by_sin[k][:, :, a:a + half], qk_ps[k][:, :, b:b + half],
                                              sin[:, :, a:a + half].to_broadcast([D, HEADS, half]),
                                              ALU.mult).then_inc(products, 1)
                        wait(dve, norms_clipped, t)
                        dve.tensor_reduce(norm2[:, k, :], squares[k][:], AX_X, ALU.add).then_inc(norms_summed, 1)

                    def subtract_max(p, t):
                        wait(dve, scores_done, t, 2, p + 1)
                        dve.tensor_reduce(neg_max[:, p, :], score_ps[p][:], AX_X, ALU.max, negate=True).then_inc(max_ready, 1)
                        wait(dve, max_ready, t, 2, p + 1)
                        wait(dve, logits_turned, t - 1, 2, p + 1)
                        dve.tensor_tensor(logits[p][:], score_ps[p][:],
                                          neg_max[:, p, :].unsqueeze(2).to_broadcast([D, PAIR, D]),
                                          ALU.add).then_inc(logits_ready, 1)

                    def normalise(p, t):
                        wait(dve, weighed, t, 2, p + 1)
                        dve.reciprocal(sum_inv[:, p, :], weighed_ps[:, :, DH]).then_inc(sum_inv_ready, 1)
                        wait(dve, sum_inv_ready, t, 2, p + 1)
                        wait(dve, turned[2], t)
                        dve.tensor_tensor(heads_out[:, p::2, :], weighed_ps[:, :, 0:DH],
                                          sum_inv[:, p, :].unsqueeze(2).to_broadcast([D, PAIR, DH]),
                                          ALU.mult).then_inc(heads_ready, 1)

                    def step(s, u):
                        w1, w2 = (u + 1) % TT, (u + 2) % TT
                        if inside(s + 2):
                            rotate(0, s + 2, w2)
                        if inside(s - 1):
                            wait(dve, y_done, s)
                            wait(dve, shifted, s + 1 if inside(s) else s, 2)
                            x = hid[:, columns(s - 1, D)]
                            dve.tensor_tensor(x, y_ps, x, ALU.add).then_inc(x_updated, 1)
                        if inside(s + 2):
                            rotate(1, s + 2, w2)
                            wait(dve, norms_summed, s + 3, 2)
                            wait(dve, norms_ln, s + 2)
                            dve.tensor_scalar(norm2_clip[:], norm2[:], 1e-24, None, ALU.max).then_inc(norms_clipped, 1)
                        if inside(s):
                            normalise(0, s)
                        if inside(s + 1):
                            subtract_max(0, s + 1)
                            subtract_max(1, s + 1)
                        if inside(s):
                            normalise(1, s)
                        if inside(s + 2):
                            wait(dve, norms_ready, s + 3)
                            for k in range(2):
                                wait(dve, sums, s + 2, 2, k + 1)
                                wait(dve, turned[k], s + 2)
                                dve.tensor_tensor(roped[k][:].rearrange("p (h d) -> p h d", h=HEADS), rope_sum[k][:],
                                                  norm_inv[:, k, :].unsqueeze(2).to_broadcast([D, HEADS, DH]),
                                                  ALU.mult).then_inc(roped_ready, 1)
                    run_tiles(dve, step, 3, 1)
    return phase


def rope_base_table():
    f = np.float32
    half = np.arange(0, DH, 2, dtype=f)
    inv_freq = (f(1.0) / f(10000.0) ** (half / f(DH))).astype(f)
    t = np.arange(N, dtype=f)
    freqs = t[:, None] * inv_freq[None, :]
    freqs = np.concatenate([freqs, freqs], -1)
    base = (half + f(0.4 * DH)) / f(1.4 * DH)
    power = (t - f(N // 2)) / f(WIN // 2)
    scale = (base[None, :] ** power[:, None]).astype(f)
    scale = np.concatenate([scale, scale], -1)
    sign = np.where(np.arange(DH) < DH // 2, f(-1), f(1))
    cos, sin = np.cos(freqs), np.sin(freqs) * sign
    kinds = np.stack([cos * scale * f(8), sin * scale * f(8), cos / scale, sin / scale], 0)
    return np.ascontiguousarray(kinds.reshape(4, TT, D, DH).transpose(2, 0, 1, 3).astype(f))


def window_mask_table():
    i, j = np.arange(WIN)[:, None], np.arange(WIN)[None, :]
    own, prev = j <= i, j >= i
    never = np.zeros_like(own)
    out = np.stack([np.block([[own, never], [prev, own]]), np.block([[own, prev], [prev, own]])], 0)
    out = np.where(out, 0.0, -1e30).astype(mybir.dt.np(BF16))
    return np.ascontiguousarray(np.repeat(out.transpose(1, 0, 2)[:, :, None, :], PAIR, 2))


HID = 341
CHUNKS = [(a, min(D, HID - a)) for a in range(0, HID, D)]


def feed_forward(nc, own, dram, centre, average, hid):
    def sb(name, shape, dt=F32):
        return own.enter_context(nc.sbuf_tensor("f_" + name, shape, dt))

    def sem(name):
        return own.enter_context(nc.semaphore("f_" + name))

    nch = len(CHUNKS)
    w1 = sb("w1", [D, 2 * HID])
    w2 = sb("w2", [D, nch, D])
    b1 = sb("b1", [D, 2, nch])
    vecs = sb("vecs", [D, 3])
    eps = sb("eps", [D, 1])
    LG, LB, B2 = range(3)
    shift = [sb(f"shift{p}", [D, N]) for p in range(2)]
    squares = sb("squares", [D, N])
    ln_var = sb("ln_var", [D, N])
    rstd = sb("rstd", [D, N])
    unit = sb("unit", [D, N])
    h = [sb(f"h{p}", [D, N]) for p in range(2)]
    gate = [sb(f"gate{p}", [D, N]) for p in range(2)]
    gated = [sb(f"gated{c}", [D, N]) for c in range(nch)]

    weights_in = sem("weights_in")
    shifted = sem("shifted")
    centred = sem("centred")
    squared = sem("squared")
    var_done = sem("var_done")
    ln_ready = sem("ln_ready")
    rstd_ready = sem("rstd_ready")
    unit_ready = sem("unit_ready")
    h_ready = sem("h_ready")
    a_done = sem("a_done")
    g_done = sem("g_done")
    gate_ready = sem("gate_ready")
    gated_ready = sem("gated_ready")
    y_done = sem("y_done")
    x_updated = sem("x_updated")
    ALL_WEIGHTS = 16 * (1 + 3 * nch + 3)

    half = D // 2

    with nc.Block() as block:

        @block.vector
        def _(dve):
            dve.memset(eps[:], EPS)
            for p in range(2):
                dve.memset(shift[p][half:D, 0:1], 0.0)

    def phase(layer):
        def wait(eng, semaphore, seqs, per=1, more=0):
            if known(seqs) and seqs * per + more <= 0:
                return
            eng.wait_ge(semaphore, layer * (B * per) + seqs * per + more)

        with ExitStack() as ctx:
            def ps(name):
                return ctx.enter_context(nc.psum_tensor("f_" + name, [D, N], F32))

            centred_ps, var_ps, y_ps = ps("centred_ps"), ps("var_ps"), ps("y_ps")
            a_ps = [ps(f"a_ps{p}") for p in range(2)]
            g_ps = [ps(f"g_ps{p}") for p in range(2)]

            with nc.Block() as block:

                @block.sync
                def _(sp):
                    one = bass.ds(layer, 1)
                    sp.dma_start(w1[:], dram["w1"][one].rearrange("l p n -> p (l n)")).then_inc(weights_in, 16)
                    for c, (a, n) in enumerate(CHUNKS):
                        sp.dma_start(w2[0:n, c, :], dram["w2"][one, a:a + n, :].rearrange("l p n -> p (l n)")).then_inc(weights_in, 16)
                        for k in range(2):
                            sp.dma_start(b1[0:n, k, c:c + 1], dram["b1"][one, k * HID + a:k * HID + a + n]
                                         .rearrange("l p -> p l")).then_inc(weights_in, 16)
                    for k, name in enumerate(("ln_g", "ln_b", "b2")):
                        sp.dma_start(vecs[:, k:k + 1], dram[name][one].rearrange("l p -> p l")).then_inc(weights_in, 16)

                @block.scalar
                def _(act):
                    act.preload_act_table_set(EXP_LN)
                    act.wait_ge(weights_in, (layer + 1) * ALL_WEIGHTS)

                    def shift_tokens(s, w):
                        wait(act, centred, s - 1)
                        act.activation(w[0:half, :], hid[0:half, columns(s)], ACT.Copy).then_inc(shifted, 1)
                        act.activation(w[half:D, 1:N], hid[half:D, bass.ds(s * N, N - 1)], ACT.Copy).then_inc(shifted, 1)

                    def step(s, u, r):
                        main = not (known(s) and s < 0)
                        ahead = not (known(s) and s + 1 >= B)

                        def gelu(c):
                            q, n = (nch * u + c) % 2, CHUNKS[c][1]
                            wait(act, g_done, s, nch, c + 1)
                            wait(act, gated_ready, s, nch, c - 1)
                            act.activation(gate[q][0:n], g_ps[q][0:n], ACT.Gelu, bias=b1[0:n, 1, c:c + 1]).then_inc(gate_ready, 1)
                        if main:
                            gelu(0)
                        if ahead:
                            if known(s) and s < 0:
                                shift_tokens(0, shift[0])
                            wait(act, centred, s + 2)
                            wait(act, var_done, s + 1)
                            act.activation(squares[:], centred_ps[:], ACT.Square).then_inc(squared, 1)
                        if main:
                            gelu(1)
                            gelu(2)
                        if not (known(s) and s + 2 >= B):
                            shift_tokens(s + 2, shift[u % 2])
                        if ahead:
                            act.preload_act_table_set(EXP_LN)
                            wait(act, var_done, s + 2)
                            act.activation(ln_var[:], var_ps[:], ACT.Ln, bias=eps[:]).then_inc(ln_ready, 1)
                            wait(act, ln_ready, s + 2)
                            wait(act, unit_ready, s + 1)
                            act.activation(rstd[:], ln_var[:], ACT.Exp, scale=-0.5).then_inc(rstd_ready, 1)
                    run_steps(act, step, B, 1, 2)

                @block.tensor
                def _(pe):
                    pe.wait_ge(weights_in, (layer + 1) * ALL_WEIGHTS)

                    def step(s, u, r):
                        main = not (known(s) and s < 0)
                        ahead = not (known(s) and s + 1 >= B)

                        def widen(c):
                            (a, n), q = CHUNKS[c], (nch * u + c) % 2
                            wait(pe, h_ready, s + 1)
                            wait(pe, gate_ready, s, nch, c - 1)
                            pe.matmul(g_ps[q][0:n], w1[:, HID + a:HID + a + n], h[u % 2][:], start=True, stop=True).then_inc(g_done, 1)
                            wait(pe, gated_ready, s, nch, c - 1)
                            pe.matmul(a_ps[q][0:n], w1[:, a:a + n], h[u % 2][:], start=True, stop=True).then_inc(a_done, 1)

                        if main:
                            widen(0)
                        if ahead:
                            wait(pe, shifted, s + 2, 2)
                            wait(pe, unit_ready, s + 1)
                            pe.matmul(centred_ps[:], centre[:], shift[(u + 1) % 2][:], start=True, stop=True).then_inc(centred, 1)
                        if main:
                            widen(1)
                        if ahead:
                            wait(pe, squared, s + 2)
                            wait(pe, ln_ready, s + 1)
                            pe.matmul(var_ps[:], average[:], squares[:], start=True, stop=True).then_inc(var_done, 1)
                        if main:
                            widen(2)
                            wait(pe, x_updated, s)
                            for c, (a, n) in enumerate(CHUNKS):
                                wait(pe, gated_ready, s, nch, c + 1)
                                ins = pe.matmul(y_ps[:], w2[0:n, c, :], gated[c][0:n], start=(c == 0), stop=(c == nch - 1))
                            ins.then_inc(y_done, 1)
                    run_steps(pe, step, B, 1, 2)

                @block.vector
                def _(dve):
                    dve.wait_ge(weights_in, (layer + 1) * ALL_WEIGHTS)

                    def step(s, u, r):
                        main = not (known(s) and s < 0)
                        ahead = not (known(s) and s + 1 >= B)

                        def apply_gate(c):
                            q, n = (nch * u + c) % 2, CHUNKS[c][1]
                            wait(dve, gate_ready, s, nch, c + 1)
                            wait(dve, a_done, s, nch, c + 1)
                            wait(dve, y_done, s)
                            dve.scalar_tensor_tensor(out=gated[c][0:n], in0=a_ps[q][0:n], scalar=b1[0:n, 0, c:c + 1],
                                                     in1=gate[q][0:n], op0=ALU.add, op1=ALU.mult).then_inc(gated_ready, 1)
                        if main:
                            for c in range(nch):
                                apply_gate(c)
                        if ahead:
                            wait(dve, rstd_ready, s + 2)
                            wait(dve, h_ready, s + 1)
                            dve.tensor_tensor(unit[:], centred_ps[:], rstd[:], ALU.mult).then_inc(unit_ready, 1)
                            wait(dve, unit_ready, s + 2)
                            wait(dve, a_done, s, nch)
                            dve.tensor_scalar(h[(u + 1) % 2][:], unit[:], vecs[:, LG:LG + 1], vecs[:, LB:LB + 1],
                                              ALU.mult, ALU.add).then_inc(h_ready, 1)
                        if main:
                            wait(dve, y_done, s + 1)
                            x = hid[:, columns(s)]
                            dve.scalar_tensor_tensor(out=x, in0=y_ps[:], scalar=vecs[:, B2:B2 + 1], in1=x,
                                                     op0=ALU.add, op1=ALU.add).then_inc(x_updated, 1)
                    run_steps(dve, step, B, 1, 2)
    return phase


EXPERTS = 8
H1, DH1 = 16, 8
LEVELS = int(np.log2(N))
HALO = 3 * N // 4
SKEW = H1
RING = 2 * N + SKEW
NSLOT = [min(3, N // 2 ** x - 1) for x in range(LEVELS)]
NCOL = [N // 2 ** x for x in range(LEVELS)]
SLOTS = 3
LEVEL = [sum(NCOL[:x]) for x in range(LEVELS + 1)]
LEVEL_COLS = LEVEL[-1]
PADS = N + SLOTS * LEVEL_COLS
NPAIR = -(-PADS // N) * N
NBANK = NPAIR // N
MADE = 2 + SLOTS - NSLOT[-1]


def phase_gate(nc, hid, s_res):
    with ExitStack() as ctx:
        th = [ctx.enter_context(nc.sbuf_tensor(f"g_tanh{p}", [D, N], F32)) for p in range(2)]
        silu2 = [ctx.enter_context(nc.sbuf_tensor(f"g_silu2{p}", [D, N], F32)) for p in range(2)]
        tanh_ready, silu_ready, gated_ready = (
            ctx.enter_context(nc.semaphore("g_" + n)) for n in ("tanh_ready", "silu_ready", "gated_ready"))
        with nc.Block() as block:

            @block.scalar
            def _(act):
                act.preload_act_table_set("exp_and_others")

                def step(s, u, r):
                    reach(act, silu_ready, s - 1)
                    act.activation(th[u][:], hid[:, columns(s)], ACT.Tanh, scale=0.5).then_inc(tanh_ready, 1)
                run_steps(act, step, B, 0, 2)

            @block.vector
            def _(dve):
                def step(s, u, r):
                    dve.wait_ge(tanh_ready, s + 1)
                    reach(dve, gated_ready, s - 1)
                    dve.scalar_tensor_tensor(out=silu2[u][:], in0=th[u][:], scalar=1.0, in1=hid[:, columns(s)],
                                             op0=ALU.add, op1=ALU.mult).then_inc(silu_ready, 1)
                    dve.wait_ge(silu_ready, s + 1)
                    dve.scalar_tensor_tensor(out=s_res[:, columns(s)], in0=silu2[u][:], scalar=0.5,
                                             in1=s_res[:, columns(s)], op0=ALU.mult, op1=ALU.mult).then_inc(gated_ready, 1)
                run_steps(dve, step, B, 0, 2)


def phase_sparse_attention(nc, dram, ident, ident_bf, centre, average, xres, s_res, gate_logits):
    with ExitStack() as ctx:
        def sb(name, shape, dt=F32):
            return ctx.enter_context(nc.sbuf_tensor("c_" + name, shape, dt))

        def ps(name):
            return ctx.enter_context(nc.psum_tensor("c_" + name, [D, N], F32))

        def sem(name):
            return ctx.enter_context(nc.semaphore("c_" + name))

        w = sb("w", [D, 6, D])
        vecs = sb("vecs", [D, 6])
        gate_w = sb("gate_w", [D, EXPERTS])
        eps = sb("eps", [D, 1])
        rope = sb("rope", [D, 2, N])
        counts = sb("counts", [D, NPAIR])
        mask = sb("mask", [D, NPAIR], BF16)
        same_head = sb("same_head", [D, D])
        x_in = [sb(f"x_in{p}", [D, TT, D]) for p in range(2)]
        xn = sb("xn", [D, N])
        tokens = [sb(f"tokens{p}", [D, N]) for p in range(2)]
        squares, rstd = sb("squares", [D, N]), sb("rstd", [D, N])
        ln_var = squares
        by_cos, by_sin = sb("by_cos", [D, N]), sb("by_sin", [D, N])
        qkv = sb("qkv", [D, 3, N])
        q_skew = sb("q_skew", [D, N])
        k_skew = sb("k_skew", [D, HALO + N])
        v_skew = [sb(f"v_skew{p}", [D, HALO + N]) for p in range(2)]
        product = sb("product", [D, NPAIR])
        logits = [sb(f"logits{p}", [D, NPAIR]) for p in range(2)]
        values = sb("values", [D, NPAIR])
        largest = sb("largest", [D, N])
        denominator = sb("denominator", [D, N])
        level_out = sb("level_out", [D, LEVEL_COLS])
        ln_sum, inverse = sb("ln_sum", [D, N]), sb("inverse", [D, N])
        mixed = sb("mixed", [D, N])
        mixed_back = sb("mixed_back", [D, N])
        ring = dram["ring"]
        back = dram["back"]

        x_ps, centred_ps, var_ps, out_ps = ps("x_ps"), ps("centred_ps"), ps("var_ps"), ps("out_ps")
        proj_ps = [ps(f"proj_ps{k}") for k in range(2)]
        pair_ps = [ps(f"pair_ps{k}") for k in range(2)]

        consts_in = sem("consts_in")
        consts_made = sem("consts_made")
        x_loaded = [sem(f"x_loaded{p}") for p in range(2)]
        x_turned = sem("x_turned")
        x_ready = sem("x_ready")
        centred = sem("centred")
        squared = sem("squared")
        var_done = sem("var_done")
        ln_ready = sem("ln_ready")
        rstd_ready = sem("rstd_ready")
        xn_ready = sem("xn_ready")
        xn_turned = sem("xn_turned")
        tokens_ready = sem("tokens_ready")
        gates_ready = sem("gates_ready")
        tokens_stored = [sem(f"tokens_stored{p}") for p in range(2)]
        proj_done = sem("proj_done")
        rope_products = sem("rope_products")
        qk_ready = sem("qk_ready")
        v_ready = sem("v_ready")
        ring_written = sem("ring_written")
        q_skewed = sem("q_skewed")
        k_skewed = sem("k_skewed")
        v_skewed = [sem(f"v_skewed{p}") for p in range(2)]
        products = sem("products")
        counted_ready = sem("counted_ready")
        pairs_done = sem("pairs_done")
        logits_ready = sem("logits_ready")
        folded = sem("folded")
        shifted = sem("shifted")
        exp_ready = sem("exp_ready")
        weighted = sem("weighted")
        summed = sem("summed")
        ln_sum_ready = sem("ln_sum_ready")
        inverse_ready = sem("inverse_ready")
        mixed_ready = sem("mixed_ready")
        back_written = sem("back_written")
        back_read = sem("back_read")
        out_done = sem("out_done")
        s_ready = sem("s_ready")
        BQ, BQR, BK, BKR, BV, BO = range(6)
        LOADS = 16 * (6 + 2 + 8 + 4 + 1)
        EXPS = 3
        NOPS = 1 + LEVELS
        FOLD = 2 + LEVELS
        MAX_FOLD, SUM_FOLD = 0, FOLD

        def slots(buf, x, n=SLOTS):
            return buf[:, N:N + SLOTS * LEVEL_COLS].rearrange("p (k m) -> p k m", k=SLOTS)[:, 0:n, LEVEL[x]:LEVEL[x + 1]]

        def queries(buf, x, n=SLOTS):
            v = buf[:, 0:N].rearrange("p (m r) -> p m r", r=2 ** x)[:, :, 0]
            return v.unsqueeze(1).to_broadcast([D, n, NCOL[x]])

        def own(buf, x):
            return buf[:, 0:N].rearrange("p (m r) -> p m r", r=2 ** x)[:, :, 0]

        def earlier(buf, x):
            r = 2 ** x
            start = HALO - NSLOT[x] * r
            base = buf[:, start:start + 1]
            a = [list(d) for d in base.ap]
            return bass.AP(base.tensor, base.offset, [a[0], [r, NSLOT[x]], [r, NCOL[x]]])

        def skewed(t, p, parts, start, width, rows, step):
            base = t[p]
            first = base.offset + start
            dims = [[DH1 * rows + step, H1], [rows, DH1]]
            if parts is not None:
                first += parts * RING
            return bass.AP(base.tensor, first, dims + [[1, width]])

        def exists(s):
            return not known(s) or 0 <= s < B

        def run(eng, step):
            run_steps(eng, step, B, 2, 2)
            for s in (B, B + 1):
                step(s, s % 2, s // 2)

        with nc.Block() as block:

            @block.sync
            def _(sp):
                for k, name in enumerate(("Wq", "Wk")):
                    half = D // 2
                    sp.dma_start(w[:, 2 * k, :], dram[name]).then_inc(consts_in, 16)
                    for a, b in ((0, half), (half, 0)):
                        sp.dma_start(w[:, 2 * k + 1, a:a + half], dram[name][:, b:b + half]).then_inc(consts_in, 16)
                for k, name in enumerate(("Wv", "Wo")):
                    sp.dma_start(w[:, 4 + k, :], dram[name]).then_inc(consts_in, 16)
                for k, name in enumerate(("bq", "bk")):
                    half = D // 2
                    sp.dma_start(vecs[:, 2 * k:2 * k + 1], dram[name]).then_inc(consts_in, 16)
                    for a, b in ((0, half), (half, 0)):
                        sp.dma_start(vecs[a:a + half, 2 * k + 1:2 * k + 2], dram[name][b:b + half]).then_inc(consts_in, 16)
                for k, name in enumerate(("bv", "bo")):
                    sp.dma_start(vecs[:, 4 + k:5 + k], dram[name]).then_inc(consts_in, 16)
                sp.dma_start(gate_w[:], dram["gate_w"]).then_inc(consts_in, 16)
                for dst, name in ((rope, "rope1"), (counts, "counts"), (mask, "pair_mask"), (same_head, "same_head")):
                    sp.dma_start(dst[:], dram[name]).then_inc(consts_in, 16)

                def step(s, u, r):
                    q = (u + 1) % 2
                    if exists(s + 2):
                        reach(sp, x_turned, s + 1)
                        src = (dram["x"][s + 2] if known(s) else
                               dram["x"][bass.ds(s + 2, 1)].rearrange("o t d -> (o t) d"))
                        sp.dma_start(x_in[u][:], src.rearrange("(t p) d -> p t d", p=D)).then_inc(x_loaded[u], 16)
                    if exists(s + 1):
                        if not known(s) or s >= 1:
                            sp.wait_ge(v_skewed[q], 16 * (r + u))
                        sp.wait_ge(qk_ready, 2 * s + 4)
                        sp.wait_ge(v_ready, s + 2)
                        sp.dma_start(ring[q][:, :, N:2 * N], qkv[:]).then_inc(ring_written, 16)
                        sp.dma_start(ring[q][:, 1:3, N - HALO:N], qkv[:, 1:3, N - HALO:N]).then_inc(ring_written, 16)
                        sp.dma_start(ring[q][:, :, 2 * N:RING], qkv[:, :, 0:SKEW]).then_inc(ring_written, 16)
                    if exists(s - 2):
                        sp.wait_ge(mixed_ready, s - 1)
                        sp.dma_start(back[u].rearrange("p (a n) -> p a n", a=2),
                                     mixed[:].unsqueeze(1).to_broadcast([D, 2, N])).then_inc(back_written, 16)
                    if exists(s + 1):
                        reach(sp, products, NOPS * s + NOPS)
                        sp.wait_ge(ring_written, 48 * s + 96)
                        sp.dma_start(q_skew[:], skewed(ring, q, 0, N, N, 3 * RING, 1)).then_inc(q_skewed, 16)
                        sp.dma_start(k_skew[:], skewed(ring, q, 1, N - HALO, HALO + N, 3 * RING, 1)).then_inc(k_skewed, 16)
                    if exists(s - 2):
                        reach(sp, out_done, s - 2)
                        sp.wait_ge(back_written, 16 * s - 16)
                        sp.dma_start(mixed_back[:], skewed(back, u, None, N, N, 2 * N, -1)).then_inc(back_read, 16)
                    if exists(s + 1):
                        sp.wait_ge(tokens_ready, s + 2)
                        sp.dma_start(dram["tokens"][s + 1] if known(s) else
                                     dram["tokens"][bass.ds(s + 1, 1)].rearrange("o p n -> (o p) n"),
                                     tokens[q][:]).then_inc(tokens_stored[q], 16)
                        reach(sp, weighted, NOPS * s)
                        sp.dma_start(v_skew[q][:], skewed(ring, q, 2, N - HALO, HALO + N, 3 * RING, 1)).then_inc(v_skewed[q], 16)
                run(sp, step)
                for p in range(2):
                    sp.wait_ge(tokens_stored[p], 16 * (B // 2))

            @block.gpsimd
            def _(pool):
                pool.memset(product[:, PADS:NPAIR], 0.0).then_inc(consts_made, 1)
                for k in range(NSLOT[LEVELS - 1], SLOTS):
                    pool.memset(product[:, N + k * LEVEL_COLS + LEVEL[LEVELS - 1]:N + (k + 1) * LEVEL_COLS],
                                0.0).then_inc(consts_made, 1)
                pool.memset(eps[:], EPS).then_inc(consts_made, 1)
                pool.wait_ge(consts_in, LOADS)
                pool.wait_ge(consts_made, MADE)

                def step(s, u, r):
                    if exists(s):
                        for x in range(LEVELS + 1):
                            src = product[:, 0:N] if x == LEVELS else slots(product, x, NSLOT[x])
                            c = counts[:, 0:N] if x == LEVELS else slots(counts, x, NSLOT[x])
                            pool.wait_ge(products, s * NOPS + 1 + x)
                            pool.tensor_tensor(src, src, c, ALU.mult).then_inc(counted_ready, 1)
                    if exists(s - 1):
                        p = (u + 1) % 2
                        for x in range(LEVELS + 1):
                            pool.wait_ge(exp_ready, EXPS * (s - 1) + (1 if x == 0 else EXPS if x == LEVELS else 2))
                            if x == 0:
                                pool.wait_ge(v_skewed[p], 16 * (r + u))
                                reach(pool, summed, s - 1)
                            out, e, v = ((values[:, 0:N], logits[p][:, 0:N], v_skew[p][:, HALO:]) if x == LEVELS else
                                         (slots(values, x, NSLOT[x]), slots(logits[p], x, NSLOT[x]), earlier(v_skew[p], x)))
                            pool.tensor_tensor(out, e, v, ALU.mult).then_inc(weighted, 1)
                run(pool, step)

            @block.scalar
            def _(act):
                act.preload_act_table_set(EXP_LN)
                act.wait_ge(consts_in, LOADS)
                act.wait_ge(consts_made, MADE)

                def step(s, u, r):
                    q = (u + 1) % 2

                    def evacuate(b):
                        act.wait_ge(pairs_done, s * NBANK + b + 1)
                        if b == 0:
                            reach(act, weighted, NOPS * (s - 1))
                            reach(act, folded, 2 * FOLD * (s - 1))
                        act.activation(logits[u][:, b * N:(b + 1) * N], pair_ps[b % 2][:], ACT.Copy).then_inc(logits_ready, 1)

                    def exponentials(part):
                        first = slots(logits[q], 0)
                        rest = (logits[q][:, N:N + SLOTS * LEVEL_COLS].rearrange("p (k m) -> p k m", k=SLOTS)
                                [:, :, LEVEL[1]:])
                        v = (first, rest, logits[q][:, 0:N])[part]
                        act.wait_ge(shifted, NOPS * (s - 1) + (1, LEVELS, NOPS)[part])
                        act.activation(v, v, ACT.Exp).then_inc(exp_ready, 1)

                    if exists(s + 1):
                        act.wait_ge(proj_done, 5 * (s + 1) + 1)
                        reach(act, ring_written, 48 * (s + 1))
                        act.activation(qkv[:, 2, :], proj_ps[0][:], ACT.Identity, bias=vecs[:, BV:BV + 1]).then_inc(v_ready, 1)
                    if exists(s - 2):
                        act.wait_ge(folded, 2 * FOLD * (s - 1))
                        act.activation(ln_sum[:], denominator[:], ACT.Ln).then_inc(ln_sum_ready, 1)
                        act.wait_ge(ln_sum_ready, s - 1)
                        reach(act, mixed_ready, s - 2)
                        act.activation(inverse[:], ln_sum[:], ACT.Exp, scale=-1.0).then_inc(inverse_ready, 1)
                    if exists(s + 1):
                        act.wait_ge(xn_turned, s + 2)
                        if not known(s) or s + 1 >= 2:
                            act.wait_ge(tokens_stored[q], 16 * (r + u))
                        act.activation(tokens[q][:], x_ps[:], ACT.Copy).then_inc(tokens_ready, 1)
                        act.activation(gate_logits[:, columns(s + 1, TT * EXPERTS)], var_ps[:, 0:TT * EXPERTS],
                                       ACT.Copy).then_inc(gates_ready, 1)
                    for part in range(EXPS):
                        if exists(s - 1):
                            exponentials(part)
                        if exists(s):
                            evacuate(part)
                    if exists(s):
                        evacuate(3)
                    if exists(s + 2):
                        act.wait_ge(centred, s + 3)
                        reach(act, var_done, s + 2)
                        act.activation(squares[:], centred_ps[:], ACT.Square).then_inc(squared, 1)
                    if exists(s):
                        for b in range(4, NBANK):
                            evacuate(b)
                    if exists(s - 2):
                        act.wait_ge(out_done, s - 1)
                        act.activation(s_res[:, columns(s - 2)], out_ps[:], ACT.Identity,
                                       bias=vecs[:, BO:BO + 1]).then_inc(s_ready, 1)
                    if exists(s + 2):
                        act.wait_ge(var_done, s + 3)
                        act.activation(ln_var[:], var_ps[:], ACT.Ln, bias=eps[:]).then_inc(ln_ready, 1)
                        act.wait_ge(ln_ready, s + 3)
                        reach(act, xn_ready, s + 2)
                        act.activation(rstd[:], ln_var[:], ACT.Exp, scale=-0.5).then_inc(rstd_ready, 1)
                run(act, step)

            @block.tensor
            def _(pe):
                pe.wait_ge(consts_in, LOADS)

                def project(k, bank, s):
                    pe.matmul(proj_ps[bank][:], w[:, k, :], xn[:], start=True, stop=True).then_inc(proj_done, 1)

                def add_values(x):
                    for k in range(NSLOT[x]):
                        ins = pe.matmul(own(out_ps, x), ident[:], slots(values, x)[:, k, :], start=False,
                                        stop=(x == LEVELS - 1), skip_group_check=True)
                    return ins

                def step(s, u, r):
                    q = (u + 1) % 2

                    def pairs(b):
                        reach(pe, logits_ready, s * NBANK + max(b - 1, 0))
                        pe.matmul(pair_ps[b % 2][:], ident_bf[:], mask[:, b * N:(b + 1) * N],
                                  start=True, stop=False, skip_group_check=True)
                        if b == 0:
                            pe.wait_ge(counted_ready, s * NOPS + NOPS)
                        pe.matmul(pair_ps[b % 2][:], same_head[:], product[:, b * N:(b + 1) * N],
                                  start=False, stop=True, skip_group_check=True).then_inc(pairs_done, 1)

                    if exists(s - 2):
                        pe.wait_ge(weighted, NOPS * (s - 1))
                        reach(pe, s_ready, s - 2)
                        pe.matmul(out_ps[:], ident[:], values[:, 0:N], start=True, stop=False, skip_group_check=True)
                        add_values(0)
                    if exists(s + 1):
                        pe.wait_ge(xn_ready, s + 2)
                        reach(pe, qk_ready, 2 * (s + 1))
                        project(4, 0, s)
                        project(1, 1, s)
                        for t in range(TT):
                            pe.transpose(x_ps[:, t * D:(t + 1) * D], xn[:, t * D:(t + 1) * D], ident[:])
                        for t in range(TT):
                            ins = pe.matmul(var_ps[:, t * EXPERTS:(t + 1) * EXPERTS], xn[:, t * D:(t + 1) * D], gate_w[:],
                                            start=True, stop=True, skip_group_check=True)
                        ins.then_inc(xn_turned, 1)
                        pe.wait_ge(v_ready, s + 2)
                        project(0, 0, s)
                    if exists(s - 2):
                        add_values(1)
                        add_values(2)
                    if exists(s + 1):
                        pe.wait_ge(rope_products, 4 * (s + 1) + 2)
                        project(2, 0, s)
                        project(3, 1, s)
                    if exists(s - 2):
                        for x in range(3, LEVELS):
                            ins = add_values(x)
                        ins.then_inc(summed, 1)
                    if exists(s + 2):
                        pe.wait_ge(x_loaded[u], 16 * (r + 2))
                        reach(pe, tokens_ready, s + 2)
                        for t in range(TT):
                            ins = pe.transpose(x_ps[:, t * D:(t + 1) * D], x_in[u][:, t, :], ident[:])
                        ins.then_inc(x_turned, 1)
                    if exists(s):
                        for b in range(3):
                            pairs(b)
                    if exists(s + 2):
                        pe.wait_ge(x_ready, s + 3)
                        reach(pe, xn_ready, s + 2)
                        pe.matmul(centred_ps[:], centre[:], xres[:, columns(s + 2)], start=True, stop=True).then_inc(centred, 1)
                    if exists(s):
                        for b in range(3, NBANK):
                            pairs(b)
                    if exists(s + 2):
                        pe.wait_ge(squared, s + 3)
                        reach(pe, gates_ready, s + 2)
                        pe.matmul(var_ps[:], average[:], squares[:], start=True, stop=True).then_inc(var_done, 1)
                    if exists(s - 2):
                        pe.wait_ge(back_read, 16 * (s - 1))
                        pe.wait_ge(mixed_ready, s - 1)
                        pe.matmul(out_ps[:], w[:, 5, :], mixed_back[:], start=True, stop=True).then_inc(out_done, 1)
                run(pe, step)

            @block.vector
            def _(dve):
                dve.wait_ge(consts_in, LOADS)

                def fold(src, out, op, n):
                    def slot(k):
                        return src[:, N + k * LEVEL_COLS:N + (k + 1) * LEVEL_COLS]
                    reach(dve, folded, n)
                    dve.tensor_tensor(level_out[:], slot(0), slot(1), op).then_inc(folded, 1)
                    dve.wait_ge(folded, n + 1)
                    dve.tensor_tensor(level_out[:], level_out[:], slot(2), op).then_inc(folded, 1)
                    for x in range(LEVELS):
                        dve.wait_ge(folded, n + 2 + x)
                        first = src[:, 0:N] if x == 0 else own(out, x)
                        dve.tensor_tensor(own(out, x), first, level_out[:, LEVEL[x]:LEVEL[x + 1]], op).then_inc(folded, 1)

                def rotate(k, s):
                    dve.wait_ge(proj_done, 5 * (s + 1) + 2 * k + 3)
                    reach(dve, qk_ready, 2 * (s + 1) + k)
                    dve.scalar_tensor_tensor(out=by_cos[:], in0=proj_ps[0][:], scalar=vecs[:, 2 * k:2 * k + 1],
                                             in1=rope[:, 0, :], op0=ALU.add, op1=ALU.mult).then_inc(rope_products, 1)
                    dve.scalar_tensor_tensor(out=by_sin[:], in0=proj_ps[1][:], scalar=vecs[:, 2 * k + 1:2 * k + 2],
                                             in1=rope[:, 1, :], op0=ALU.add, op1=ALU.mult).then_inc(rope_products, 1)
                    dve.wait_ge(rope_products, 4 * (s + 1) + 2 * k + 2)
                    if k == 0:
                        reach(dve, ring_written, 48 * (s + 1))
                    dve.tensor_tensor(qkv[:, k, :], by_cos[:], by_sin[:], ALU.add).then_inc(qk_ready, 1)

                def step(s, u, r):
                    q = (u + 1) % 2
                    cols = columns(s + 2)

                    def shift_level(x):
                        dve.tensor_tensor(slots(logits[q], x), slots(logits[q], x), queries(largest, x),
                                          ALU.subtract).then_inc(shifted, 1)

                    if exists(s):
                        dve.wait_ge(q_skewed, 16 * (s + 1))
                        dve.wait_ge(k_skewed, 16 * (s + 1))
                        reach(dve, pairs_done, NBANK * s)
                        for x in range(LEVELS):
                            dve.tensor_tensor(slots(product, x, NSLOT[x]), queries(q_skew, x, NSLOT[x]), earlier(k_skew, x),
                                              ALU.mult).then_inc(products, 1)
                        dve.tensor_tensor(product[:, 0:N], q_skew[:], k_skew[:, HALO:], ALU.mult).then_inc(products, 1)
                    if exists(s + 1):
                        dve.wait_ge(rstd_ready, s + 2)
                        reach(dve, xn_turned, s + 1)
                        dve.tensor_tensor(xn[:], centred_ps[:], rstd[:], ALU.mult).then_inc(xn_ready, 1)
                    n = 2 * FOLD * (s - 1)
                    if exists(s - 1):
                        dve.wait_ge(logits_ready, s * NBANK)
                        fold(logits[q], largest, ALU.max, n + MAX_FOLD)
                        dve.wait_ge(folded, n + FOLD)
                    if exists(s + 1):
                        rotate(0, s)
                    if exists(s - 1):
                        shift_level(0)
                    if exists(s + 1):
                        rotate(1, s)
                    if exists(s - 1):
                        for x in range(1, LEVELS):
                            shift_level(x)
                        dve.tensor_tensor(logits[q][:, 0:N], logits[q][:, 0:N], largest[:], ALU.subtract).then_inc(shifted, 1)
                    if exists(s - 2):
                        dve.wait_ge(inverse_ready, s - 1)
                        dve.wait_ge(summed, s - 1)
                        reach(dve, back_written, 16 * (s - 2))
                        dve.tensor_tensor(mixed[:], out_ps[:], inverse[:], ALU.mult).then_inc(mixed_ready, 1)
                    if exists(s + 2):
                        dve.wait_ge(x_turned, s + 3)
                        dve.tensor_tensor(xres[:, cols], x_ps[:], s_res[:, cols], ALU.add).then_inc(x_ready, 1)
                    if exists(s - 1):
                        dve.wait_ge(exp_ready, EXPS * s)
                        reach(dve, ln_sum_ready, s - 1)
                        fold(logits[q], denominator, ALU.add, n + SUM_FOLD)
                run(dve, step)


def rope1_table():
    f = np.float32
    inv_freq = (f(1.0) / f(15000.0) ** (np.arange(0, D, 2, dtype=f) / f(D))).astype(f)
    freqs = np.arange(N, dtype=f)[:, None] * inv_freq[None, :]
    emb = np.concatenate([freqs, freqs], -1).T
    sign = np.where(np.arange(D) < D // 2, f(-1), f(1))[:, None]
    return np.ascontiguousarray(np.stack([np.cos(emb), np.sin(emb) * sign], 1).astype(f))


def pair_tables():
    counts = np.zeros((H1, NPAIR), np.float32)
    idx = np.arange(N)
    for h in range(H1):
        count = np.zeros((N, N), np.float32)
        for x in range(LEVELS):
            ok = idx % 2 ** x == h % 2 ** x
            count += (idx[:, None] // 2 ** (x + 2) == idx[None, :] // 2 ** (x + 2)) & ok[:, None] & ok[None, :]
        taken = np.zeros((N, N), bool)
        counts[h, 0:N] = count[(idx + h) % N, (idx + h) % N]
        for x in reversed(range(LEVELS)):
            r = 2 ** x
            for slot in range(NSLOT[x]):
                k = NSLOT[x] - slot
                for m in range(NCOL[x]):
                    i = (m * r + h) % N
                    j = i - k * r
                    if j < 0 or taken[i, j] or count[i, j] == 0:
                        continue
                    taken[i, j] = True
                    counts[h, N + slot * LEVEL_COLS + LEVEL[x] + m] = count[i, j]
        need = (count > 0) & (idx[None, :] < idx[:, None])
        assert (taken == need).all()
    mask = np.where(counts > 0, 0.0, -1e30).astype(mybir.dt.np(BF16))
    return np.repeat(counts, DH1, 0), np.repeat(mask, DH1, 0)


DFF = 512
FC = DFF // D
NT = B * TT
BLOCK = 2 * D
NBLOCK = (B * N + EXPERTS * (BLOCK - 1)) // BLOCK
SORTED = NBLOCK * BLOCK
B1_COL, B2_COL = 2 * DFF, 2 * DFF + FC
EXPERT_ROW = 2 * DFF + FC + 4
RNE = 2.0 ** 23


def route_tokens(nc, dram, gate_logits, places, weight_rows):
    with ExitStack() as ctx:
        def sb(name, shape, dt=F32):
            return ctx.enter_context(nc.sbuf_tensor("r_" + name, shape, dt))

        def sem(name):
            return ctx.enter_context(nc.semaphore("r_" + name))

        xn_tokens = sb("xn_tokens", [D, B * N])
        gate_b = sb("gate_b", [D, 2, EXPERTS])
        rank = sb("rank", [D, EXPERTS])
        triangle = sb("triangle", [D, 2, D], BF16)
        restart = sb("restart", [D, EXPERTS * NT])
        block_number = sb("block_number", [D, NBLOCK])
        partition = sb("partition", [D, 1])
        logit, logit2, best = (sb(n, [D, NT, EXPERTS]) for n in ("logit", "logit2", "best"))
        top = [sb(f"top{k}", [D, NT]) for k in range(2)]
        one_hot = sb("one_hot", [D, NT, EXPERTS], BF16)
        total, seen = sb("total", [D, EXPERTS * NT]), sb("seen", [D, EXPERTS * NT])
        share = [sb(f"share{k}", [D, EXPERTS]) for k in range(3)]
        ones8 = sb("ones8", [D, EXPERTS])
        block_end, base = sb("block_end", [D, EXPERTS]), sb("base", [D, EXPERTS])
        place = sb("place", [D, NT, EXPERTS])
        place_f = sb("place_f", [D, NT])
        ended = sb("ended", [D, NBLOCK, EXPERTS])
        expert = [sb(f"expert{k}", [D, NBLOCK]) for k in range(3)]
        before_ps, total_ps = (ctx.enter_context(nc.psum_tensor("r_" + n, [D, NT, EXPERTS], F32)) for n in ("before_ps", "total_ps"))

        consts_in = sem("consts_in")
        tokens_in = sem("tokens_in")
        chain = sem("chain")
        chosen = sem("chosen")
        counted = sem("counted")
        placed = sem("placed")
        scattered = sem("scattered")

        with nc.Block() as block:

            @block.sync
            def _(sp):
                for k, name in enumerate(("gate_b", "expert_bias")):
                    sp.dma_start(gate_b[:, k, :], dram[name].to_broadcast([D, EXPERTS])).then_inc(consts_in, 16)
                for dst, name in ((rank, "rank"), (triangle, "triangle"), (restart, "restart"),
                                  (block_number, "block_number"), (partition, "partition")):
                    sp.dma_start(dst[:], dram[name]).then_inc(consts_in, 16)
                parts = 4
                for k in range(parts):
                    some = slice(k * B // parts, (k + 1) * B // parts)
                    sp.dma_start(xn_tokens[:, some.start * N:some.stop * N].rearrange("p (s n) -> p s n", n=N),
                                 dram["tokens"][some].rearrange("s p n -> p s n")).then_inc(tokens_in, 16)
                sp.wait_ge(tokens_in, 16 * parts)

            @block.tensor
            def _(pe):
                pe.wait_ge(chosen, 1)
                pe.matmul(before_ps[:], triangle[:, 0, :], one_hot[:], start=True, stop=True)
                pe.matmul(total_ps[:], triangle[:, 1, :], one_hot[:], start=True, stop=True).then_inc(counted, 1)

            @block.vector
            def _(dve):
                dve.wait_ge(consts_in, 7 * 16)
                steps = [0]

                def then(ins):
                    ins.then_inc(chain, 1)
                    steps[0] += 1
                    dve.wait_ge(chain, steps[0])

                def by_tile(row):
                    return row.unsqueeze(1).to_broadcast([D, NT, EXPERTS])

                def by_expert(column):
                    return column.unsqueeze(2).to_broadcast([D, NT, EXPERTS])

                products = gate_logits[:].rearrange("p (j e) -> p j e", e=EXPERTS)
                then(dve.tensor_tensor(logit[:], products, by_tile(gate_b[:, 0, :]), ALU.add))
                then(dve.tensor_tensor(logit2[:], logit[:], by_tile(gate_b[:, 1, :]), ALU.add))
                then(dve.tensor_reduce(top[0][:], logit2[:], AX_X, ALU.max))
                tied = logit
                then(dve.tensor_tensor(tied[:], logit2[:], by_expert(top[0][:]), ALU.is_ge))
                then(dve.tensor_tensor(best[:], tied[:], by_tile(rank[:]), ALU.mult))
                then(dve.tensor_reduce(top[1][:], best[:], AX_X, ALU.max))
                dve.tensor_tensor(one_hot[:], best[:], by_expert(top[1][:]), ALU.is_equal).then_inc(chosen, 1)
                dve.wait_ge(counted, 1)
                then(dve.tensor_copy(total[:].rearrange("p (e j) -> p e j", e=EXPERTS), total_ps[:].rearrange("p j e -> p e j")))
                then(dve.tensor_tensor_scan(seen[:], restart[:], total[:], 0.0, ALU.mult, ALU.add))
                then(dve.tensor_scalar(share[0][:], seen[:, NT - 1::NT], 1.0 / BLOCK,
                                       (BLOCK - 1.0) / BLOCK - 0.5 + 0.5 / BLOCK, ALU.mult, ALU.add))
                then(dve.tensor_scalar(share[1][:], share[0][:], RNE, None, ALU.add))
                then(dve.tensor_scalar(share[2][:], share[1][:], -RNE, None, ALU.add))
                then(dve.memset(ones8[:], 1.0))
                then(dve.tensor_tensor_scan(block_end[:], ones8[:], share[2][:], 0.0, ALU.mult, ALU.add))
                then(dve.tensor_tensor(share[0][:], block_end[:], share[2][:], ALU.subtract))
                then(dve.tensor_scalar(base[:], share[0][:], float(BLOCK), None, ALU.mult))
                then(dve.tensor_tensor(place[:], before_ps[:], seen[:].rearrange("p (e j) -> p j e", e=EXPERTS), ALU.add))
                then(dve.tensor_tensor(logit[:], place[:], total[:].rearrange("p (e j) -> p j e", e=EXPERTS), ALU.subtract))
                then(dve.tensor_tensor(logit2[:], logit[:], by_tile(base[:]), ALU.add))
                then(dve.tensor_tensor(place[:], logit2[:], one_hot[:], ALU.mult))
                then(dve.tensor_reduce(place_f[:], place[:], AX_X, ALU.add))
                dve.tensor_copy(places[:], place_f[:]).then_inc(placed, 1)
                then(dve.tensor_tensor(ended[:], block_end[:].unsqueeze(1).to_broadcast([D, NBLOCK, EXPERTS]),
                                       block_number[:].unsqueeze(2).to_broadcast([D, NBLOCK, EXPERTS]), ALU.is_le))
                then(dve.tensor_reduce(expert[0][:], ended[:], AX_X, ALU.add))
                then(dve.tensor_scalar(expert[1][:], expert[0][:], float(EXPERTS - 1), float(D), ALU.min, ALU.mult))
                then(dve.tensor_scalar(expert[2][:], expert[1][:], partition[:], None, ALU.add))
                dve.tensor_copy(weight_rows[:], expert[2][:]).then_inc(placed, 1)

            @block.gpsimd
            def _(pool):
                pool.wait_ge(tokens_in, 64)
                pool.wait_ge(placed, 1)
                for j in range(NT):
                    pool.indirect_dma_start(dram["sorted"], bass.IndirectOffsetOnAxis(ap=places[:, j:j + 1], axis=0),
                                            xn_tokens[:, j * D:(j + 1) * D], None).then_inc(scattered, 16)
                pool.wait_ge(scattered, 16 * NT)


def run_experts(nc, dram, ident, weight_rows):
    with ExitStack() as ctx:
        def sb(name, shape, dt=F32):
            return ctx.enter_context(nc.sbuf_tensor("e_" + name, shape, dt))

        def ps(name, shape):
            return ctx.enter_context(nc.psum_tensor("e_" + name, shape, F32))

        def sem(name):
            return ctx.enter_context(nc.semaphore("e_" + name))

        U = 3
        HALF = FC // 2
        HT = BLOCK // D
        rows_in = [sb(f"rows_in{u}", [D, HT, D]) for u in range(U)]
        w = [sb(f"w{u}", [D, EXPERT_ROW]) for u in range(U)]
        x_t = [sb(f"x_t{u}", [D, BLOCK]) for u in range(U)]
        hidden = [sb(f"hidden{u}", [D, FC, BLOCK]) for u in range(U)]
        y_t = [sb(f"y_t{u}", [D, BLOCK]) for u in range(U)]
        rows_out = [sb(f"rows_out{u}", [D, HT, D]) for u in range(U)]
        x_ps, y_ps = ps("x_ps", [D, 512]), ps("y_ps", [D, 512])
        rows_ps = ps("rows_ps", [D, 512])
        hidden_ps = [ps(f"hidden_ps{k}", [D, HALF, BLOCK]) for k in range(2)]

        weights_in = [sem(f"weights_in{u}") for u in range(U)]
        rows_loaded = [sem(f"rows_loaded{u}") for u in range(U)]
        x_turned = sem("x_turned")
        x_ready = sem("x_ready")
        hidden_done = [sem(f"hidden_done{k}") for k in range(2)]
        relu_ready = [sem(f"relu_ready{k}") for k in range(2)]
        y_done = sem("y_done")
        y_ready = sem("y_ready")
        y_turned = sem("y_turned")
        rows_ready = sem("rows_ready")
        rows_stored = [sem(f"rows_stored{u}") for u in range(U)]

        def exists(s):
            return not known(s) or 0 <= s < NBLOCK

        def run(eng, step):
            run_steps(eng, step, NBLOCK, 2, U)
            for s in (NBLOCK, NBLOCK + 1):
                step(s, s % U, s // U)

        def block_rows(t, s):
            if known(s):
                return t[s * BLOCK:(s + 1) * BLOCK].rearrange("(h p) d -> p h d", p=D)
            return t.rearrange("(b h p) d -> b p h d", p=D, h=HT)[bass.ds(s, 1)].rearrange("o p h d -> p (o h) d")

        with nc.Block() as block:

            @block.sync
            def _(sp):
                def step(s, u, r):
                    if exists(s + 2):
                        q = (u + 2) % U
                        reach(sp, x_turned, s)
                        sp.dma_start(rows_in[q][:], block_rows(dram["sorted"], s + 2)).then_inc(rows_loaded[q], 16)
                    if exists(s - 2):
                        q = (u + 1) % U
                        sp.wait_ge(rows_ready, s - 1)
                        sp.dma_start(block_rows(dram["answers"], s - 2), rows_out[q][:]).then_inc(rows_stored[q], 16)
                run(sp, step)
                for u in range(U):
                    sp.wait_ge(rows_stored[u], 16 * (NBLOCK // U))

            @block.gpsimd
            def _(pool):
                for s in range(NBLOCK):
                    reach(pool, y_ready, s - U + 1)
                    pool.indirect_dma_start(w[s % U][:], None, dram["weights"],
                                            bass.IndirectOffsetOnAxis(ap=weight_rows[:, s:s + 1], axis=0)
                                            ).then_inc(weights_in[s % U], 16)

            @block.scalar
            def _(act):
                act.preload_act_table_set("exp_and_others")

                def step(s, u, r):
                    if exists(s + 1):
                        act.wait_ge(x_turned, s + 2)
                        reach(act, hidden_done[1], s - 1)
                        act.activation(x_t[(u + 1) % U][:], x_ps[:, 0:BLOCK], ACT.Copy).then_inc(x_ready, 1)
                    if exists(s):
                        act.wait_ge(hidden_done[0], s + 1)
                        reach(act, y_done, s - 2)
                        for c in range(HALF):
                            act.activation(hidden[u][:, c, :], hidden_ps[0][:, c, :], ACT.Relu,
                                           bias=w[u][:, B1_COL + c:B1_COL + c + 1]).then_inc(relu_ready[0], 1)
                    if exists(s - 1):
                        q = (u + 2) % U
                        act.wait_ge(y_done, s)
                        reach(act, y_turned, s - 3)
                        act.activation(y_t[q][:], y_ps[:, 0:BLOCK], ACT.Identity,
                                       bias=w[q][:, B2_COL:B2_COL + 1]).then_inc(y_ready, 1)
                run(act, step)

            @block.vector
            def _(dve):
                def step(s, u, r):
                    if exists(s):
                        dve.wait_ge(hidden_done[1], s + 1)
                        reach(dve, y_done, s - 2)
                        for c in range(HALF, FC):
                            dve.tensor_scalar(hidden[u][:, c, :], hidden_ps[1][:, c - HALF, :],
                                              w[u][:, B1_COL + c:B1_COL + c + 1], 0.0,
                                              ALU.add, ALU.max).then_inc(relu_ready[1], 1)
                    if exists(s - 2):
                        q = (u + 1) % U
                        dve.wait_ge(y_turned, s - 1)
                        if not known(s) or s - 2 >= U:
                            dve.wait_ge(rows_stored[q], 16 * (r - (1 if u < 2 else 0)))
                        dve.tensor_copy(rows_out[q][:].rearrange("p h d -> p (h d)"), rows_ps[:, 0:BLOCK]).then_inc(rows_ready, 1)
                run(dve, step)

            @block.tensor
            def _(pe):
                def step(s, u, r):
                    if exists(s + 1):
                        q = (u + 1) % U
                        pe.wait_ge(rows_loaded[q], 16 * (r + (u + 1) // U + 1))
                        reach(pe, x_ready, s + 1)
                        for h in range(HT):
                            ins = pe.transpose(x_ps[:, h * D:(h + 1) * D], rows_in[q][:, h, :], ident[:])
                        ins.then_inc(x_turned, 1)
                    if exists(s):
                        pe.wait_ge(weights_in[u], 16 * (r + 1))
                        pe.wait_ge(x_ready, s + 1)
                        for k in range(2):
                            reach(pe, relu_ready[k], HALF * s)
                            for c in range(HALF):
                                f = k * HALF + c
                                ins = pe.matmul(hidden_ps[k][:, c, :], w[u][:, f * D:(f + 1) * D], x_t[u][:],
                                                start=True, stop=True, skip_group_check=True)
                            ins.then_inc(hidden_done[k], 1)
                    if exists(s - 1):
                        q = (u + 2) % U
                        for k in range(2):
                            pe.wait_ge(relu_ready[k], HALF * s)
                        reach(pe, y_ready, s - 1)
                        for f in range(FC):
                            ins = pe.matmul(y_ps[:, 0:BLOCK], w[q][:, DFF + f * D:DFF + (f + 1) * D], hidden[q][:, f, :],
                                            start=(f == 0), stop=(f == FC - 1))
                        ins.then_inc(y_done, 1)
                    if exists(s - 2):
                        q = (u + 1) % U
                        pe.wait_ge(y_ready, s - 1)
                        reach(pe, rows_ready, s - 2)
                        for h in range(HT):
                            ins = pe.transpose(rows_ps[:, h * D:(h + 1) * D], y_t[q][:, h * D:(h + 1) * D], ident[:])
                        ins.then_inc(y_turned, 1)
                run(pe, step)


def combine(nc, dram, ident, xres, s_res, places):
    with ExitStack() as ctx:
        def sb(name, shape, dt=F32):
            return ctx.enter_context(nc.sbuf_tensor("o_" + name, shape, dt))

        def sem(name):
            return ctx.enter_context(nc.semaphore("o_" + name))

        U = 4
        answer = [sb(f"answer{u}", [D, TT, D]) for u in range(U)]
        out_sb = [sb(f"out_sb{u}", [D, TT, D]) for u in range(U)]
        th, silu2, mixed, result = ([sb(f"{n}{p}", [D, N]) for p in range(2)] for n in ("th", "silu2", "mixed", "result"))
        y_ps = [ctx.enter_context(nc.psum_tensor(f"o_y_ps{p}", [D, N], F32)) for p in range(2)]
        out_ps = [ctx.enter_context(nc.psum_tensor(f"o_out_ps{p}", [D, TT, D], F32)) for p in range(2)]

        gathered = [sem(f"gathered{u}") for u in range(U)]
        y_turned = sem("y_turned")
        tanh_ready = sem("tanh_ready")
        silu_ready = sem("silu_ready")
        mixed_ready = sem("mixed_ready")
        result_ready = sem("result_ready")
        result_turned = sem("result_turned")
        out_ready = sem("out_ready")
        out_stored = [sem(f"out_stored{u}") for u in range(U)]

        with nc.Block() as block:

            @block.gpsimd
            def _(pool):
                for s in range(B):
                    reach(pool, y_turned, s - U + 1)
                    for t in range(TT):
                        j = s * TT + t
                        pool.indirect_dma_start(answer[s % U][:, t, :], None, dram["answers"],
                                                bass.IndirectOffsetOnAxis(ap=places[:, j:j + 1], axis=0)
                                                ).then_inc(gathered[s % U], 16)

            @block.sync
            def _(sp):
                def step(s, u, r):
                    sp.wait_ge(out_ready, s + 1)
                    dst = (dram["out"][s] if known(s) else dram["out"][bass.ds(s, 1)].rearrange("o t d -> (o t) d"))
                    sp.dma_start(dst.rearrange("(t p) d -> p t d", p=D), out_sb[u][:]).then_inc(out_stored[u], 16)
                run_steps(sp, step, B, 0, U)
                for u in range(U):
                    sp.wait_ge(out_stored[u], 16 * (B // U))

            @block.scalar
            def _(act):
                act.preload_act_table_set("exp_and_others")

                def copy_out(s, u, r):
                    act.wait_ge(result_turned, s + 1)
                    if not known(s) or s >= U:
                        act.wait_ge(out_stored[u], 16 * r)
                    act.activation(out_sb[u][:], out_ps[u % 2][:], ACT.Copy).then_inc(out_ready, 1)

                def step(s, u, r):
                    act.wait_ge(y_turned, s + 1)
                    reach(act, silu_ready, s - 1)
                    act.activation(th[u % 2][:], y_ps[u % 2][:], ACT.Tanh, scale=0.5).then_inc(tanh_ready, 1)
                    if not (known(s) and s < 1):
                        copy_out(s - 1, (u + 3) % U, r - (1 if u == 0 else 0))
                run_steps(act, step, B, 0, U)
                copy_out(B - 1, U - 1, B // U - 1)

            @block.vector
            def _(dve):
                def step(s, u, r):
                    cols = columns(s)
                    p = u % 2
                    dve.wait_ge(tanh_ready, s + 1)
                    dve.scalar_tensor_tensor(out=silu2[p][:], in0=th[p][:], scalar=1.0, in1=y_ps[p][:],
                                             op0=ALU.add, op1=ALU.mult).then_inc(silu_ready, 1)
                    dve.wait_ge(silu_ready, s + 1)
                    dve.scalar_tensor_tensor(out=mixed[p][:], in0=silu2[p][:], scalar=0.5, in1=s_res[:, cols],
                                             op0=ALU.mult, op1=ALU.mult).then_inc(mixed_ready, 1)
                    dve.wait_ge(mixed_ready, s + 1)
                    reach(dve, result_turned, s - 1)
                    dve.tensor_tensor(result[p][:], mixed[p][:], xres[:, cols], ALU.add).then_inc(result_ready, 1)
                run_steps(dve, step, B, 0, U)

            @block.tensor
            def _(pe):
                def turn_back(s, p):
                    pe.wait_ge(result_ready, s + 1)
                    reach(pe, out_ready, s - 1)
                    for t in range(TT):
                        ins = pe.transpose(out_ps[p][:, t, :], result[p][:, t * D:(t + 1) * D], ident[:])
                    ins.then_inc(result_turned, 1)

                def step(s, u, r):
                    pe.wait_ge(gathered[u], 16 * TT * (r + 1))
                    reach(pe, silu_ready, s - 1)
                    for t in range(TT):
                        ins = pe.transpose(y_ps[u % 2][:, t * D:(t + 1) * D], answer[u][:, t, :], ident[:])
                    ins.then_inc(y_turned, 1)
                    if not (known(s) and s < 1):
                        turn_back(s - 1, (u + 1) % 2)
                run_steps(pe, step, B, 0, U)
                turn_back(B - 1, (B - 1) % 2)


def phase_experts(nc, dram, ident, xres, s_res, gate_logits):
    with ExitStack() as ctx:
        U32 = mybir.dt.uint32
        places = ctx.enter_context(nc.sbuf_tensor("places", [D, NT], U32))
        weight_rows = ctx.enter_context(nc.sbuf_tensor("weight_rows", [D, NBLOCK], U32))
        route_tokens(nc, dram, gate_logits, places, weight_rows)
        run_experts(nc, dram, ident, weight_rows)
        combine(nc, dram, ident, xres, s_res, places)


def routing_tables():
    f = np.float32
    earlier = (np.arange(D)[:, None] < np.arange(D)[None, :]).astype(f)
    restart = np.ones((D, EXPERTS, NT), f)
    restart[:, :, 0] = 0
    return {"rank": np.tile(np.arange(EXPERTS, 0, -1, dtype=f), (D, 1)),
            "triangle": np.stack([earlier, np.ones((D, D), f)], 1).astype(mybir.dt.np(BF16)),
            "restart": restart.reshape(D, -1),
            "block_number": np.tile(np.arange(NBLOCK, dtype=f), (D, 1)),
            "partition": np.arange(D, dtype=f)[:, None]}


def expert_rows(w1, b1, w2, b2):
    chunks = w2.reshape(EXPERTS, FC, D, D).transpose(0, 2, 1, 3).reshape(EXPERTS, D, DFF)
    return np.concatenate([w1, chunks, b1.reshape(EXPERTS, FC, D).transpose(0, 2, 1), b2[:, :, None],
                           np.zeros((EXPERTS, D, EXPERT_ROW - B2_COL - 1), w1.dtype)], 2).reshape(EXPERTS * D, EXPERT_ROW)


def build(nc, dram):
    with ExitStack() as ctx:
        def sb(name, shape, dt=F32):
            return ctx.enter_context(nc.sbuf_tensor(name, shape, dt))

        ident, centre, average = sb("ident", [D, D]), sb("centre", [D, D]), sb("average", [D, D])
        ident_bf = sb("ident_bf", [D, D], BF16)
        hid = sb("hid", [D, B * N])
        s_res = sb("s_res", [D, B * N])
        consts_in = ctx.enter_context(nc.semaphore("consts_in"))
        with nc.Block() as block:

            @block.sync
            def _(sp):
                for dst, name in ((ident, "ident"), (centre, "centre"), (average, "average"), (ident_bf, "ident_bf")):
                    sp.dma_start(dst[:], dram[name]).then_inc(consts_in, 16)
                sp.wait_ge(consts_in, 64)

        phase_mixer(nc, dram["x"], dram["A_w"], dram["A_vecs"], ident, hid, s_res, dram["sorted"])
        with ExitStack() as own:
            attend = local_attention(nc, own, sub(dram, "B_"), ident, ident_bf, hid)
            feed = feed_forward(nc, own, sub(dram, "B_"), centre, average, hid)
            with nc.Fori(0, DEPTH) as layer:
                attend(layer)
                feed(layer)
        phase_gate(nc, hid, s_res)
        gate_logits = sb("gate_logits", [D, NT * EXPERTS])
        phase_sparse_attention(nc, {**sub(dram, "C_"), "x": dram["x"], "tokens": dram["tokens"]}, ident, ident_bf,
                               centre, average, hid, s_res, gate_logits)
        phase_experts(nc, {**sub(dram, "D_"), **{k: dram[k] for k in ("out", "tokens", "sorted", "answers")}},
                      ident, hid, s_res, gate_logits)


def sub(dram, prefix):
    return {k[len(prefix):]: v for k, v in dram.items() if k.startswith(prefix)}


def kernel(**inputs):
    import concourse.bacc as _bacc
    from concourse.bass_utils import run_bass_kernel_spmd as _run

    a = {k: np.asarray(v) for k, v in inputs.items()}
    data = {"x": a["L0_attn_hidden_states"]}
    data["A_w"] = np.stack([a["L0_attn_" + k].T for k in ("Wk", "Wka", "Wv")], 1)
    data["A_vecs"] = np.stack([a["L0_attn_" + k] for k in ("gamma", "beta", "bk", "bka", "bv")], 1)
    for k in ("wqkv", "wo", "q_scale", "k_scale", "w1", "w2", "b1", "b2", "ln_g", "ln_b"):
        data["B_" + k] = a["L0_ffn_" + k]
    for k in ("Wq", "Wk", "Wv", "Wo"):
        data["C_" + k] = a["L1_attn_" + k].T
    for k in ("bq", "bk", "bv", "bo"):
        data["C_" + k] = a["L1_attn_" + k][:, None]
    data["C_gate_w"] = a["L1_ffn_gate_w"].T
    data["D_gate_b"], data["D_expert_bias"] = a["L1_ffn_gate_b"][None], a["L1_ffn_expert_bias"][None]
    data["D_weights"] = expert_rows(*(a["L1_ffn_" + k] for k in ("w1", "b1", "w2", "b2")))
    mean = np.full((D, D), 1.0 / D, np.float32)
    data["ident"], data["average"], data["centre"] = np.eye(D, dtype=np.float32), mean, np.eye(D, dtype=np.float32) - mean
    data["ident_bf"] = np.eye(D).astype(mybir.dt.np(BF16))
    data["B_rope_base"], data["B_window_mask"] = rope_base_table(), window_mask_table()
    data["C_counts"], data["C_pair_mask"] = pair_tables()
    data["C_rope1"] = rope1_table()
    data["C_same_head"] = np.kron(np.eye(H1), np.ones((DH1, DH1))).astype(np.float32)
    for k, table in routing_tables().items():
        data["D_" + k] = table

    nc = _bacc.Bacc("TRN2", target_bir_lowering=False, num_devices=1)
    arrays, dram = {}, {}
    for name, value in data.items():
        arrays[f"in_{name}"] = np.ascontiguousarray(value)
        dram[name] = nc.dram_tensor(f"in_{name}", value.shape, mybir.dt.from_np(value.dtype), kind="ExternalInput").ap()
    dram["C_ring"] = nc.dram_tensor("ring", (2, D, 3, RING), F32).ap()
    dram["C_back"] = nc.dram_tensor("back", (2, D, 2 * N), F32).ap()
    dram["tokens"] = nc.dram_tensor("tokens", (B, D, N), F32).ap()
    dram["sorted"] = nc.dram_tensor("sorted", (SORTED, D), F32).ap()
    dram["answers"] = nc.dram_tensor("answers", (SORTED, D), F32).ap()
    dram["out"] = nc.dram_tensor("out", (B, N, D), F32, kind="ExternalOutput").ap()
    build(nc, dram)
    return _run(nc, [arrays], core_ids=[0]).results[0]["out"]
```

```python
from contextlib import ExitStack

import numpy as np
import concourse.bass as bass
from concourse import mybir

DEPTH = 2
F32 = mybir.dt.float32
BF16 = mybir.dt.bfloat16
ALU = mybir.AluOpType
ACT = mybir.ActivationFunctionType
AX_X = mybir.AxisListType.X

D = 128
B, N = 16, 512
TT = N // D
CLEARING = 104
EPS = 1e-5
EXP_LN = "natural_log_exp_and_others"


def reach(eng, sem, count):
    if isinstance(count, (int, np.integer)) and count <= 0:
        return
    eng.wait_ge(sem, count)


def columns(i, width=N):
    return bass.ds(i * width, width)


def run_steps(eng, step, steps, lead, unroll, peel=1):
    for s in range(-lead, peel * unroll):
        step(s, s % unroll, s // unroll)
    with eng.Fori(peel, steps // unroll - 1) as r:
        for u in range(unroll):
            step(r * unroll + u, u, r)
    for u in range(unroll):
        step(steps - unroll + u, u, steps // unroll - 1)


def known(s):
    return isinstance(s, (int, np.integer))


def phase_mixer(nc, x_dram, weights, vectors, ident, hid, s_res, sorted_dram, prefetch):
    with ExitStack() as ctx:
        def sb(name, shape, dt=F32):
            return ctx.enter_context(nc.sbuf_tensor("a_" + name, shape, dt))

        def ps(name):
            return ctx.enter_context(nc.psum_tensor("a_" + name, [D, N], F32))

        sems = []

        def sem(name):
            sems.append(ctx.enter_context(nc.semaphore("a_" + name)))
            return sems[-1]

        x_in = [sb(f"x_in{p}", [D, TT, D]) for p in range(2)]
        xn = [sb(f"xn{p}", [D, TT, D]) for p in range(2)]
        hn = [sb(f"hn{p}", [D, TT, D]) for p in range(2)]
        stats = [sb(f"stats{k}", [D, TT, 6]) for k in range(2)]
        mean_var = [sb(f"mean_var{k}", [D, TT, 2]) for k in range(2)]
        var_eps = [sb(f"var_eps{k}", [D, TT]) for k in range(2)]
        ln_var = [sb(f"ln_var{k}", [D, TT]) for k in range(2)]
        rstd = [sb(f"rstd{k}", [D, TT]) for k in range(2)]
        h_t = [sb(f"h_t{p}", [D, N]) for p in range(2)]
        w_t = sb("w_t", [D, 3, D])
        vecs = sb("vecs", [D, 6])
        bka_scaled = sb("bka_scaled", [D, 1])
        ones = sb("ones", [D, N])
        cleared_rows = sorted_dram.shape[0] // B
        zeros = sb("zeros", [CLEARING, cleared_rows // CLEARING * D])
        carrier = sb("carrier", [D, 4])
        keys = [sb(f"keys{p}", [D, N]) for p in range(2)]
        kw = sb("kw", [D, N])
        kw_sum = sb("kw_sum", [D, N])
        kw_ln, kw_inv = sb("kw_ln", [D, N]), sb("kw_inv", [D, N])
        share = sb("share", [D, N])
        weighted = sb("weighted", [D, N])
        pooled = sb("pooled", [D, N])
        xn_ps, hn_ps, k_ps, ka_ps = (ps(n) for n in ("xn_ps", "hn_ps", "k_ps", "ka_ps"))
        v_ps = [ps(f"v_ps{p}") for p in range(2)]

        consts_in = sem("consts_in")
        consts_made = sem("consts_made")
        zeros_made = sem("zeros_made")
        rows_cleared = sem("rows_cleared")
        x_loaded = [sem(f"x_loaded{p}") for p in range(2)]
        bn_done = sem("bn_done")
        aggr_done = sem("aggr_done")
        var_ready = sem("var_ready")
        ln_ready = sem("ln_ready")
        rstd_ready = sem("rstd_ready")
        xn_ready = sem("xn_ready")
        hn_ready = sem("hn_ready")
        xn_turned = sem("xn_turned")
        hn_turned = sem("hn_turned")
        hid_ready = sem("hid_ready")
        h_ready = sem("h_ready")
        k_done = sem("k_done")
        v_done = sem("v_done")
        keys_ready = sem("keys_ready")
        ka_done = sem("ka_done")
        kw_ready = sem("kw_ready")
        sum_ready = sem("sum_ready")
        sum_ln_ready = sem("sum_ln_ready")
        inv_ready = sem("inv_ready")
        share_ready = sem("share_ready")
        weighted_ready = sem("weighted_ready")
        pooled_ready = sem("pooled_ready")
        s_ready = sem("s_ready")

        scale = 1.0 / np.sqrt(np.float32(D))
        GAMMA, BETA, BK, BKA, BV = range(5)

        def exists(s):
            return not known(s) or 0 <= s < B

        def run(eng, step):
            run_steps(eng, step, B, 1, 2)
            step(B, 0, B // 2)

        with nc.Block() as block:

            @block.sync
            def _(sp):
                sp.dma_start(w_t[:], weights).then_inc(consts_in, 16)
                sp.dma_start(vecs[:, 0:5], vectors).then_inc(consts_in, 16)

                def clear(s):
                    if known(s) and s < 0:
                        return
                    rows = (sorted_dram[s * cleared_rows:(s + 1) * cleared_rows].rearrange("(p k) d -> p (k d)", p=CLEARING)
                            if known(s) else
                            sorted_dram.rearrange("(s p k) d -> s p (k d)", s=B, p=CLEARING)[bass.ds(s, 1)]
                            .rearrange("o p n -> (o p) n"))
                    sp.dma_start(rows, zeros[:]).then_inc(rows_cleared, 16)

                def step(s, u, r):
                    if known(s) and s == 0:
                        sp.wait_ge(zeros_made, 1)
                    load(s, u)
                    clear(s)

                def load(s, u):
                    if known(s) and s + 1 >= B:
                        return
                    reach(sp, xn_ready, (s + 1 - 1) * TT)
                    sp.dma_start(x_in[(u + 1) % 2][:], x_dram[s + 1 if known(s) else bass.ds(s + 1, 1)]
                                 .rearrange("(t p) d -> p t d" if known(s) else "o (t p) d -> p (o t) d", p=D)
                                 ).then_inc(x_loaded[(u + 1) % 2], 16)
                run_steps(sp, step, B, 1, 2)
                prefetch(sp)
                sp.wait_ge(rows_cleared, 16 * B)

            @block.gpsimd
            def _(pool):
                pool.memset(ones[:], 1.0).then_inc(consts_made, 1)
                pool.memset(zeros[:], 0.0).then_inc(zeros_made, 1)

                def step(s, u, r):
                    if exists(s - 1):
                        pool.wait_ge(share_ready, s)
                        pool.wait_ge(keys_ready, s)
                        reach(pool, pooled_ready, s - 1)
                        pool.tensor_tensor(weighted[:], share[:], keys[(u + 1) % 2][:], ALU.mult).then_inc(weighted_ready, 1)
                run(pool, step)

            @block.scalar
            def _(act):
                act.preload_act_table_set(EXP_LN)
                act.wait_ge(consts_in, 32)
                act.mul(bka_scaled[:], vecs[:, BKA:BKA + 1], float(scale)).then_inc(consts_made, 1)
                act.wait_ge(consts_made, 2)

                def rstd_of(k, n):
                    act.wait_ge(var_ready, n)
                    act.activation(ln_var[k][:], var_eps[k][:], ACT.Ln).then_inc(ln_ready, 1)
                    act.wait_ge(ln_ready, n)
                    act.activation(rstd[k][:], ln_var[k][:], ACT.Exp, scale=-0.5).then_inc(rstd_ready, 1)

                def step(s, u, r):
                    main, ahead = exists(s), exists(s + 1)
                    if ahead:
                        rstd_of(0, 2 * s + 3)
                    if main:
                        act.wait_ge(k_done, s + 1)
                        reach(act, weighted_ready, s - 1)
                        act.activation(keys[u][:], k_ps[:], ACT.Identity,
                                       bias=vecs[:, BK:BK + 1]).then_inc(keys_ready, 1)
                        act.wait_ge(ka_done, s + 1)
                        reach(act, share_ready, s)
                        act.activation(kw[:], ka_ps[:], ACT.Exp, scale=float(scale),
                                       bias=bka_scaled[:]).then_inc(kw_ready, 1)
                    if ahead:
                        act.wait_ge(xn_turned, s + 2)
                        act.activation(hid[:, columns(s + 1)], xn_ps[:], ACT.Copy).then_inc(hid_ready, 1)
                        rstd_of(1, 2 * s + 4)
                    if main:
                        act.wait_ge(sum_ready, s + 1)
                        act.activation(kw_ln[:], kw_sum[:], ACT.Ln).then_inc(sum_ln_ready, 1)
                        act.wait_ge(sum_ln_ready, s + 1)
                        reach(act, share_ready, s)
                        act.activation(kw_inv[:], kw_ln[:], ACT.Exp, scale=-1.0).then_inc(inv_ready, 1)
                    if ahead:
                        act.wait_ge(hn_turned, s + 2)
                        reach(act, v_done, s)
                        act.activation(h_t[(u + 1) % 2][:], hn_ps[:], ACT.Identity,
                                       scale=vecs[:, GAMMA:GAMMA + 1],
                                       bias=vecs[:, BETA:BETA + 1]).then_inc(h_ready, 1)
                run(act, step)

            @block.tensor
            def _(pe):
                pe.wait_ge(consts_in, 32)

                def turn(out, src, done):
                    for t in range(TT):
                        ins = pe.transpose(out[:, t * D:(t + 1) * D], src[:, t, :], ident[:])
                    ins.then_inc(done, 1)

                def step(s, u, r):
                    main, ahead = exists(s), exists(s + 1)
                    if main:
                        pe.wait_ge(h_ready, s + 1)
                        reach(pe, keys_ready, s)
                        pe.matmul(k_ps[:], w_t[:, 0, :], h_t[u % 2][:], start=True, stop=True).then_inc(k_done, 1)
                        reach(pe, s_ready, s - 1)
                        pe.matmul(v_ps[u][:], w_t[:, 2, :], h_t[u % 2][:], start=True, stop=True).then_inc(v_done, 1)
                    if ahead:
                        pe.wait_ge(xn_ready, TT * (s + 2))
                        reach(pe, hid_ready, s + 1)
                        turn(xn_ps, xn[(u + 1) % 2], xn_turned)
                    if main:
                        pe.wait_ge(keys_ready, s + 1)
                        reach(pe, kw_ready, s)
                        pe.matmul(ka_ps[:], w_t[:, 1, :], keys[u][:], start=True, stop=True).then_inc(ka_done, 1)
                    if ahead:
                        pe.wait_ge(hn_ready, TT * (s + 2))
                        reach(pe, h_ready, s + 1)
                        turn(hn_ps, hn[(u + 1) % 2], hn_turned)
                run(pe, step)

            @block.vector
            def _(dve):
                dve.wait_ge(consts_made, 2)

                def variance(k, src, s):
                    n = 2 * s + 3 + k
                    for t in range(TT):
                        dve.bn_stats(stats[k][:, t, :], src[:, t, :]).then_inc(bn_done, 1)
                    dve.wait_ge(bn_done, TT * n)
                    reach(dve, (xn_ready, hn_ready)[k], TT * (s + 1))
                    dve.memset(carrier[:, 2 * k:2 * k + 1], 0.0)
                    for t in range(TT):
                        dve.bn_aggr(mean_var[k][:, t, :], stats[k][:, t, :]).then_inc(aggr_done, 1)
                    dve.wait_ge(aggr_done, TT * n)
                    dve.tensor_scalar(var_eps[k][:], mean_var[k][:, :, 1], EPS, None, ALU.add).then_inc(var_ready, 1)

                def normalise(k, dst, src, n, ready):
                    dve.wait_ge(rstd_ready, n)
                    for t in range(TT):
                        dve.tensor_scalar(dst[:, t, :], src[:, t, :], mean_var[k][:, t, 0:1], rstd[k][:, t:t + 1],
                                          ALU.subtract, ALU.mult).then_inc(ready, 1)

                def step(s, u, r):
                    main, ahead, late = exists(s), exists(s + 1), exists(s - 1)
                    q = (u + 1) % 2
                    if ahead:
                        dve.wait_ge(x_loaded[q], 16 * (r + (u + 1) // 2 + 1))
                        variance(0, x_in[q], s)
                    if late:
                        dve.wait_ge(inv_ready, s)
                        reach(dve, weighted_ready, s - 1)
                        dve.tensor_tensor(share[:], kw[:], kw_inv[:], ALU.mult).then_inc(share_ready, 1)
                    if ahead:
                        reach(dve, xn_turned, s)
                        normalise(0, xn[q], x_in[q], 2 * s + 3, xn_ready)
                        dve.wait_ge(xn_ready, TT * (s + 2))
                        variance(1, xn[q], s)
                    if main:
                        dve.wait_ge(kw_ready, s + 1)
                        reach(dve, sum_ln_ready, s)
                        dve.tensor_tensor_scan(kw_sum[:], ones[:], kw[:], 0.0, ALU.mult, ALU.add).then_inc(sum_ready, 1)
                    if ahead:
                        reach(dve, hn_turned, s)
                        normalise(1, hn[q], xn[q], 2 * s + 4, hn_ready)
                    if late:
                        dve.wait_ge(weighted_ready, s)
                        reach(dve, s_ready, s - 1)
                        dve.tensor_tensor_scan(pooled[:], ones[:], weighted[:], 0.0, ALU.mult, ALU.add).then_inc(pooled_ready, 1)
                        dve.wait_ge(pooled_ready, s)
                        dve.wait_ge(v_done, s)
                        dve.scalar_tensor_tensor(out=s_res[:, columns(s - 1)], in0=v_ps[q][:], scalar=vecs[:, BV:BV + 1],
                                                 in1=pooled[:], op0=ALU.add, op1=ALU.mult).then_inc(s_ready, 1)
                run(dve, step)

        with nc.Block() as block:

            @block.gpsimd
            def _(pool):
                for used in sems:
                    pool.sem_clear(used)


HEADS, DH = 8, 64
WIN = 64
INNER = HEADS * DH
NT = B * TT
PAIR = HEADS // 2


def run_tiles(eng, step, lead, lag):
    for s in range(-lead, TT):
        step(s, s % TT)
    with eng.Fori(1, B - 1) as seq:
        for u in range(TT):
            step(seq * TT + u, u)
    for s in range(NT - TT, NT + lag):
        step(s, s % TT)


def inside(t):
    return not known(t) or 0 <= t < NT


def local_attention(nc, own, dram, ident, ident_bf, hid):
    def sb(name, shape, dt=F32):
        return own.enter_context(nc.sbuf_tensor("b_" + name, shape, dt))

    def sem(name):
        return own.enter_context(nc.semaphore("b_" + name))

    wqkv = sb("wqkv", [D, 3 * INNER])
    wo = sb("wo", [D, INNER // D, D])
    scales = sb("scales", [D, 4, DH])
    rope_base = sb("rope_base", [D, 4, TT, DH])
    rope = sb("rope", [D, 4, TT, DH])
    mask = sb("mask", [D, 2, PAIR, D], BF16)
    shift = [sb(f"shift{u}", [D, D]) for u in range(TT)]
    squares = [sb(f"squares{k}", [D, HEADS, DH]) for k in range(2)]
    norm2 = sb("norm2", [D, 2, HEADS])
    norm2_clip = sb("norm2_clip", [D, 2, HEADS])
    norm_ln = sb("norm_ln", [D, 2, HEADS])
    norm_inv = sb("norm_inv", [D, 2, HEADS])
    half_log = sb("half_log", [D, 1])
    by_cos = [sb(f"by_cos{k}", [D, HEADS, DH]) for k in range(2)]
    by_sin = [sb(f"by_sin{k}", [D, HEADS, DH]) for k in range(2)]
    rope_sum = [sb(f"rope_sum{k}", [D, HEADS, DH]) for k in range(2)]
    roped = [sb(f"roped{k}", [D, INNER]) for k in range(2)]
    q_t = sb("q_t", [D, PAIR, D])
    k_t = [sb(f"k_t{u}", [D, PAIR, D]) for u in range(TT)]
    v_odd = [sb(f"v_odd{u}", [D, HEADS, DH + 1]) for u in range(TT)]
    v_even = [sb(f"v_even{u}", [D, HEADS, DH + 1]) for u in range(TT)]
    neg_max = sb("neg_max", [D, 2, PAIR])
    logits = [sb(f"logits{p}", [D, PAIR, D]) for p in range(2)]
    probs = [sb(f"probs{p}", [D, PAIR, D]) for p in range(2)]
    sum_inv = sb("sum_inv", [D, 2, PAIR])
    heads_out = sb("heads_out", [D, HEADS, DH])
    o_t = sb("o_t", [D, INNER // D, D])

    weights_in = sem("weights_in")
    fixed_in = sem("fixed_in")
    tables_ready = sem("tables_ready")
    shifted = sem("shifted")
    proj_done = [sem(f"{x}_done") for x in "qkv"]
    squared = [sem(f"{x}_squared") for x in "qk"]
    products = sem("rope_products")
    sums = sem("rope_sums")
    norms_summed = sem("norms_summed")
    norms_clipped = sem("norms_clipped")
    norms_ln = sem("norms_ln")
    norms_ready = sem("norms_ready")
    roped_ready = sem("roped_ready")
    turned = [sem(f"{x}_turned") for x in "qko"]
    turned_out = [sem(f"{x}_t_ready") for x in "qko"]
    v_ready = sem("v_ready")
    scores_done = sem("scores_done")
    max_ready = sem("max_ready")
    logits_ready = sem("logits_ready")
    logits_turned = sem("logits_turned")
    probs_ready = sem("probs_ready")
    weighed = sem("weighed")
    sum_inv_ready = sem("sum_inv_ready")
    heads_ready = sem("heads_ready")
    y_done = sem("y_done")
    x_updated = sem("x_updated")

    LIFT = 2.0 ** 30

    with nc.Block() as block:

        @block.vector
        def _(dve):
            for u in range(TT):
                for v in (v_odd, v_even):
                    dve.memset(v[u][:, :, DH:DH + 1], 1.0)
            dve.memset(half_log[:], float(0.5 * np.log(LIFT)))
            dve.memset(shift[0][DH:D, 0:1], 0.0)

    def load_weights(sp, layer):
        if known(layer):
            sp.dma_start(rope_base[:], dram["rope_base"]).then_inc(fixed_in, 16)
            sp.dma_start(mask[:], dram["window_mask"]).then_inc(fixed_in, 16)
        one = slice(layer, layer + 1) if known(layer) else bass.ds(layer, 1)
        sp.dma_start(wqkv[:], dram["wqkv"][one].rearrange("l p n -> p (l n)")).then_inc(weights_in, 16)
        sp.dma_start(wo[:], dram["wo"][one].rearrange("l (c p) n -> p (l c) n", p=D)).then_inc(weights_in, 16)
        for k, name in enumerate(("q_scale", "k_scale")):
            row = dram[name][one]
            sp.dma_start(scales[:, 2 * k, :], row.to_broadcast([D, DH])).then_inc(weights_in, 16)
            for a, b in ((0, DH // 2), (DH // 2, 0)):
                sp.dma_start(scales[:, 2 * k + 1, a:a + DH // 2],
                             row[:, b:b + DH // 2].to_broadcast([D, DH // 2])).then_inc(weights_in, 16)

    def weights_loaded(eng, layers):
        eng.wait_ge(fixed_in, 32)
        eng.wait_ge(weights_in, layers * 128)

    def phase(layer, prefetch):
        def wait(eng, semaphore, tiles, per=1, more=0):
            if known(tiles) and tiles * per + more <= 0:
                return
            eng.wait_ge(semaphore, layer * (NT * per) + tiles * per + more)

        with ExitStack() as ctx:
            def ps(name, shape):
                return ctx.enter_context(nc.psum_tensor("b_" + name, shape, F32))

            qk_ps = [ps("q_ps", [D, HEADS, DH]), ps("k_ps", [D, HEADS, DH])]
            v_ps = ps("v_ps", [D, HEADS, DH])
            turn_ps = ps("turn_ps", [D, PAIR, D])
            score_ps = [ps(f"score_ps{p}", [D, PAIR, D]) for p in range(2)]
            probs_ps = ps("probs_ps", [D, PAIR, D])
            out_ps = ps("out_ps", [D, 512])
            weighed_ps = out_ps[:, 0:PAIR * (DH + 1)].rearrange("p (h d) -> p h d", h=PAIR)
            y_ps = out_ps[:, 512 - D:512]

            with nc.Block() as block:

                @block.sync
                def _(sp):
                    prefetch(sp, layer)

                @block.gpsimd
                def _(pool):
                    def step(s, u):
                        w = (u + 3) % TT
                        if inside(s + 2):
                            for k in range(2):
                                wait(pool, products, s + 2, 6, 3 * k + 3)
                                wait(pool, roped_ready, s + 1, 2, k + 1)
                                pool.tensor_tensor(rope_sum[k][:], by_cos[k][:], by_sin[k][:], ALU.add).then_inc(sums, 1)
                            for k in range(2):
                                wait(pool, norms_ready, s + 3)
                                wait(pool, sums, s + 2, 2, k + 1)
                                wait(pool, turned[k], s + 2)
                                pool.tensor_tensor(roped[k][:].rearrange("p (h d) -> p h d", h=HEADS), rope_sum[k][:],
                                                   norm_inv[:, k, :].unsqueeze(2).to_broadcast([D, HEADS, DH]),
                                                   ALU.mult).then_inc(roped_ready, 1)
                    run_tiles(pool, step, 2, 0)

                @block.scalar
                def _(act):
                    act.preload_act_table_set(EXP_LN)

                    def turn_out(i, dst, t):
                        wait(act, turned[i], t + 1)
                        act.activation(dst[:], turn_ps[:], ACT.Copy).then_inc(turned_out[i], 1)

                    def square(k, t):
                        wait(act, proj_done[k], t + 1)
                        wait(act, norms_summed, t, 2)
                        act.activation(squares[k][:], qk_ps[k][:], ACT.Square).then_inc(squared[k], 1)

                    def exponentials(p, t):
                        wait(act, logits_turned, t, 2, p + 1)
                        wait(act, weighed, t - 1, 2, p + 1)
                        act.activation(probs[p][:], probs_ps[:], ACT.Exp).then_inc(probs_ready, 1)

                    def shift_tokens(t, w):
                        wait(act, proj_done[2], t - 3)
                        act.activation(shift[w][0:DH, :], hid[0:DH, columns(t, D)], ACT.Copy).then_inc(shifted, 1)
                        a = 1 if w == 0 else 0
                        act.activation(shift[w][DH:D, a:D], hid[DH:D, bass.ds(t * D - 1 + a, D - a)],
                                       ACT.Copy).then_inc(shifted, 1)

                    def step(s, u):
                        if inside(s - 1):
                            wait(act, y_done, s - 1)
                            turn_out(2, o_t, s - 1)
                        if inside(s):
                            exponentials(0, s)
                        if inside(s + 3):
                            shift_tokens(s + 3, (u + 3) % TT)
                        if inside(s + 1):
                            wait(act, scores_done, s + 1, 2)
                            turn_out(0, q_t, s + 1)
                            w = (u + 1) % TT
                            wait(act, proj_done[2], s + 2)
                            wait(act, weighed, s, 2)
                            act.activation(v_odd[w][:, :, 0:DH], v_ps[:], ACT.Copy).then_inc(v_ready, 1)
                            turn_out(1, k_t[w], s + 1)
                        if inside(s):
                            exponentials(1, s)
                        if inside(s + 1):
                            w = (u + 1) % TT
                            act.activation(v_even[w][0:WIN, :, 0:DH], v_ps[0:WIN], ACT.Copy).then_inc(v_ready, 1)
                            act.activation(v_even[(w + 1) % TT][WIN:D, :, 0:DH], v_ps[WIN:D], ACT.Copy).then_inc(v_ready, 1)
                        if inside(s + 2):
                            wait(act, norms_clipped, s + 3)
                            act.activation(norm_ln[:], norm2_clip[:], ACT.Ln, scale=LIFT).then_inc(norms_ln, 1)
                            wait(act, norms_ln, s + 3)
                            wait(act, roped_ready, s + 2, 2)
                            act.activation(norm_inv[:], norm_ln[:], ACT.Exp, scale=-0.5, bias=half_log[:]).then_inc(norms_ready, 1)
                        if inside(s + 3):
                            square(0, s + 3)
                            square(1, s + 3)
                    run_tiles(act, step, 3, 1)

                @block.tensor
                def _(pe):
                    weights_loaded(pe, layer + 1)

                    def project(i, t, w, out):
                        wait(pe, shifted, t + 1, 2)
                        pe.matmul(out, shift[w][:], wqkv[:, i * INNER:(i + 1) * INNER],
                                  start=True, stop=True).then_inc(proj_done[i], 1)

                    def turn(i, src, t):
                        for c in range(PAIR):
                            ins = pe.transpose(turn_ps[:, c, :], src[:, c * D:(c + 1) * D], ident[:])
                        ins.then_inc(turned[i], 1)

                    def turn_logits(p, t):
                        wait(pe, logits_ready, t, 2, p + 1)
                        wait(pe, probs_ready, t, 2, p)
                        for h in range(PAIR):
                            ins = pe.transpose(probs_ps[:, h, :], logits[p][:, h, :], ident[:])
                        ins.then_inc(logits_turned, 1)

                    def scores(t, w):
                        wait(pe, turned_out[0], t + 1)
                        wait(pe, turned_out[1], t + 1)
                        for p in range(2):
                            wait(pe, logits_ready, t - 1, 2, p + 1)
                            pe.matmul(score_ps[p][:], ident_bf[:], mask[:, 0 if w == 0 else 1],
                                      start=True, stop=False, skip_group_check=True)
                        for h in range(PAIR):
                            for p in range(2):
                                rows = slice(p * DH, (p + 1) * DH)
                                pe.matmul(score_ps[p][0:WIN, h, 0:WIN], q_t[rows, h, 0:WIN], k_t[w][rows, h, 0:WIN],
                                          start=False, stop=True, skip_group_check=True)
                                if w > 0:
                                    pe.matmul(score_ps[p][0:WIN, h, WIN:D], q_t[rows, h, 0:WIN],
                                              k_t[w - 1][rows, h, WIN:D], start=False, stop=True, skip_group_check=True)
                                ins = pe.matmul(score_ps[p][WIN:D, h, :], q_t[rows, h, WIN:D], k_t[w][rows, h, :],
                                                start=False, stop=True, skip_group_check=True)
                                if h == PAIR - 1:
                                    ins.then_inc(scores_done, 1)

                    def weigh(p, t, w):
                        wait(pe, probs_ready, t, 2, p + 1)
                        wait(pe, v_ready, t + 1, 3)
                        if p == 0:
                            wait(pe, x_updated, t)
                        wait(pe, heads_ready, t, 2, p)
                        keys = D if w > 0 else WIN
                        for h in range(PAIR):
                            pe.matmul(weighed_ps[WIN:D, h, :], probs[p][:, h, WIN:D], v_odd[w][:, 2 * h + p, :],
                                      start=True, stop=True, skip_group_check=True)
                            ins = pe.matmul(weighed_ps[0:WIN, h, :], probs[p][0:keys, h, 0:WIN],
                                            v_even[w][0:keys, 2 * h + p, :], start=True, stop=True, skip_group_check=True)
                        ins.then_inc(weighed, 1)

                    def step(s, u):
                        w1, w2, w3 = (u + 1) % TT, (u + 2) % TT, (u + 3) % TT
                        if inside(s - 1):
                            wait(pe, heads_ready, s, 2)
                            wait(pe, turned_out[1], s + 1 if inside(s) else s)
                            turn(2, heads_out[:].rearrange("p h d -> p (h d)"), s - 1)
                        if inside(s):
                            turn_logits(0, s)
                        if inside(s + 1):
                            wait(pe, roped_ready, s + 1, 2, 1)
                            wait(pe, turned_out[2], s)
                            turn(0, roped[0], s + 1)
                        if inside(s - 1):
                            wait(pe, turned_out[2], s)
                            wait(pe, heads_ready, s, 2)
                            for c in range(INNER // D):
                                ins = pe.matmul(y_ps, wo[:, c, :], o_t[:, c, :], start=(c == 0), stop=(c == INNER // D - 1))
                            ins.then_inc(y_done, 1)
                        if inside(s + 1):
                            wait(pe, roped_ready, s + 2, 2)
                            wait(pe, turned_out[0], s + 2)
                            turn(1, roped[1], s + 1)
                        if inside(s):
                            turn_logits(1, s)
                            weigh(0, s, u)
                        if inside(s + 1):
                            scores(s + 1, w1)
                        if inside(s):
                            weigh(1, s, u)
                        if inside(s + 3):
                            wait(pe, products, s + 2, 6, 3)
                            project(0, s + 3, w3, qk_ps[0][:])
                            wait(pe, products, s + 3, 6)
                            project(1, s + 3, w3, qk_ps[1][:])
                        if inside(s + 2):
                            wait(pe, v_ready, s + 2, 3)
                            project(2, s + 2, w2, v_ps[:])
                    run_tiles(pe, step, 3, 1)

                @block.vector
                def _(dve):
                    weights_loaded(dve, layer + 1)
                    for k in range(4):
                        dve.tensor_tensor(rope[:, k], rope_base[:, k],
                                          scales[:, k:k + 1, :].to_broadcast([D, TT, DH]), ALU.mult).then_inc(tables_ready, 1)
                    dve.wait_ge(tables_ready, layer * 4 + 4)

                    half = DH // 2

                    def rotate(k, t, w):
                        wait(dve, squared[k], t + 1)
                        wait(dve, sums, t - 1, 2, k + 1)
                        cos = rope[:, 2 * k, w:w + 1, :]
                        sin = rope[:, 2 * k + 1, w:w + 1, :]
                        dve.tensor_tensor(by_cos[k][:], qk_ps[k][:], cos.to_broadcast([D, HEADS, DH]),
                                          ALU.mult).then_inc(products, 1)
                        for a, b in ((0, half), (half, 0)):
                            dve.tensor_tensor(by_sin[k][:, :, a:a + half], qk_ps[k][:, :, b:b + half],
                                              sin[:, :, a:a + half].to_broadcast([D, HEADS, half]),
                                              ALU.mult).then_inc(products, 1)
                        wait(dve, norms_clipped, t)
                        dve.tensor_reduce(norm2[:, k, :], squares[k][:], AX_X, ALU.add).then_inc(norms_summed, 1)

                    def subtract_max(p, t):
                        wait(dve, scores_done, t, 2, p + 1)
                        dve.tensor_reduce(neg_max[:, p, :], score_ps[p][:], AX_X, ALU.max, negate=True).then_inc(max_ready, 1)
                        wait(dve, max_ready, t, 2, p + 1)
                        wait(dve, logits_turned, t - 1, 2, p + 1)
                        dve.tensor_tensor(logits[p][:], score_ps[p][:],
                                          neg_max[:, p, :].unsqueeze(2).to_broadcast([D, PAIR, D]),
                                          ALU.add).then_inc(logits_ready, 1)

                    def normalise(p, t):
                        wait(dve, weighed, t, 2, p + 1)
                        dve.reciprocal(sum_inv[:, p, :], weighed_ps[:, :, DH]).then_inc(sum_inv_ready, 1)
                        wait(dve, sum_inv_ready, t, 2, p + 1)
                        wait(dve, turned[2], t)
                        dve.tensor_tensor(heads_out[:, p::2, :], weighed_ps[:, :, 0:DH],
                                          sum_inv[:, p, :].unsqueeze(2).to_broadcast([D, PAIR, DH]),
                                          ALU.mult).then_inc(heads_ready, 1)

                    def step(s, u):
                        w1, w2 = (u + 1) % TT, (u + 2) % TT
                        if inside(s + 2):
                            rotate(0, s + 2, w2)
                        if inside(s - 1):
                            wait(dve, y_done, s)
                            wait(dve, shifted, s + 1 if inside(s) else s, 2)
                            x = hid[:, columns(s - 1, D)]
                            dve.tensor_tensor(x, y_ps, x, ALU.add).then_inc(x_updated, 1)
                        if inside(s + 2):
                            rotate(1, s + 2, w2)
                            wait(dve, norms_summed, s + 3, 2)
                            wait(dve, norms_ln, s + 2)
                            dve.tensor_scalar(norm2_clip[:], norm2[:], 1e-24, None, ALU.max).then_inc(norms_clipped, 1)
                        if inside(s):
                            normalise(0, s)
                        if inside(s + 1):
                            subtract_max(0, s + 1)
                            subtract_max(1, s + 1)
                        if inside(s):
                            normalise(1, s)
                    run_tiles(dve, step, 3, 1)
    return phase, load_weights, weights_loaded


def rope_base_table():
    f = np.float32
    half = np.arange(0, DH, 2, dtype=f)
    inv_freq = (f(1.0) / f(10000.0) ** (half / f(DH))).astype(f)
    t = np.arange(N, dtype=f)
    freqs = t[:, None] * inv_freq[None, :]
    freqs = np.concatenate([freqs, freqs], -1)
    base = (half + f(0.4 * DH)) / f(1.4 * DH)
    power = (t - f(N // 2)) / f(WIN // 2)
    scale = (base[None, :] ** power[:, None]).astype(f)
    scale = np.concatenate([scale, scale], -1)
    sign = np.where(np.arange(DH) < DH // 2, f(-1), f(1))
    cos, sin = np.cos(freqs), np.sin(freqs) * sign
    kinds = np.stack([cos * scale * f(8), sin * scale * f(8), cos / scale, sin / scale], 0)
    return np.ascontiguousarray(kinds.reshape(4, TT, D, DH).transpose(2, 0, 1, 3).astype(f))


def window_mask_table():
    i, j = np.arange(WIN)[:, None], np.arange(WIN)[None, :]
    own, prev = j <= i, j >= i
    never = np.zeros_like(own)
    out = np.stack([np.block([[own, never], [prev, own]]), np.block([[own, prev], [prev, own]])], 0)
    out = np.where(out, 0.0, -1e30).astype(mybir.dt.np(BF16))
    return np.ascontiguousarray(np.repeat(out.transpose(1, 0, 2)[:, :, None, :], PAIR, 2))


HID = 341
CHUNKS = [(a, min(D, HID - a)) for a in range(0, HID, D)]


def feed_forward(nc, own, dram, centre, average, hid):
    def sb(name, shape, dt=F32):
        return own.enter_context(nc.sbuf_tensor("f_" + name, shape, dt))

    def sem(name):
        return own.enter_context(nc.semaphore("f_" + name))

    nch = len(CHUNKS)
    w1 = sb("w1", [D, 2 * HID])
    w2 = sb("w2", [D, nch, D])
    b1 = sb("b1", [D, 2, nch])
    vecs = sb("vecs", [D, 3])
    eps = sb("eps", [D, 1])
    LG, LB, B2 = range(3)
    shift = [sb(f"shift{p}", [D, N]) for p in range(2)]
    squares = sb("squares", [D, N])
    ln_var = sb("ln_var", [D, N])
    rstd = sb("rstd", [D, N])
    unit = sb("unit", [D, N])
    h = [sb(f"h{p}", [D, N]) for p in range(2)]
    gate = [sb(f"gate{p}", [D, N]) for p in range(2)]
    gated = [sb(f"gated{c}", [D, N]) for c in range(nch)]

    weights_in = sem("weights_in")
    shifted = sem("shifted")
    centred = sem("centred")
    squared = sem("squared")
    var_done = sem("var_done")
    ln_ready = sem("ln_ready")
    rstd_ready = sem("rstd_ready")
    unit_ready = sem("unit_ready")
    h_ready = sem("h_ready")
    a_done = sem("a_done")
    g_done = sem("g_done")
    gate_ready = sem("gate_ready")
    gated_ready = sem("gated_ready")
    y_done = sem("y_done")
    x_updated = sem("x_updated")
    ALL_WEIGHTS = 16 * (1 + 3 * nch + 3)

    half = D // 2

    with nc.Block() as block:

        @block.vector
        def _(dve):
            dve.memset(eps[:], EPS)
            for p in range(2):
                dve.memset(shift[p][half:D, 0:1], 0.0)

    def load_weights(sp, layer):
        one = bass.ds(layer, 1)
        sp.dma_start(w1[:], dram["w1"][one].rearrange("l p n -> p (l n)")).then_inc(weights_in, 16)
        for c, (a, n) in enumerate(CHUNKS):
            sp.dma_start(w2[0:n, c, :], dram["w2"][one, a:a + n, :].rearrange("l p n -> p (l n)")).then_inc(weights_in, 16)
            for k in range(2):
                sp.dma_start(b1[0:n, k, c:c + 1], dram["b1"][one, k * HID + a:k * HID + a + n]
                             .rearrange("l p -> p l")).then_inc(weights_in, 16)
        for k, name in enumerate(("ln_g", "ln_b", "b2")):
            sp.dma_start(vecs[:, k:k + 1], dram[name][one].rearrange("l p -> p l")).then_inc(weights_in, 16)

    def phase(layer, prefetch, prefetched):
        def wait(eng, semaphore, seqs, per=1, more=0):
            if known(seqs) and seqs * per + more <= 0:
                return
            eng.wait_ge(semaphore, layer * (B * per) + seqs * per + more)

        with ExitStack() as ctx:
            def ps(name):
                return ctx.enter_context(nc.psum_tensor("f_" + name, [D, N], F32))

            centred_ps, var_ps, y_ps = ps("centred_ps"), ps("var_ps"), ps("y_ps")
            a_ps = [ps(f"a_ps{p}") for p in range(2)]
            g_ps = [ps(f"g_ps{p}") for p in range(2)]

            with nc.Block() as block:

                @block.sync
                def _(sp):
                    prefetch(sp, layer)

                @block.gpsimd
                def _(pool):
                    prefetched(pool, layer + 2)

                @block.scalar
                def _(act):
                    act.preload_act_table_set(EXP_LN)
                    act.wait_ge(weights_in, (layer + 1) * ALL_WEIGHTS)

                    def shift_tokens(s, w):
                        wait(act, centred, s - 1)
                        act.activation(w[0:half, :], hid[0:half, columns(s)], ACT.Copy).then_inc(shifted, 1)
                        act.activation(w[half:D, 1:N], hid[half:D, bass.ds(s * N, N - 1)], ACT.Copy).then_inc(shifted, 1)

                    def step(s, u, r):
                        main = not (known(s) and s < 0)
                        ahead = not (known(s) and s + 2 >= B)

                        def gelu(c):
                            q, n = (nch * u + c) % 2, CHUNKS[c][1]
                            wait(act, g_done, s, nch, c + 1)
                            wait(act, gated_ready, s, nch, c - 1)
                            act.activation(gate[q][0:n], g_ps[q][0:n], ACT.Gelu, bias=b1[0:n, 1, c:c + 1]).then_inc(gate_ready, 1)
                        if ahead:
                            shift_tokens(s + 2, shift[u])
                        if main:
                            gelu(0)
                        if ahead:
                            wait(act, centred, s + 3)
                            wait(act, var_done, s + 2)
                            act.activation(squares[:], centred_ps[:], ACT.Square).then_inc(squared, 1)
                        if main:
                            gelu(1)
                            gelu(2)
                        if ahead:
                            act.preload_act_table_set(EXP_LN)
                            wait(act, var_done, s + 3)
                            act.activation(ln_var[:], var_ps[:], ACT.Ln, bias=eps[:]).then_inc(ln_ready, 1)
                            wait(act, ln_ready, s + 3)
                            wait(act, unit_ready, s + 2)
                            act.activation(rstd[:], ln_var[:], ACT.Exp, scale=-0.5).then_inc(rstd_ready, 1)
                    run_steps(act, step, B, 2, 2)

                @block.tensor
                def _(pe):
                    pe.wait_ge(weights_in, (layer + 1) * ALL_WEIGHTS)

                    def step(s, u, r):
                        main = not (known(s) and s < 0)
                        ahead = not (known(s) and s + 2 >= B)

                        def widen(c):
                            (a, n), q = CHUNKS[c], (nch * u + c) % 2
                            wait(pe, h_ready, s + 1)
                            wait(pe, gate_ready, s, nch, c - 1)
                            pe.matmul(g_ps[q][0:n], w1[:, HID + a:HID + a + n], h[u % 2][:], start=True, stop=True).then_inc(g_done, 1)
                            wait(pe, gated_ready, s, nch, c - 1)
                            pe.matmul(a_ps[q][0:n], w1[:, a:a + n], h[u % 2][:], start=True, stop=True).then_inc(a_done, 1)

                        if main:
                            widen(0)
                        if ahead:
                            wait(pe, shifted, s + 3, 2)
                            wait(pe, unit_ready, s + 2)
                            pe.matmul(centred_ps[:], centre[:], shift[u][:], start=True, stop=True).then_inc(centred, 1)
                        if main:
                            widen(1)
                        if ahead:
                            wait(pe, squared, s + 3)
                            wait(pe, ln_ready, s + 2)
                            pe.matmul(var_ps[:], average[:], squares[:], start=True, stop=True).then_inc(var_done, 1)
                        if main:
                            widen(2)
                            wait(pe, x_updated, s)
                            for c, (a, n) in enumerate(CHUNKS):
                                wait(pe, gated_ready, s, nch, c + 1)
                                ins = pe.matmul(y_ps[:], w2[0:n, c, :], gated[c][0:n], start=(c == 0), stop=(c == nch - 1))
                            ins.then_inc(y_done, 1)
                    run_steps(pe, step, B, 2, 2)

                @block.vector
                def _(dve):
                    dve.wait_ge(weights_in, (layer + 1) * ALL_WEIGHTS)

                    def step(s, u, r):
                        main = not (known(s) and s < 0)
                        ahead = not (known(s) and s + 2 >= B)

                        def apply_gate(c):
                            q, n = (nch * u + c) % 2, CHUNKS[c][1]
                            wait(dve, gate_ready, s, nch, c + 1)
                            wait(dve, a_done, s, nch, c + 1)
                            wait(dve, y_done, s)
                            dve.scalar_tensor_tensor(out=gated[c][0:n], in0=a_ps[q][0:n], scalar=b1[0:n, 0, c:c + 1],
                                                     in1=gate[q][0:n], op0=ALU.add, op1=ALU.mult).then_inc(gated_ready, 1)
                        if main:
                            for c in range(nch):
                                apply_gate(c)
                        if main:
                            wait(dve, y_done, s + 1)
                            x = hid[:, columns(s)]
                            dve.scalar_tensor_tensor(out=x, in0=y_ps[:], scalar=vecs[:, B2:B2 + 1], in1=x,
                                                     op0=ALU.add, op1=ALU.add).then_inc(x_updated, 1)
                        if ahead:
                            wait(dve, rstd_ready, s + 3)
                            wait(dve, h_ready, s + 2)
                            dve.tensor_tensor(unit[:], centred_ps[:], rstd[:], ALU.mult).then_inc(unit_ready, 1)
                            wait(dve, unit_ready, s + 3)
                            wait(dve, a_done, s + 1, nch)
                            dve.tensor_scalar(h[u][:], unit[:], vecs[:, LG:LG + 1], vecs[:, LB:LB + 1],
                                              ALU.mult, ALU.add).then_inc(h_ready, 1)
                    run_steps(dve, step, B, 2, 2)
    return phase, load_weights


EXPERTS = 8
H1, DH1 = 16, 8
LEVELS = int(np.log2(N))
HALO = 3 * N // 4
SKEW = H1
RING = 2 * N + SKEW
NSLOT = [min(3, N // 2 ** x - 1) for x in range(LEVELS)]
NCOL = [N // 2 ** x for x in range(LEVELS)]
SLOTS = 3
LEVEL = [sum(NCOL[:x]) for x in range(LEVELS + 1)]
LEVEL_COLS = LEVEL[-1]
PADS = N + SLOTS * LEVEL_COLS
NPAIR = -(-PADS // N) * N
NBANK = NPAIR // N
MADE = 2 + SLOTS - NSLOT[-1]


BLOCK = 2 * D
NBLOCK = (B * N + EXPERTS * (BLOCK - 1)) // BLOCK
SORTED = NBLOCK * BLOCK
RNE = 2.0 ** 23


def phase_gate(nc, hid, s_res, th, silu2, prefetch):
    with ExitStack() as ctx:
        tanh_ready, silu_ready, gated_ready = (
            ctx.enter_context(nc.semaphore("g_" + n)) for n in ("tanh_ready", "silu_ready", "gated_ready"))
        with nc.Block() as block:

            @block.sync
            def _(sp):
                prefetch(sp)

            @block.scalar
            def _(act):
                act.preload_act_table_set("exp_and_others")

                def step(s, u, r):
                    reach(act, silu_ready, s - 1)
                    act.activation(th[u], hid[:, columns(s)], ACT.Tanh, scale=0.5).then_inc(tanh_ready, 1)
                run_steps(act, step, B, 0, 2)

            @block.vector
            def _(dve):
                def step(s, u, r):
                    dve.wait_ge(tanh_ready, s + 1)
                    reach(dve, gated_ready, s - 1)
                    dve.scalar_tensor_tensor(out=silu2[u], in0=th[u], scalar=1.0, in1=hid[:, columns(s)],
                                             op0=ALU.add, op1=ALU.mult).then_inc(silu_ready, 1)
                    dve.wait_ge(silu_ready, s + 1)
                    dve.scalar_tensor_tensor(out=s_res[:, columns(s)], in0=silu2[u], scalar=0.5,
                                             in1=s_res[:, columns(s)], op0=ALU.mult, op1=ALU.mult).then_inc(gated_ready, 1)
                run_steps(dve, step, B, 0, 2)


def phase_sparse_attention(nc, dram, ident, ident_bf, centre, average, xres, s_res, places, weight_rows):
    with ExitStack() as ctx:
        def sb(name, shape, dt=F32):
            return ctx.enter_context(nc.sbuf_tensor("c_" + name, shape, dt))

        def ps(name):
            return ctx.enter_context(nc.psum_tensor("c_" + name, [D, N], F32))

        def sem(name):
            return ctx.enter_context(nc.semaphore("c_" + name))

        w = sb("w", [D, 6, D])
        vecs = sb("vecs", [D, 6])
        gate_w = sb("gate_w", [D, EXPERTS])
        eps = sb("eps", [D, 1])
        rope = sb("rope", [D, 2, N])
        counts = sb("counts", [D, NPAIR], BF16)
        mask = sb("mask", [D, NPAIR], BF16)
        same_head = sb("same_head", [D, D])
        x_in = [sb(f"x_in{p}", [D, TT, D]) for p in range(2)]
        xn = sb("xn", [D, N])
        tokens = [sb(f"tokens{p}", [D, N]) for p in range(2)]
        squares, rstd = sb("squares", [D, N]), sb("rstd", [D, N])
        ln_var = squares
        by_cos, by_sin = sb("by_cos", [D, N]), sb("by_sin", [D, N])
        qkv = sb("qkv", [D, 3, N])
        q_skew = sb("q_skew", [D, N])
        k_skew = sb("k_skew", [D, HALO + N])
        v_skew = [sb(f"v_skew{p}", [D, HALO + N]) for p in range(2)]
        product = sb("product", [D, NPAIR])
        logits = [sb(f"logits{p}", [D, NPAIR]) for p in range(2)]
        values = sb("values", [D, NPAIR])
        largest = sb("largest", [D, N])
        denominator = sb("denominator", [D, N])
        level_out = sb("level_out", [D, LEVEL_COLS])
        ln_sum, inverse = sb("ln_sum", [D, N]), sb("inverse", [D, N])
        mixed = sb("mixed", [D, N])
        mixed_back = sb("mixed_back", [D, N])
        gate_logits = sb("gate_logits", [D, NT * EXPERTS])

        gate_b = sb("gate_b", [D, 2, EXPERTS])
        rank = sb("rank", [D, EXPERTS])
        triangle = sb("triangle", [D, 2, D], BF16)
        restart = sb("restart", [D, EXPERTS * NT])
        block_number = sb("block_number", [D, NBLOCK])
        partition = sb("partition", [D, 1])
        one_hot = sb("one_hot", [D, NT, EXPERTS], BF16)
        top = [sb(f"top{k}", [D, NT]) for k in range(2)]
        taken = [0]

        def part_of_product(*shape):
            n = int(np.prod(shape))
            cols = product[:, taken[0]:taken[0] + n]
            taken[0] += n
            assert taken[0] <= NPAIR
            return cols.rearrange("p (a b) -> p a b", b=shape[1]) if len(shape) == 2 else cols

        logit, logit2, best, place = (part_of_product(NT, EXPERTS) for _ in range(4))
        total, seen = part_of_product(EXPERTS * NT), part_of_product(EXPERTS * NT)
        ended = part_of_product(NBLOCK, EXPERTS)
        share = [part_of_product(EXPERTS) for _ in range(3)]
        ones8, block_end, base = (part_of_product(EXPERTS) for _ in range(3))
        expert = [top[0][:, 0:NBLOCK], top[1][:, 0:NBLOCK]]
        place_f = part_of_product(NT)
        in_logits = NPAIR // N
        places_of_tokens = ([logits[0][:, k * N:(k + 1) * N] for k in range(in_logits)] + [qkv[:, k, :] for k in range(3)] +
                            [rope[:, k, :] for k in range(2)] + [by_cos[:], by_sin[:]])
        assert len(places_of_tokens) >= B - 2
        places_of_tokens = places_of_tokens[:B - 2] + [tokens[0][:], tokens[1][:]]
        ring = dram["ring"]
        back = dram["back"]

        x_ps, centred_ps, var_ps, out_ps = ps("x_ps"), ps("centred_ps"), ps("var_ps"), ps("out_ps")
        proj_ps = [ps(f"proj_ps{k}") for k in range(2)]
        pair_ps = [ps(f"pair_ps{k}") for k in range(2)]

        consts_in = sem("consts_in")
        tables_in = sem("tables_in")
        routing_in = sem("routing_in")
        chain = sem("chain")
        chosen = sem("chosen")
        counted = sem("counted")
        placed = sem("placed")
        tokens_back = sem("tokens_back")
        scattered = sem("scattered")
        consts_made = sem("consts_made")
        x_loaded = [sem(f"x_loaded{p}") for p in range(2)]
        x_turned = sem("x_turned")
        x_ready = sem("x_ready")
        centred = sem("centred")
        squared = sem("squared")
        var_done = sem("var_done")
        ln_ready = sem("ln_ready")
        rstd_ready = sem("rstd_ready")
        xn_ready = sem("xn_ready")
        xn_turned = sem("xn_turned")
        tokens_ready = sem("tokens_ready")
        gates_ready = sem("gates_ready")
        tokens_stored = [sem(f"tokens_stored{p}") for p in range(2)]
        proj_done = sem("proj_done")
        rope_products = sem("rope_products")
        qk_ready = sem("qk_ready")
        v_ready = sem("v_ready")
        ring_written = sem("ring_written")
        q_skewed = sem("q_skewed")
        k_skewed = sem("k_skewed")
        v_skewed = [sem(f"v_skewed{p}") for p in range(2)]
        products = sem("products")
        counted_ready = sem("counted_ready")
        pairs_done = sem("pairs_done")
        logits_ready = sem("logits_ready")
        folded = sem("folded")
        shifted = sem("shifted")
        exp_ready = sem("exp_ready")
        weighted = sem("weighted")
        summed = sem("summed")
        ln_sum_ready = sem("ln_sum_ready")
        inverse_ready = sem("inverse_ready")
        mixed_ready = sem("mixed_ready")
        back_written = sem("back_written")
        back_read = sem("back_read")
        out_done = sem("out_done")
        s_ready = sem("s_ready")
        BQ, BQR, BK, BKR, BV, BO = range(6)
        LOADS = 16 * (6 + 2 + 8 + 1 + 1)
        EXPS = 3
        NOPS = 1 + LEVELS
        FOLD = 2 + LEVELS
        MAX_FOLD, SUM_FOLD = 0, FOLD

        def slots(buf, x, n=SLOTS):
            return buf[:, N:N + SLOTS * LEVEL_COLS].rearrange("p (k m) -> p k m", k=SLOTS)[:, 0:n, LEVEL[x]:LEVEL[x + 1]]

        def queries(buf, x, n=SLOTS):
            v = buf[:, 0:N].rearrange("p (m r) -> p m r", r=2 ** x)[:, :, 0]
            return v.unsqueeze(1).to_broadcast([D, n, NCOL[x]])

        def own(buf, x):
            return buf[:, 0:N].rearrange("p (m r) -> p m r", r=2 ** x)[:, :, 0]

        def earlier(buf, x):
            r = 2 ** x
            start = HALO - NSLOT[x] * r
            base = buf[:, start:start + 1]
            a = [list(d) for d in base.ap]
            return bass.AP(base.tensor, base.offset, [a[0], [r, NSLOT[x]], [r, NCOL[x]]])

        def skewed(t, p, parts, start, width, rows, step):
            base = t[p]
            first = base.offset + start
            dims = [[DH1 * rows + step, H1], [rows, DH1]]
            if parts is not None:
                first += parts * RING
            return bass.AP(base.tensor, first, dims + [[1, width]])

        def exists(s):
            return not known(s) or 0 <= s < B

        def run(eng, step, route=lambda: None):
            run_steps(eng, step, B, 2, 2, peel=2)
            route()
            for s in (B, B + 1):
                step(s, s % 2, s // 2)

        def load(sp):
            for k, name in enumerate(("Wq", "Wk")):
                half = D // 2
                sp.dma_start(w[:, 2 * k, :], dram[name]).then_inc(consts_in, 16)
                for a, b in ((0, half), (half, 0)):
                    sp.dma_start(w[:, 2 * k + 1, a:a + half], dram[name][:, b:b + half]).then_inc(consts_in, 16)
            for k, name in enumerate(("Wv", "Wo")):
                sp.dma_start(w[:, 4 + k, :], dram[name]).then_inc(consts_in, 16)
            for k, name in enumerate(("bq", "bk")):
                half = D // 2
                sp.dma_start(vecs[:, 2 * k:2 * k + 1], dram[name]).then_inc(consts_in, 16)
                for a, b in ((0, half), (half, 0)):
                    sp.dma_start(vecs[a:a + half, 2 * k + 1:2 * k + 2], dram[name][b:b + half]).then_inc(consts_in, 16)
            for k, name in enumerate(("bv", "bo")):
                sp.dma_start(vecs[:, 4 + k:5 + k], dram[name]).then_inc(consts_in, 16)
            sp.dma_start(gate_w[:], dram["gate_w"]).then_inc(consts_in, 16)
            sp.dma_start(rope[:], dram["rope1"]).then_inc(consts_in, 16)
            for dst, name in ((same_head, "same_head"), (counts, "counts"), (mask, "pair_mask")):
                sp.dma_start(dst[:], dram[name]).then_inc(tables_in, 16)
            for k, name in enumerate(("gate_b", "expert_bias")):
                sp.dma_start(gate_b[:, k, :], dram[name].to_broadcast([D, EXPERTS])).then_inc(routing_in, 16)
            for dst, name in ((rank, "rank"), (triangle, "triangle"), (restart, "restart"),
                              (block_number, "block_number"), (partition, "partition")):
                sp.dma_start(dst[:], dram[name]).then_inc(routing_in, 16)

        phase_gate(nc, xres, s_res, [logits[0][:, p * N:(p + 1) * N] for p in range(2)],
                   [logits[1][:, p * N:(p + 1) * N] for p in range(2)], load)

        with nc.Block() as block:

            @block.sync
            def _(sp):
                def step(s, u, r):
                    q = (u + 1) % 2
                    if exists(s + 2):
                        reach(sp, x_turned, s + 1)
                        src = (dram["x"][s + 2] if known(s) else
                               dram["x"][bass.ds(s + 2, 1)].rearrange("o t d -> (o t) d"))
                        sp.dma_start(x_in[u][:], src.rearrange("(t p) d -> p t d", p=D)).then_inc(x_loaded[u], 16)
                    if exists(s + 1):
                        if not known(s) or s >= 1:
                            sp.wait_ge(v_skewed[q], 16 * (r + u))
                        sp.wait_ge(qk_ready, 2 * s + 4)
                        sp.wait_ge(v_ready, s + 2)
                        sp.dma_start(ring[q][:, :, N:2 * N], qkv[:]).then_inc(ring_written, 16)
                        sp.dma_start(ring[q][:, 1:3, N - HALO:N], qkv[:, 1:3, N - HALO:N]).then_inc(ring_written, 16)
                        sp.dma_start(ring[q][:, :, 2 * N:RING], qkv[:, :, 0:SKEW]).then_inc(ring_written, 16)
                    if exists(s - 2):
                        sp.wait_ge(mixed_ready, s - 1)
                        sp.dma_start(back[u].rearrange("p (a n) -> p a n", a=2),
                                     mixed[:].unsqueeze(1).to_broadcast([D, 2, N])).then_inc(back_written, 16)
                    if exists(s + 1):
                        reach(sp, products, NOPS * s + NOPS)
                        sp.wait_ge(ring_written, 48 * s + 96)
                        sp.dma_start(q_skew[:], skewed(ring, q, 0, N, N, 3 * RING, 1)).then_inc(q_skewed, 16)
                        sp.dma_start(k_skew[:], skewed(ring, q, 1, N - HALO, HALO + N, 3 * RING, 1)).then_inc(k_skewed, 16)
                    if exists(s - 2):
                        reach(sp, out_done, s - 2)
                        sp.wait_ge(back_written, 16 * s - 16)
                        sp.dma_start(mixed_back[:], skewed(back, u, None, N, N, 2 * N, -1)).then_inc(back_read, 16)
                    if exists(s + 1):
                        sp.wait_ge(tokens_ready, s + 2)
                        sp.dma_start(dram["tokens"][s + 1] if known(s) else
                                     dram["tokens"][bass.ds(s + 1, 1)].rearrange("o p n -> (o p) n"),
                                     tokens[q][:]).then_inc(tokens_stored[q], 16)
                        reach(sp, weighted, NOPS * s)
                        sp.dma_start(v_skew[q][:], skewed(ring, q, 2, N - HALO, HALO + N, 3 * RING, 1)).then_inc(v_skewed[q], 16)
                def route():
                    for p in range(2):
                        sp.wait_ge(tokens_stored[p], 16 * (B // 2))
                    sp.wait_ge(weighted, NOPS * (B - 1))
                    sp.wait_ge(folded, 2 * FOLD * (B - 1))
                    sp.wait_ge(ring_written, 48 * B)
                    sp.wait_ge(qk_ready, 2 * B)
                    for i in range(B - 2):
                        sp.dma_start(places_of_tokens[i], dram["tokens"][i]).then_inc(tokens_back, 16)
                run(sp, step, route)

            @block.gpsimd
            def _(pool):
                pool.memset(product[:, PADS:NPAIR], 0.0).then_inc(consts_made, 1)
                for k in range(NSLOT[LEVELS - 1], SLOTS):
                    pool.memset(product[:, N + k * LEVEL_COLS + LEVEL[LEVELS - 1]:N + (k + 1) * LEVEL_COLS],
                                0.0).then_inc(consts_made, 1)
                pool.memset(eps[:], EPS).then_inc(consts_made, 1)
                pool.wait_ge(tables_in, 48)
                pool.wait_ge(consts_made, MADE)

                def step(s, u, r):
                    if exists(s):
                        for x in range(LEVELS + 1):
                            src = product[:, 0:N] if x == LEVELS else slots(product, x, NSLOT[x])
                            c = counts[:, 0:N] if x == LEVELS else slots(counts, x, NSLOT[x])
                            pool.wait_ge(products, s * NOPS + 1 + x)
                            pool.tensor_tensor(src, src, c, ALU.mult).then_inc(counted_ready, 1)
                    if exists(s + 1):
                        for k in range(2):
                            if k == 0:
                                reach(pool, ring_written, 48 * (s + 1))
                            pool.wait_ge(rope_products, 4 * (s + 1) + 2 * k + 2)
                            pool.tensor_tensor(qkv[:, k, :], by_cos[:], by_sin[:], ALU.add).then_inc(qk_ready, 1)
                    if exists(s - 1):
                        p = (u + 1) % 2
                        for x in range(LEVELS + 1):
                            pool.wait_ge(exp_ready, EXPS * (s - 1) + (1 if x == 0 else EXPS if x == LEVELS else 2))
                            if x == 0:
                                pool.wait_ge(v_skewed[p], 16 * (r + u))
                                reach(pool, summed, s - 1)
                            out, e, v = ((values[:, 0:N], logits[p][:, 0:N], v_skew[p][:, HALO:]) if x == LEVELS else
                                         (slots(values, x, NSLOT[x]), slots(logits[p], x, NSLOT[x]), earlier(v_skew[p], x)))
                            pool.tensor_tensor(out, e, v, ALU.mult).then_inc(weighted, 1)
                def scatter(first, last):
                    for j in range(first, last):
                        i, t = j // TT, j % TT
                        pool.indirect_dma_start(dram["sorted"], bass.IndirectOffsetOnAxis(ap=places[:, j:j + 1], axis=0),
                                                places_of_tokens[i][:, t * D:(t + 1) * D], None).then_inc(scattered, 16)

                def route():
                    pool.wait_ge(tokens_back, 16 * (B - 2))
                    pool.wait_ge(placed, 1)
                    scatter(0, NT // 4)
                run(pool, step, route)
                scatter(NT // 4, NT)
                pool.wait_ge(scattered, 16 * NT)

            @block.scalar
            def _(act):
                act.preload_act_table_set(EXP_LN)
                act.wait_ge(consts_in, LOADS)
                act.wait_ge(consts_made, MADE)

                def step(s, u, r):
                    q = (u + 1) % 2

                    def evacuate(b):
                        act.wait_ge(pairs_done, s * NBANK + b + 1)
                        if b == 0:
                            reach(act, weighted, NOPS * (s - 1))
                            reach(act, folded, 2 * FOLD * (s - 1))
                        act.activation(logits[u][:, b * N:(b + 1) * N], pair_ps[b % 2][:], ACT.Copy).then_inc(logits_ready, 1)

                    def exponentials(part):
                        first = slots(logits[q], 0)
                        rest = (logits[q][:, N:N + SLOTS * LEVEL_COLS].rearrange("p (k m) -> p k m", k=SLOTS)
                                [:, :, LEVEL[1]:])
                        v = (first, rest, logits[q][:, 0:N])[part]
                        act.wait_ge(shifted, NOPS * (s - 1) + (1, LEVELS, NOPS)[part])
                        act.activation(v, v, ACT.Exp).then_inc(exp_ready, 1)

                    if exists(s + 1):
                        act.wait_ge(proj_done, 5 * (s + 1) + 1)
                        reach(act, ring_written, 48 * (s + 1))
                        act.activation(qkv[:, 2, :], proj_ps[0][:], ACT.Identity, bias=vecs[:, BV:BV + 1]).then_inc(v_ready, 1)
                    if exists(s - 2):
                        act.wait_ge(folded, 2 * FOLD * (s - 1))
                        act.activation(ln_sum[:], denominator[:], ACT.Ln).then_inc(ln_sum_ready, 1)
                        act.wait_ge(ln_sum_ready, s - 1)
                        reach(act, mixed_ready, s - 2)
                        act.activation(inverse[:], ln_sum[:], ACT.Exp, scale=-1.0).then_inc(inverse_ready, 1)
                    if exists(s + 1):
                        act.wait_ge(xn_turned, s + 2)
                        if not known(s) or s + 1 >= 2:
                            act.wait_ge(tokens_stored[q], 16 * (r + u))
                        act.activation(tokens[q][:], x_ps[:], ACT.Copy).then_inc(tokens_ready, 1)
                        act.activation(gate_logits[:, columns(s + 1, TT * EXPERTS)], var_ps[:, 0:TT * EXPERTS],
                                       ACT.Copy).then_inc(gates_ready, 1)
                    if exists(s - 1):
                        exponentials(0)
                        exponentials(1)
                    if exists(s):
                        evacuate(0)
                    if exists(s - 1):
                        exponentials(2)
                    if exists(s):
                        for b in range(1, 4):
                            evacuate(b)
                    if exists(s + 2):
                        act.wait_ge(centred, s + 3)
                        reach(act, var_done, s + 2)
                        act.activation(squares[:], centred_ps[:], ACT.Square).then_inc(squared, 1)
                    if exists(s):
                        for b in range(4, NBANK):
                            evacuate(b)
                    if exists(s - 2):
                        act.wait_ge(out_done, s - 1)
                        act.activation(s_res[:, columns(s - 2)], out_ps[:], ACT.Identity,
                                       bias=vecs[:, BO:BO + 1]).then_inc(s_ready, 1)
                    if exists(s + 2):
                        act.wait_ge(var_done, s + 3)
                        act.activation(ln_var[:], var_ps[:], ACT.Ln, bias=eps[:]).then_inc(ln_ready, 1)
                        act.wait_ge(ln_ready, s + 3)
                        reach(act, xn_ready, s + 2)
                        act.activation(rstd[:], ln_var[:], ACT.Exp, scale=-0.5).then_inc(rstd_ready, 1)
                run(act, step)

            @block.tensor
            def _(pe):
                pe.wait_ge(consts_in, LOADS)

                def project(k, bank, s):
                    pe.matmul(proj_ps[bank][:], w[:, k, :], xn[:], start=True, stop=True).then_inc(proj_done, 1)

                def add_values(x):
                    for k in range(NSLOT[x]):
                        ins = pe.matmul(own(out_ps, x), ident[:], slots(values, x)[:, k, :], start=False,
                                        stop=(x == LEVELS - 1), skip_group_check=True)
                    return ins

                def step(s, u, r):
                    q = (u + 1) % 2

                    def pairs(b):
                        reach(pe, logits_ready, s * NBANK + max(b - 1, 0))
                        pe.matmul(pair_ps[b % 2][:], ident_bf[:], mask[:, b * N:(b + 1) * N],
                                  start=True, stop=False, skip_group_check=True)
                        if b == 0:
                            pe.wait_ge(counted_ready, s * NOPS + NOPS)
                        pe.matmul(pair_ps[b % 2][:], same_head[:], product[:, b * N:(b + 1) * N],
                                  start=False, stop=True, skip_group_check=True).then_inc(pairs_done, 1)

                    if exists(s - 2):
                        pe.wait_ge(weighted, NOPS * (s - 1))
                        reach(pe, s_ready, s - 2)
                        pe.matmul(out_ps[:], ident[:], values[:, 0:N], start=True, stop=False, skip_group_check=True)
                        add_values(0)
                    if exists(s + 1):
                        pe.wait_ge(xn_ready, s + 2)
                        reach(pe, qk_ready, 2 * (s + 1))
                        project(4, 0, s)
                        project(1, 1, s)
                        for t in range(TT):
                            pe.transpose(x_ps[:, t * D:(t + 1) * D], xn[:, t * D:(t + 1) * D], ident[:])
                        for t in range(TT):
                            ins = pe.matmul(var_ps[:, t * EXPERTS:(t + 1) * EXPERTS], xn[:, t * D:(t + 1) * D], gate_w[:],
                                            start=True, stop=True, skip_group_check=True)
                        ins.then_inc(xn_turned, 1)
                        pe.wait_ge(v_ready, s + 2)
                        project(0, 0, s)
                    if exists(s - 2):
                        add_values(1)
                        add_values(2)
                    if exists(s + 1):
                        pe.wait_ge(rope_products, 4 * (s + 1) + 2)
                        project(2, 0, s)
                        project(3, 1, s)
                    if exists(s - 2):
                        for x in range(3, LEVELS):
                            ins = add_values(x)
                        ins.then_inc(summed, 1)
                    if exists(s + 2):
                        pe.wait_ge(x_loaded[u], 16 * (r + 2))
                        reach(pe, tokens_ready, s + 2)
                        for t in range(TT):
                            ins = pe.transpose(x_ps[:, t * D:(t + 1) * D], x_in[u][:, t, :], ident[:])
                        ins.then_inc(x_turned, 1)
                    if known(s) and s == 0:
                        pe.wait_ge(tables_in, 48)
                    if exists(s):
                        for b in range(3):
                            pairs(b)
                    if exists(s + 2):
                        pe.wait_ge(x_ready, s + 3)
                        reach(pe, xn_ready, s + 2)
                        pe.matmul(centred_ps[:], centre[:], xres[:, columns(s + 2)], start=True, stop=True).then_inc(centred, 1)
                    if exists(s):
                        for b in range(3, NBANK):
                            pairs(b)
                    if exists(s + 2):
                        pe.wait_ge(squared, s + 3)
                        reach(pe, gates_ready, s + 2)
                        pe.matmul(var_ps[:], average[:], squares[:], start=True, stop=True).then_inc(var_done, 1)
                    if exists(s - 2):
                        pe.wait_ge(back_read, 16 * (s - 1))
                        pe.wait_ge(mixed_ready, s - 1)
                        pe.matmul(out_ps[:], w[:, 5, :], mixed_back[:], start=True, stop=True).then_inc(out_done, 1)
                def route():
                    pe.wait_ge(routing_in, 7 * 16)
                    pe.wait_ge(chosen, 1)
                    pe.wait_ge(v_ready, B)
                    pe.wait_ge(qk_ready, 2 * B)
                    pe.matmul(proj_ps[0][:], triangle[:, 0, :], one_hot[:], start=True, stop=True)
                    pe.matmul(proj_ps[1][:], triangle[:, 1, :], one_hot[:], start=True, stop=True).then_inc(counted, 1)
                run(pe, step, route)

            @block.vector
            def _(dve):
                dve.wait_ge(consts_in, LOADS)

                def fold(src, out, op, n):
                    def slot(k):
                        return src[:, N + k * LEVEL_COLS:N + (k + 1) * LEVEL_COLS]
                    reach(dve, folded, n)
                    dve.tensor_tensor(level_out[:], slot(0), slot(1), op).then_inc(folded, 1)
                    dve.wait_ge(folded, n + 1)
                    dve.tensor_tensor(level_out[:], level_out[:], slot(2), op).then_inc(folded, 1)
                    for x in range(LEVELS):
                        dve.wait_ge(folded, n + 2 + x)
                        first = src[:, 0:N] if x == 0 else own(out, x)
                        dve.tensor_tensor(own(out, x), first, level_out[:, LEVEL[x]:LEVEL[x + 1]], op).then_inc(folded, 1)

                def rotate(k, s):
                    dve.wait_ge(proj_done, 5 * (s + 1) + 2 * k + 3)
                    reach(dve, qk_ready, 2 * (s + 1) + k)
                    dve.scalar_tensor_tensor(out=by_cos[:], in0=proj_ps[0][:], scalar=vecs[:, 2 * k:2 * k + 1],
                                             in1=rope[:, 0, :], op0=ALU.add, op1=ALU.mult).then_inc(rope_products, 1)
                    dve.scalar_tensor_tensor(out=by_sin[:], in0=proj_ps[1][:], scalar=vecs[:, 2 * k + 1:2 * k + 2],
                                             in1=rope[:, 1, :], op0=ALU.add, op1=ALU.mult).then_inc(rope_products, 1)

                def step(s, u, r):
                    q = (u + 1) % 2
                    cols = columns(s + 2)

                    def shift_level(x):
                        dve.tensor_tensor(slots(logits[q], x), slots(logits[q], x), queries(largest, x),
                                          ALU.subtract).then_inc(shifted, 1)

                    if exists(s):
                        dve.wait_ge(q_skewed, 16 * (s + 1))
                        dve.wait_ge(k_skewed, 16 * (s + 1))
                        reach(dve, pairs_done, NBANK * s)
                        for x in range(LEVELS):
                            dve.tensor_tensor(slots(product, x, NSLOT[x]), queries(q_skew, x, NSLOT[x]), earlier(k_skew, x),
                                              ALU.mult).then_inc(products, 1)
                        dve.tensor_tensor(product[:, 0:N], q_skew[:], k_skew[:, HALO:], ALU.mult).then_inc(products, 1)
                    if exists(s + 1):
                        dve.wait_ge(rstd_ready, s + 2)
                        reach(dve, xn_turned, s + 1)
                        dve.tensor_tensor(xn[:], centred_ps[:], rstd[:], ALU.mult).then_inc(xn_ready, 1)
                    n = 2 * FOLD * (s - 1)
                    if exists(s - 1):
                        dve.wait_ge(logits_ready, s * NBANK)
                        fold(logits[q], largest, ALU.max, n + MAX_FOLD)
                        dve.wait_ge(folded, n + FOLD)
                    if exists(s + 1):
                        rotate(0, s)
                    if exists(s - 1):
                        shift_level(0)
                    if exists(s + 1):
                        rotate(1, s)
                    if exists(s - 1):
                        for x in range(1, LEVELS):
                            shift_level(x)
                        dve.tensor_tensor(logits[q][:, 0:N], logits[q][:, 0:N], largest[:], ALU.subtract).then_inc(shifted, 1)
                    if exists(s - 2):
                        dve.wait_ge(inverse_ready, s - 1)
                        dve.wait_ge(summed, s - 1)
                        reach(dve, back_written, 16 * (s - 2))
                        dve.tensor_tensor(mixed[:], out_ps[:], inverse[:], ALU.mult).then_inc(mixed_ready, 1)
                    if exists(s + 2):
                        dve.wait_ge(x_turned, s + 3)
                        dve.tensor_tensor(xres[:, cols], x_ps[:], s_res[:, cols], ALU.add).then_inc(x_ready, 1)
                    if exists(s - 1):
                        dve.wait_ge(exp_ready, EXPS * s)
                        reach(dve, ln_sum_ready, s - 1)
                        fold(logits[q], denominator, ALU.add, n + SUM_FOLD)
                def route():
                    dve.wait_ge(routing_in, 7 * 16)
                    dve.wait_ge(gates_ready, B)
                    dve.wait_ge(pairs_done, NBANK * B)

                    def by_tile_and_expert(bank):
                        return bank[:].rearrange("p (j e) -> p j e", e=EXPERTS)

                    steps = [0]

                    def then(ins):
                        ins.then_inc(chain, 1)
                        steps[0] += 1
                        dve.wait_ge(chain, steps[0])

                    def by_tile(row):
                        return row.unsqueeze(1).to_broadcast([D, NT, EXPERTS])

                    def by_expert(column):
                        return column.unsqueeze(2).to_broadcast([D, NT, EXPERTS])

                    products = gate_logits[:].rearrange("p (j e) -> p j e", e=EXPERTS)
                    then(dve.tensor_tensor(logit[:], products, by_tile(gate_b[:, 0, :]), ALU.add))
                    then(dve.tensor_tensor(logit2[:], logit[:], by_tile(gate_b[:, 1, :]), ALU.add))
                    then(dve.tensor_reduce(top[0][:], logit2[:], AX_X, ALU.max))
                    tied = logit
                    then(dve.tensor_tensor(tied[:], logit2[:], by_expert(top[0][:]), ALU.is_ge))
                    then(dve.tensor_tensor(best[:], tied[:], by_tile(rank[:]), ALU.mult))
                    then(dve.tensor_reduce(top[1][:], best[:], AX_X, ALU.max))
                    dve.tensor_tensor(one_hot[:], best[:], by_expert(top[1][:]), ALU.is_equal).then_inc(chosen, 1)
                    dve.wait_ge(counted, 1)
                    then(dve.tensor_copy(total[:].rearrange("p (e j) -> p e j", e=EXPERTS), by_tile_and_expert(proj_ps[1]).rearrange("p j e -> p e j")))
                    then(dve.tensor_tensor_scan(seen[:], restart[:], total[:], 0.0, ALU.mult, ALU.add))
                    then(dve.tensor_scalar(share[0][:], seen[:, NT - 1::NT], 1.0 / BLOCK,
                                           (BLOCK - 1.0) / BLOCK - 0.5 + 0.5 / BLOCK, ALU.mult, ALU.add))
                    then(dve.tensor_scalar(share[1][:], share[0][:], RNE, None, ALU.add))
                    then(dve.tensor_scalar(share[2][:], share[1][:], -RNE, None, ALU.add))
                    then(dve.memset(ones8[:], 1.0))
                    then(dve.tensor_tensor_scan(block_end[:], ones8[:], share[2][:], 0.0, ALU.mult, ALU.add))
                    then(dve.tensor_tensor(share[0][:], block_end[:], share[2][:], ALU.subtract))
                    then(dve.tensor_scalar(base[:], share[0][:], float(BLOCK), None, ALU.mult))
                    then(dve.tensor_tensor(place[:], by_tile_and_expert(proj_ps[0]), seen[:].rearrange("p (e j) -> p j e", e=EXPERTS), ALU.add))
                    then(dve.tensor_tensor(logit[:], place[:], total[:].rearrange("p (e j) -> p j e", e=EXPERTS), ALU.subtract))
                    then(dve.tensor_tensor(logit2[:], logit[:], by_tile(base[:]), ALU.add))
                    then(dve.tensor_tensor(place[:], logit2[:], one_hot[:], ALU.mult))
                    then(dve.tensor_reduce(place_f[:], place[:], AX_X, ALU.add))
                    dve.tensor_copy(places[:], place_f[:]).then_inc(placed, 1)
                    then(dve.tensor_tensor(ended[:], block_end[:].unsqueeze(1).to_broadcast([D, NBLOCK, EXPERTS]),
                                           block_number[:].unsqueeze(2).to_broadcast([D, NBLOCK, EXPERTS]), ALU.is_le))
                    then(dve.tensor_reduce(expert[0], ended[:], AX_X, ALU.add))
                    then(dve.tensor_scalar(expert[1], expert[0], float(EXPERTS - 1), float(D), ALU.min, ALU.mult))
                    then(dve.tensor_scalar(expert[0], expert[1], partition[:], None, ALU.add))
                    dve.tensor_copy(weight_rows[:], expert[0]).then_inc(placed, 1)
                run(dve, step, route)


def rope1_table():
    f = np.float32
    inv_freq = (f(1.0) / f(15000.0) ** (np.arange(0, D, 2, dtype=f) / f(D))).astype(f)
    freqs = np.arange(N, dtype=f)[:, None] * inv_freq[None, :]
    emb = np.concatenate([freqs, freqs], -1).T
    sign = np.where(np.arange(D) < D // 2, f(-1), f(1))[:, None]
    return np.ascontiguousarray(np.stack([np.cos(emb), np.sin(emb) * sign], 1).astype(f))


def pair_tables():
    counts = np.zeros((H1, NPAIR), np.float32)
    idx = np.arange(N)
    for h in range(H1):
        count = np.zeros((N, N), np.float32)
        for x in range(LEVELS):
            ok = idx % 2 ** x == h % 2 ** x
            count += (idx[:, None] // 2 ** (x + 2) == idx[None, :] // 2 ** (x + 2)) & ok[:, None] & ok[None, :]
        taken = np.zeros((N, N), bool)
        counts[h, 0:N] = count[(idx + h) % N, (idx + h) % N]
        for x in reversed(range(LEVELS)):
            r = 2 ** x
            for slot in range(NSLOT[x]):
                k = NSLOT[x] - slot
                for m in range(NCOL[x]):
                    i = (m * r + h) % N
                    j = i - k * r
                    if j < 0 or taken[i, j] or count[i, j] == 0:
                        continue
                    taken[i, j] = True
                    counts[h, N + slot * LEVEL_COLS + LEVEL[x] + m] = count[i, j]
        need = (count > 0) & (idx[None, :] < idx[:, None])
        assert (taken == need).all()
    mask = np.where(counts > 0, 0.0, -1e30).astype(mybir.dt.np(BF16))
    return np.repeat(counts.astype(mybir.dt.np(BF16)), DH1, 0), np.repeat(mask, DH1, 0)


DFF = 512
FC = DFF // D
B1_COL, B2_COL = 2 * DFF, 2 * DFF + FC
EXPERT_ROW = 2 * DFF + FC + 4


def run_experts(nc, dram, ident, weight_rows):
    with ExitStack() as ctx:
        def sb(name, shape, dt=F32):
            return ctx.enter_context(nc.sbuf_tensor("e_" + name, shape, dt))

        def ps(name, shape):
            return ctx.enter_context(nc.psum_tensor("e_" + name, shape, F32))

        def sem(name):
            return ctx.enter_context(nc.semaphore("e_" + name))

        U = 3
        HALF = FC // 2
        HT = BLOCK // D
        rows_in = [sb(f"rows_in{u}", [D, HT, D]) for u in range(U)]
        w = [sb(f"w{u}", [D, EXPERT_ROW]) for u in range(U)]
        x_t = [sb(f"x_t{u}", [D, BLOCK]) for u in range(U)]
        hidden = [sb(f"hidden{u}", [D, FC, BLOCK]) for u in range(U)]
        y_t = [sb(f"y_t{u}", [D, BLOCK]) for u in range(U)]
        rows_out = [sb(f"rows_out{u}", [D, HT, D]) for u in range(U)]
        x_ps, y_ps = ps("x_ps", [D, 512]), ps("y_ps", [D, 512])
        rows_ps = ps("rows_ps", [D, 512])
        hidden_ps = [ps(f"hidden_ps{k}", [D, HALF, BLOCK]) for k in range(2)]

        weights_in = [sem(f"weights_in{u}") for u in range(U)]
        rows_loaded = [sem(f"rows_loaded{u}") for u in range(U)]
        x_turned = sem("x_turned")
        x_ready = sem("x_ready")
        hidden_done = [sem(f"hidden_done{k}") for k in range(2)]
        relu_ready = [sem(f"relu_ready{k}") for k in range(2)]
        y_done = sem("y_done")
        y_ready = sem("y_ready")
        y_turned = sem("y_turned")
        rows_ready = sem("rows_ready")
        rows_stored = [sem(f"rows_stored{u}") for u in range(U)]

        def exists(s):
            return not known(s) or 0 <= s < NBLOCK

        def run(eng, step):
            run_steps(eng, step, NBLOCK, 2, U, peel=2)
            for s in (NBLOCK, NBLOCK + 1):
                step(s, s % U, s // U)

        def block_rows(t, s):
            if known(s):
                return t[s * BLOCK:(s + 1) * BLOCK].rearrange("(h p) d -> p h d", p=D)
            return t.rearrange("(b h p) d -> b p h d", p=D, h=HT)[bass.ds(s, 1)].rearrange("o p h d -> p (o h) d")

        with nc.Block() as block:

            @block.sync
            def _(sp):
                def step(s, u, r):
                    if exists(s + 2):
                        q = (u + 2) % U
                        reach(sp, x_turned, s)
                        sp.dma_start(rows_in[q][:], block_rows(dram["sorted"], s + 2)).then_inc(rows_loaded[q], 16)
                    if exists(s - 2):
                        q = (u + 1) % U
                        sp.wait_ge(rows_ready, s - 1)
                        sp.dma_start(block_rows(dram["answers"], s - 2), rows_out[q][:]).then_inc(rows_stored[q], 16)
                run(sp, step)
                for u in range(U):
                    sp.wait_ge(rows_stored[u], 16 * (NBLOCK // U))

            @block.gpsimd
            def _(pool):
                for s in range(NBLOCK):
                    reach(pool, y_ready, s - U + 1)
                    pool.indirect_dma_start(w[s % U][:], None, dram["weights"],
                                            bass.IndirectOffsetOnAxis(ap=weight_rows[:, s:s + 1], axis=0)
                                            ).then_inc(weights_in[s % U], 16)

            @block.scalar
            def _(act):
                act.preload_act_table_set("exp_and_others")

                def step(s, u, r):
                    if exists(s + 1):
                        act.wait_ge(x_turned, s + 2)
                        reach(act, hidden_done[1], s - 1)
                        act.activation(x_t[(u + 1) % U][:], x_ps[:, 0:BLOCK], ACT.Copy).then_inc(x_ready, 1)
                    if exists(s):
                        act.wait_ge(hidden_done[0], s + 1)
                        reach(act, y_done, s - 2)
                        for c in range(HALF):
                            act.activation(hidden[u][:, c, :], hidden_ps[0][:, c, :], ACT.Relu,
                                           bias=w[u][:, B1_COL + c:B1_COL + c + 1]).then_inc(relu_ready[0], 1)
                    if exists(s - 1):
                        q = (u + 2) % U
                        act.wait_ge(y_done, s)
                        reach(act, y_turned, s - 3)
                        act.activation(y_t[q][:], y_ps[:, 0:BLOCK], ACT.Identity,
                                       bias=w[q][:, B2_COL:B2_COL + 1]).then_inc(y_ready, 1)
                run(act, step)

            @block.vector
            def _(dve):
                def step(s, u, r):
                    if exists(s):
                        dve.wait_ge(hidden_done[1], s + 1)
                        reach(dve, y_done, s - 2)
                        for c in range(HALF, FC):
                            dve.tensor_scalar(hidden[u][:, c, :], hidden_ps[1][:, c - HALF, :],
                                              w[u][:, B1_COL + c:B1_COL + c + 1], 0.0,
                                              ALU.add, ALU.max).then_inc(relu_ready[1], 1)
                    if exists(s - 2):
                        q = (u + 1) % U
                        dve.wait_ge(y_turned, s - 1)
                        if not known(s) or s - 2 >= U:
                            dve.wait_ge(rows_stored[q], 16 * (r - (1 if u < 2 else 0)))
                        dve.tensor_copy(rows_out[q][:].rearrange("p h d -> p (h d)"), rows_ps[:, 0:BLOCK]).then_inc(rows_ready, 1)
                run(dve, step)

            @block.tensor
            def _(pe):
                def step(s, u, r):
                    if exists(s + 1):
                        q = (u + 1) % U
                        pe.wait_ge(rows_loaded[q], 16 * (r + (u + 1) // U + 1))
                        reach(pe, x_ready, s + 1)
                        for h in range(HT):
                            ins = pe.transpose(x_ps[:, h * D:(h + 1) * D], rows_in[q][:, h, :], ident[:])
                        ins.then_inc(x_turned, 1)
                    if exists(s):
                        pe.wait_ge(weights_in[u], 16 * (r + 1))
                        pe.wait_ge(x_ready, s + 1)
                        for k in range(2):
                            reach(pe, relu_ready[k], HALF * s)
                            for c in range(HALF):
                                f = k * HALF + c
                                ins = pe.matmul(hidden_ps[k][:, c, :], w[u][:, f * D:(f + 1) * D], x_t[u][:],
                                                start=True, stop=True, skip_group_check=True)
                            ins.then_inc(hidden_done[k], 1)
                    if exists(s - 1):
                        q = (u + 2) % U
                        for k in range(2):
                            pe.wait_ge(relu_ready[k], HALF * s)
                        reach(pe, y_ready, s - 1)
                        for f in range(FC):
                            ins = pe.matmul(y_ps[:, 0:BLOCK], w[q][:, DFF + f * D:DFF + (f + 1) * D], hidden[q][:, f, :],
                                            start=(f == 0), stop=(f == FC - 1))
                        ins.then_inc(y_done, 1)
                    if exists(s - 2):
                        q = (u + 1) % U
                        pe.wait_ge(y_ready, s - 1)
                        reach(pe, rows_ready, s - 2)
                        for h in range(HT):
                            ins = pe.transpose(rows_ps[:, h * D:(h + 1) * D], y_t[q][:, h * D:(h + 1) * D], ident[:])
                        ins.then_inc(y_turned, 1)
                run(pe, step)


def combine(nc, dram, ident, xres, s_res, places):
    with ExitStack() as ctx:
        def sb(name, shape, dt=F32):
            return ctx.enter_context(nc.sbuf_tensor("o_" + name, shape, dt))

        def sem(name):
            return ctx.enter_context(nc.semaphore("o_" + name))

        U = 4
        answer = [sb(f"answer{u}", [D, TT, D]) for u in range(U)]
        out_sb = [sb(f"out_sb{u}", [D, TT, D]) for u in range(U)]
        th, silu2, mixed, result = ([sb(f"{n}{p}", [D, N]) for p in range(2)] for n in ("th", "silu2", "mixed", "result"))
        y_ps = [ctx.enter_context(nc.psum_tensor(f"o_y_ps{p}", [D, N], F32)) for p in range(2)]
        out_ps = [ctx.enter_context(nc.psum_tensor(f"o_out_ps{p}", [D, TT, D], F32)) for p in range(2)]

        gathered = [sem(f"gathered{u}") for u in range(U)]
        y_turned = sem("y_turned")
        tanh_ready = sem("tanh_ready")
        silu_ready = sem("silu_ready")
        mixed_ready = sem("mixed_ready")
        result_ready = sem("result_ready")
        result_turned = sem("result_turned")
        out_ready = sem("out_ready")
        out_stored = [sem(f"out_stored{u}") for u in range(U)]

        with nc.Block() as block:

            @block.gpsimd
            def _(pool):
                for u in range(U):
                    pool.sem_inc(out_stored[u], 16)
                for s in range(B):
                    reach(pool, y_turned, s - U + 1)
                    for t in range(TT):
                        j = s * TT + t
                        pool.indirect_dma_start(answer[s % U][:, t, :], None, dram["answers"],
                                                bass.IndirectOffsetOnAxis(ap=places[:, j:j + 1], axis=0)
                                                ).then_inc(gathered[s % U], 16)

            @block.sync
            def _(sp):
                def step(s, u, r):
                    sp.wait_ge(out_ready, s + 1)
                    dst = (dram["out"][s] if known(s) else dram["out"][bass.ds(s, 1)].rearrange("o t d -> (o t) d"))
                    sp.dma_start(dst.rearrange("(t p) d -> p t d", p=D), out_sb[u][:]).then_inc(out_stored[u], 16)
                run_steps(sp, step, B, 0, U)
                for u in range(U):
                    sp.wait_ge(out_stored[u], 16 * (B // U + 1))

            @block.scalar
            def _(act):
                act.preload_act_table_set("exp_and_others")

                def copy_out(s, u, r):
                    act.wait_ge(result_turned, s + 1)
                    act.wait_ge(out_stored[u], 16 * r + 16)
                    act.activation(out_sb[u][:], out_ps[u % 2][:], ACT.Copy).then_inc(out_ready, 1)

                def step(s, u, r):
                    act.wait_ge(y_turned, s + 1)
                    reach(act, silu_ready, s - 1)
                    act.activation(th[u % 2][:], y_ps[u % 2][:], ACT.Tanh, scale=0.5).then_inc(tanh_ready, 1)
                    if not (known(s) and s < 1):
                        copy_out(s - 1, (u + 3) % U, r - (1 if u == 0 else 0))
                run_steps(act, step, B, 0, U)
                copy_out(B - 1, U - 1, B // U - 1)

            @block.vector
            def _(dve):
                def step(s, u, r):
                    cols = columns(s)
                    p = u % 2
                    dve.wait_ge(tanh_ready, s + 1)
                    dve.scalar_tensor_tensor(out=silu2[p][:], in0=th[p][:], scalar=1.0, in1=y_ps[p][:],
                                             op0=ALU.add, op1=ALU.mult).then_inc(silu_ready, 1)
                    dve.wait_ge(silu_ready, s + 1)
                    dve.scalar_tensor_tensor(out=mixed[p][:], in0=silu2[p][:], scalar=0.5, in1=s_res[:, cols],
                                             op0=ALU.mult, op1=ALU.mult).then_inc(mixed_ready, 1)
                    dve.wait_ge(mixed_ready, s + 1)
                    reach(dve, result_turned, s - 1)
                    dve.tensor_tensor(result[p][:], mixed[p][:], xres[:, cols], ALU.add).then_inc(result_ready, 1)
                run_steps(dve, step, B, 0, U)

            @block.tensor
            def _(pe):
                def turn_back(s, p):
                    pe.wait_ge(result_ready, s + 1)
                    reach(pe, out_ready, s - 1)
                    for t in range(TT):
                        ins = pe.transpose(out_ps[p][:, t, :], result[p][:, t * D:(t + 1) * D], ident[:])
                    ins.then_inc(result_turned, 1)

                def step(s, u, r):
                    pe.wait_ge(gathered[u], 16 * TT * (r + 1))
                    reach(pe, silu_ready, s - 1)
                    for t in range(TT):
                        ins = pe.transpose(y_ps[u % 2][:, t * D:(t + 1) * D], answer[u][:, t, :], ident[:])
                    ins.then_inc(y_turned, 1)
                    if not (known(s) and s < 1):
                        turn_back(s - 1, (u + 1) % 2)
                run_steps(pe, step, B, 0, U)
                turn_back(B - 1, (B - 1) % 2)


def phase_experts(nc, dram, ident, xres, s_res, places, weight_rows):
    run_experts(nc, dram, ident, weight_rows)
    combine(nc, dram, ident, xres, s_res, places)


def routing_tables():
    f = np.float32
    earlier = (np.arange(D)[:, None] < np.arange(D)[None, :]).astype(f)
    restart = np.ones((D, EXPERTS, NT), f)
    restart[:, :, 0] = 0
    return {"rank": np.tile(np.arange(EXPERTS, 0, -1, dtype=f), (D, 1)),
            "triangle": np.stack([earlier, np.ones((D, D), f)], 1).astype(mybir.dt.np(BF16)),
            "restart": restart.reshape(D, -1),
            "block_number": np.tile(np.arange(NBLOCK, dtype=f), (D, 1)),
            "partition": np.arange(D, dtype=f)[:, None]}


def expert_rows(w1, b1, w2, b2):
    chunks = w2.reshape(EXPERTS, FC, D, D).transpose(0, 2, 1, 3).reshape(EXPERTS, D, DFF)
    return np.concatenate([w1, chunks, b1.reshape(EXPERTS, FC, D).transpose(0, 2, 1), b2[:, :, None],
                           np.zeros((EXPERTS, D, EXPERT_ROW - B2_COL - 1), w1.dtype)], 2).reshape(EXPERTS * D, EXPERT_ROW)


def build(nc, dram):
    with ExitStack() as ctx:
        def sb(name, shape, dt=F32):
            return ctx.enter_context(nc.sbuf_tensor(name, shape, dt))

        ident, centre, average = sb("ident", [D, D]), sb("centre", [D, D]), sb("average", [D, D])
        ident_bf = sb("ident_bf", [D, D], BF16)
        hid = sb("hid", [D, B * N])
        s_res = sb("s_res", [D, B * N])
        consts_in = ctx.enter_context(nc.semaphore("consts_in"))
        with nc.Block() as block:

            @block.sync
            def _(sp):
                for dst, name in ((ident, "ident"), (centre, "centre"), (average, "average"), (ident_bf, "ident_bf")):
                    sp.dma_start(dst[:], dram[name]).then_inc(consts_in, 16)
                sp.wait_ge(consts_in, 64)

        with ExitStack() as own:
            attend, load_attention, attention_loaded = local_attention(nc, own, sub(dram, "B_"), ident, ident_bf, hid)
            phase_mixer(nc, dram["x"], dram["A_w"], dram["A_vecs"], ident, hid, s_res, dram["sorted"],
                        prefetch=lambda sp: load_attention(sp, 0))
            feed, load_feed = feed_forward(nc, own, sub(dram, "B_"), centre, average, hid)
            assert DEPTH == 2

            def load_other_layer(sp, layer):
                load_attention(sp, layer * -1 + 1)

            with nc.Fori(0, DEPTH) as layer:
                attend(layer, prefetch=load_feed)
                feed(layer, prefetch=load_other_layer, prefetched=attention_loaded)
        places = sb("places", [D, NT], mybir.dt.uint32)
        weight_rows = sb("weight_rows", [D, NBLOCK], mybir.dt.uint32)
        phase_sparse_attention(nc, {**sub(dram, "C_"), **sub(dram, "D_"), **{k: dram[k] for k in ("x", "tokens", "sorted")}},
                               ident, ident_bf, centre, average, hid, s_res, places, weight_rows)
        phase_experts(nc, {**sub(dram, "D_"), **{k: dram[k] for k in ("out", "sorted", "answers")}},
                      ident, hid, s_res, places, weight_rows)


def sub(dram, prefix):
    return {k[len(prefix):]: v for k, v in dram.items() if k.startswith(prefix)}


def kernel(**inputs):
    import concourse.bacc as _bacc
    from concourse.bass_utils import run_bass_kernel_spmd as _run

    a = {k: np.asarray(v) for k, v in inputs.items()}
    data = {"x": a["L0_attn_hidden_states"]}
    data["A_w"] = np.stack([a["L0_attn_" + k].T for k in ("Wk", "Wka", "Wv")], 1)
    data["A_vecs"] = np.stack([a["L0_attn_" + k] for k in ("gamma", "beta", "bk", "bka", "bv")], 1)
    for k in ("wqkv", "wo", "q_scale", "k_scale", "w1", "w2", "b1", "b2", "ln_g", "ln_b"):
        data["B_" + k] = a["L0_ffn_" + k]
    for k in ("Wq", "Wk", "Wv", "Wo"):
        data["C_" + k] = a["L1_attn_" + k].T
    for k in ("bq", "bk", "bv", "bo"):
        data["C_" + k] = a["L1_attn_" + k][:, None]
    data["C_gate_w"] = a["L1_ffn_gate_w"].T
    data["D_gate_b"], data["D_expert_bias"] = a["L1_ffn_gate_b"][None], a["L1_ffn_expert_bias"][None]
    data["D_weights"] = expert_rows(*(a["L1_ffn_" + k] for k in ("w1", "b1", "w2", "b2")))
    mean = np.full((D, D), 1.0 / D, np.float32)
    data["ident"], data["average"], data["centre"] = np.eye(D, dtype=np.float32), mean, np.eye(D, dtype=np.float32) - mean
    data["ident_bf"] = np.eye(D).astype(mybir.dt.np(BF16))
    data["B_rope_base"], data["B_window_mask"] = rope_base_table(), window_mask_table()
    data["C_counts"], data["C_pair_mask"] = pair_tables()
    data["C_rope1"] = rope1_table()
    data["C_same_head"] = np.kron(np.eye(H1), np.ones((DH1, DH1))).astype(np.float32)
    for k, table in routing_tables().items():
        data["D_" + k] = table

    nc = _bacc.Bacc("TRN2", target_bir_lowering=False, num_devices=1)
    arrays, dram = {}, {}
    for name, value in data.items():
        arrays[f"in_{name}"] = np.ascontiguousarray(value)
        dram[name] = nc.dram_tensor(f"in_{name}", value.shape, mybir.dt.from_np(value.dtype), kind="ExternalInput").ap()
    dram["C_ring"] = nc.dram_tensor("ring", (2, D, 3, RING), F32).ap()
    dram["C_back"] = nc.dram_tensor("back", (2, D, 2 * N), F32).ap()
    dram["tokens"] = nc.dram_tensor("tokens", (B, D, N), F32).ap()
    dram["sorted"] = nc.dram_tensor("sorted", (SORTED, D), F32).ap()
    dram["answers"] = nc.dram_tensor("answers", (SORTED, D), F32).ap()
    dram["out"] = nc.dram_tensor("out", (B, N, D), F32, kind="ExternalOutput").ap()
    build(nc, dram)
    return _run(nc, [arrays], core_ids=[0]).results[0]["out"]
```
